# Optimizing a Trainium2 kernel written in Bass

```python
import numpy as np
import jax
import jax.numpy as jnp

def _softmax(x, axis=-1):
    return jax.nn.softmax(x, axis=axis)

def _gelu(x):
    return jax.nn.gelu(x, approximate=True)

def _silu(x):
    return jax.nn.silu(x)

def _sigmoid(x):
    return jax.nn.sigmoid(x)

def _layernorm(x, axis=-1, eps=1e-05):
    m = jnp.mean(x, axis=axis, keepdims=True)
    v = jnp.var(x, axis=axis, keepdims=True)
    return (x - m) / jnp.sqrt(v + eps)

def _scatter_add(tgt, idx, src, axis=0):
    return tgt.at[idx].add(src)

def _segment_sum(src, seg, n):
    return jax.ops.segment_sum(src, seg, n)
kernel_name = 'mk_prb_d1_jaxref_r4_67fb46'

def setup_inputs(seed: int=0):
    np.random.seed(seed)
    _w = jnp.asarray

    def _L0_attn_setup():
        import jax, jax.numpy as jnp
        import numpy as np
        D = 256
        key = jax.random.key(seed)
        ks = jax.random.split(key, 9)
        s = 1.0 / np.sqrt(D)
        x = jax.random.normal(ks[0], (8, 1024, D), dtype=jnp.float32)
        Wq = jax.random.uniform(ks[1], (D, D), jnp.float32, -s, s)
        bq = jax.random.uniform(ks[2], (D,), jnp.float32, -s, s)
        Wk = jax.random.uniform(ks[3], (D, D), jnp.float32, -s, s)
        bk = jax.random.uniform(ks[4], (D,), jnp.float32, -s, s)
        Wv = jax.random.uniform(ks[5], (D, D), jnp.float32, -s, s)
        bv = jax.random.uniform(ks[6], (D,), jnp.float32, -s, s)
        Wo = jax.random.uniform(ks[7], (D, D), jnp.float32, -s, s)
        bo = jax.random.uniform(ks[8], (D,), jnp.float32, -s, s)
        return {'x': x, 'Wq': Wq, 'bq': bq, 'Wk': Wk, 'bk': bk, 'Wv': Wv, 'bv': bv, 'Wo': Wo, 'bo': bo}
    _L0_attn_in = _L0_attn_setup()

    def _L0_ffn_setup():
        import jax, jax.numpy as jnp
        import numpy as np
        TOP_K = 4
        N_GROUP = 4
        TOPK_GROUP = 2
        ROUTED_SCALING = 2.5

        def _route(x, gate_weight):
            scores = jax.nn.sigmoid(x @ gate_weight.T)
            T, E = scores.shape
            gs = E // N_GROUP
            top2, _ = jax.lax.top_k(scores.reshape(T, N_GROUP, gs), 2)
            group_scores = top2.sum(-1)
            _, gidx = jax.lax.top_k(group_scores, TOPK_GROUP)
            gmask = jax.nn.one_hot(gidx, N_GROUP, dtype=jnp.float32).sum(1)
            smask = jnp.repeat(gmask, gs, axis=1) > 0.5
            masked = jnp.where(smask, scores, 0.0)
            topk_idx = jax.lax.top_k(masked, TOP_K)[1]
            topk_w = jnp.take_along_axis(scores, topk_idx, axis=1)
            topk_w = topk_w / (topk_w.sum(-1, keepdims=True) + 1e-20)
            topk_w = topk_w * ROUTED_SCALING
            combine = jnp.zeros((T, E), jnp.float32).at[jnp.arange(T)[:, None], topk_idx].add(topk_w)
            return combine
        key = jax.random.key(seed)
        ks = jax.random.split(key, 6)
        B, S, H = (2, 256, 256)
        E, I, Is = (16, 128, 512)
        g = lambda k, shape, scale: jax.random.normal(k, shape, dtype=jnp.float32) * scale
        return {'hidden_states': g(ks[0], (B, S, H), 1.0), 'gate_weight': g(ks[1], (E, H), 0.02), 'expert_up': g(ks[2], (E, H, I), 0.02), 'expert_down': g(ks[3], (E, I, H), 0.02), 'shared_up': g(ks[4], (H, Is), 0.02), 'shared_down': g(ks[5], (Is, H), 0.02)}
    _L0_ffn_in = _L0_ffn_setup()
    _d = {'L0_attn_x': _L0_attn_in['x'], 'L0_attn_Wq': _L0_attn_in['Wq'], 'L0_attn_bq': _L0_attn_in['bq'], 'L0_attn_Wk': _L0_attn_in['Wk'], 'L0_attn_bk': _L0_attn_in['bk'], 'L0_attn_Wv': _L0_attn_in['Wv'], 'L0_attn_bv': _L0_attn_in['bv'], 'L0_attn_Wo': _L0_attn_in['Wo'], 'L0_attn_bo': _L0_attn_in['bo'], 'L0_ffn_gate_weight': _L0_ffn_in['gate_weight'], 'L0_ffn_expert_up': _L0_ffn_in['expert_up'], 'L0_ffn_expert_down': _L0_ffn_in['expert_down'], 'L0_ffn_shared_up': _L0_ffn_in['shared_up'], 'L0_ffn_shared_down': _L0_ffn_in['shared_down']}
    _x0 = _d['L0_attn_x']
    _d['L0_attn_x'] = jax.random.normal(jax.random.fold_in(jax.random.key(seed), 1), (16, 512, 256), dtype=_x0.dtype)
    del _x0
    return _d

def reference(L0_attn_x, L0_attn_Wq, L0_attn_bq, L0_attn_Wk, L0_attn_bk, L0_attn_Wv, L0_attn_bv, L0_attn_Wo, L0_attn_bo, L0_ffn_gate_weight, L0_ffn_expert_up, L0_ffn_expert_down, L0_ffn_shared_up, L0_ffn_shared_down):

    def _L0_attn_ref(x, Wq, bq, Wk, bk, Wv, bv, Wo, bo):
        import jax, jax.numpy as jnp
        import numpy as np
        D = 256
        Q = x @ Wq.T + bq
        K = x @ Wk.T + bk
        V = x @ Wv.T + bv
        Q = jax.nn.elu(Q) + 1.0
        K = jax.nn.elu(K) + 1.0
        KV = jnp.einsum('bnd,bne->bde', K, V)
        Z = jnp.einsum('bnd,bd->bn', Q, K.sum(axis=1) + 1e-06)
        context = jnp.einsum('bnd,bde->bne', Q, KV) / Z[..., None]
        return context @ Wo.T + bo

    def _L0_ffn_ref(hidden_states, gate_weight, expert_up, expert_down, shared_up, shared_down):
        import jax, jax.numpy as jnp
        import numpy as np
        TOP_K = 4
        N_GROUP = 4
        TOPK_GROUP = 2
        ROUTED_SCALING = 2.5

        def _route(x, gate_weight):
            scores = jax.nn.sigmoid(x @ gate_weight.T)
            T, E = scores.shape
            gs = E // N_GROUP
            top2, _ = jax.lax.top_k(scores.reshape(T, N_GROUP, gs), 2)
            group_scores = top2.sum(-1)
            _, gidx = jax.lax.top_k(group_scores, TOPK_GROUP)
            gmask = jax.nn.one_hot(gidx, N_GROUP, dtype=jnp.float32).sum(1)
            smask = jnp.repeat(gmask, gs, axis=1) > 0.5
            masked = jnp.where(smask, scores, 0.0)
            topk_idx = jax.lax.top_k(masked, TOP_K)[1]
            topk_w = jnp.take_along_axis(scores, topk_idx, axis=1)
            topk_w = topk_w / (topk_w.sum(-1, keepdims=True) + 1e-20)
            topk_w = topk_w * ROUTED_SCALING
            combine = jnp.zeros((T, E), jnp.float32).at[jnp.arange(T)[:, None], topk_idx].add(topk_w)
            return combine
        B, S, H = hidden_states.shape
        x = hidden_states.reshape(-1, H)
        combine = _route(x.astype(jnp.float32), gate_weight)
        up = jnp.einsum('th,ehi->eti', x, expert_up)
        down = jnp.einsum('eti,eih->eth', jax.nn.silu(up), expert_down)
        moe_out = jnp.einsum('te,eth->th', combine, down)
        shared = jax.nn.silu(x @ shared_up) @ shared_down
        return (moe_out + shared).reshape(B, S, H)
    x = L0_attn_x
    xn = _layernorm(x, axis=-1)
    x = x + _L0_attn_ref(xn, L0_attn_Wq, L0_attn_bq, L0_attn_Wk, L0_attn_bk, L0_attn_Wv, L0_attn_bv, L0_attn_Wo, L0_attn_bo) + _L0_ffn_ref(xn, L0_ffn_gate_weight, L0_ffn_expert_up, L0_ffn_expert_down, L0_ffn_shared_up, L0_ffn_shared_down)
    return x

_drawn_inputs = setup_inputs


def setup_inputs(seed=0):
    import zlib

    import numpy as np

    out = dict(_drawn_inputs(seed))
    spreads = {}
    factors = {'L0_attn_Wq': 8.0,
     'L0_attn_bq': 8.0,
     'L0_attn_Wk': 8.0,
     'L0_attn_bk': 8.0,
     'L0_attn_Wv': 3.912,
     'L0_attn_bv': 2.822}
    for name, (base, spread) in spreads.items():
        noise = np.random.default_rng([zlib.crc32(name.encode()), seed]).standard_normal(out[name].shape)
        drawn = base * np.exp(spread * noise) if base else spread * noise
        out[name] = jnp.asarray(drawn.astype(out[name].dtype))
    for name, factor in factors.items():
        out[name] = (out[name] * factor).astype(out[name].dtype)
    return out
```

```python
from contextlib import ExitStack

import concourse.bass as bass
from concourse import mybir

F32 = mybir.dt.float32
F32R = mybir.dt.float32r
U32 = mybir.dt.uint32
ALU = mybir.AluOpType
ACT = mybir.ActivationFunctionType
AX_X = mybir.AxisListType.X

P = 128
N_GROUP = 4
ROUTED_SCALING = 2.5
LN_EPS = 1e-5
Z_EPS = 1e-6
SUM_EPS = 1e-20


def attention_and_routed_ffn(
    nc: bass.Bass,
    x: bass.AP,
    Wq: bass.AP,
    bq: bass.AP,
    Wk: bass.AP,
    bk: bass.AP,
    Wv: bass.AP,
    bv: bass.AP,
    Wo: bass.AP,
    bo: bass.AP,
    gate: bass.AP,
    expert_up: bass.AP,
    expert_down: bass.AP,
    shared_up: bass.AP,
    shared_down: bass.AP,
    out: bass.AP,
):
    B, S, D = x.shape
    E, _, I = expert_up.shape
    T = B * S
    KD = D // P
    SUB = S // P
    GE = E // N_GROUP
    SH = shared_up.shape[1] // I
    NE = E + SH
    ROW = D + E
    NT = T // P
    NG = NE // GE
    assert KD == 2 and SUB == 4 and GE == 4 and SH == 4 and B % 2 == 0 and I == P and B == E

    x_rows = x.rearrange("b (s p) d -> b p s d", p=P)
    out_rows = out.rearrange("b (s p) d -> (b s) p d", p=P)
    normed = nc.dram_tensor("normed_rows", (T, ROW), F32, kind="Internal").ap()
    partial = nc.dram_tensor("attention_rows", (T, D), F32, kind="Internal").ap()
    normed_b = normed.rearrange("(b s p) r -> b p s r", s=SUB, p=P)
    partial_b = partial.rearrange("(b s p) d -> b p s d", s=SUB, p=P)
    normed_t = normed.rearrange("(t p) r -> t p r", p=P)
    partial_t = partial.rearrange("(t p) d -> t p d", p=P)

    def batch_of(view, index):
        return view[bass.ds(index, 1)].rearrange("o p s d -> (o p) s d")

    def tile_of(view, index):
        return view[bass.ds(index, 1)].rearrange("o p d -> (o p) d")

    with ExitStack() as ctx:
        def sb(name, shape, dt=F32):
            return ctx.enter_context(nc.sbuf_tensor(name, shape, dt))

        def sem(name):
            return ctx.enter_context(nc.semaphore(name))

        bank = [ctx.enter_context(nc.psum_tensor(f"bank{i}", [P, 512], F32)) for i in range(8)]

        ident = sb("ident", [P, P])
        ones_r = sb("ones_r", [P, 2], F32R)
        lower = sb("lower", [P, N_GROUP, N_GROUP])
        expert_iota = sb("expert_iota", [P, E], U32)
        minus_half = sb("minus_half", [P, SUB])
        minus_one = sb("minus_one", [P, 1])
        w_raw = sb("w_raw", [P, 4, KD, D])
        gate_raw = sb("gate_raw", [E, D])
        woT = sb("woT", [P, KD, D])
        bv_col = sb("bv_col", [P, KD])
        bv_wide = sb("bv_wide", [P, KD, P])
        bq_col = sb("bq_col", [P, KD])
        bq1_col = sb("bq1_col", [P, KD])
        bk1_all = sb("bk1_all", [P, ROW])
        bo_all = sb("bo_all", [P, D])
        bvo_all = sb("bvo_all", [P, D])
        wqT_h = sb("wqT_h", [P, KD, D], F32R)
        wqT_l = sb("wqT_l", [P, KD, D], F32R)
        wkg_h = sb("wkg_h", [P, KD, ROW], F32R)
        wkg_l = sb("wkg_l", [P, KD, ROW], F32R)
        wvo_h = sb("wvo_h", [P, KD, D], F32R)
        wvo_l = sb("wvo_l", [P, KD, D], F32R)
        UPW = KD * I
        we_h = sb("we_h", [P, NE, UPW + D], F32R)
        we_l = sb("we_l", [P, NE, UPW + D], F32R)
        we_raw = sb("we_raw", [P, 2, UPW + D])
        x_in = sb("x_in", [P, 2, SUB, D])
        stats = sb("stats", [P, SUB, 6])
        mean_var = sb("mean_var", [P, 2, SUB, 2])
        var_eps = sb("var_eps", [P, SUB])
        rstd = sb("rstd", [P, 2, SUB])
        xn = sb("xn", [P, 2, SUB, ROW])
        x_bo = sb("x_bo", [P, 2, SUB, D])
        xr_h = sb("xr_h", [P, SUB, D], F32R)
        xr_l = sb("xr_l", [P, SUB, D], F32R)
        xt_h = sb("xt_h", [P, KD, S], F32R)
        xt_l = sb("xt_l", [P, KD, S], F32R)
        k_t1 = sb("k_t1", [P, SUB, ROW])
        k_f = sb("k_f", [P, SUB, D])
        k_h = sb("k_h", [P, SUB, D], F32R)
        k_l = sb("k_l", [P, SUB, D], F32R)
        q_f = sb("q_f", [P, KD, S])
        q_h = sb("q_h", [P, KD, S], F32R)
        q_l = sb("q_l", [P, KD, S], F32R)
        m_h = sb("m_h", [P, KD, D], F32R)
        m_l = sb("m_l", [P, KD, D], F32R)
        ksum = sb("ksum", [P, KD])
        PW = D + 2
        p_f = sb("p_f", [P, KD, PW])
        p_h = sb("p_h", [P, KD, PW], F32R)
        p_l = sb("p_l", [P, KD, PW], F32R)
        rz = sb("rz", [P, SUB])
        attn_out = sb("attn_out", [P, 2, SUB, D])
        r_exp = sb("r_exp", [P, SUB, E])
        r_den = sb("r_den", [P, SUB, E])
        score = sb("score", [P, SUB, E])
        g_hi = sb("g_hi", [P, SUB * N_GROUP, 2])
        g_lo = sb("g_lo", [P, SUB * N_GROUP, 2])
        g_top = sb("g_top", [P, SUB * N_GROUP])
        g_mid = sb("g_mid", [P, SUB * N_GROUP])
        g_low = sb("g_low", [P, SUB * N_GROUP])
        g_second = sb("g_second", [P, SUB * N_GROUP])
        g_score = sb("g_score", [P, SUB, N_GROUP])
        g_gt = sb("g_gt", [P, SUB, N_GROUP, N_GROUP])
        g_ge = sb("g_ge", [P, SUB, N_GROUP, N_GROUP])
        g_tie = sb("g_tie", [P, SUB, N_GROUP, N_GROUP])
        g_beats = sb("g_beats", [P, SUB, N_GROUP, N_GROUP])
        g_rank = sb("g_rank", [P, SUB, N_GROUP])
        g_in = sb("g_in", [P, SUB, N_GROUP])
        masked = sb("masked", [P, SUB, E])
        top8 = sb("top8", [P, SUB, 8])
        top8_at = sb("top8_at", [P, SUB, 8], U32)
        hit = sb("hit", [P, SUB, E, 4])
        chosen = sb("chosen", [P, SUB, E])
        w_raw4 = sb("w_raw4", [P, SUB, E])
        w_sum = sb("w_sum", [P, SUB])
        w_sum_eps = sb("w_sum_eps", [P, SUB])
        w_rsum = sb("w_rsum", [P, SUB])
        def reused(t, shape):
            names = " ".join("abcd"[:len(t.shape) - 1])
            flat = t[tuple(slice(None) for _ in t.shape)].rearrange(f"p {names} -> p ({names})")
            size = 1
            for n in shape:
                size *= n
            names = " ".join("abcd"[:len(shape)])
            return flat[:, 0:size].rearrange(f"p ({names}) -> p {names}", **dict(zip("abcd", shape)))

        f_rows = reused(k_t1, (2, ROW))
        f_acc = reused(x_in, (4, D))[:, 0:2]
        f_out = reused(x_in, (4, D))[:, 2:4]
        fx_h = reused(xt_h, (2, KD, P))
        fx_l = reused(xt_l, (2, KD, P))
        hid = reused(k_f, (2, GE, I))
        hidw = reused(q_f, (2, GE, I))
        ht_h = reused(q_h, (2, GE, P))
        ht_l = reused(q_l, (2, GE, P))

        setup_loads = [sem(f"setup_load{i}") for i in range(4)]
        bias_loaded = sem("bias_loaded")
        shared_loaded = [sem(f"shared_loaded{i}") for i in range(2)]
        expert_loaded = [sem(f"expert_loaded{i}") for i in range(2)]
        consts_made = sem("consts_made")
        waits_met = sem("waits_met")
        const_step = sem("const_step")
        bias_ready = sem("bias_ready")
        turned = sem("turned")
        turned_hi = sem("turned_hi")
        turned_lo = sem("turned_lo")
        wo_copied = sem("wo_copied")
        folded = sem("folded")
        folded_hi = sem("folded_hi")
        folded_lo = sem("folded_lo")
        bvo_ready = sem("bvo_ready")
        expert_hi = sem("expert_hi")
        expert_lo = sem("expert_lo")
        x_loaded = [sem(f"x_loaded{i}") for i in range(2)]
        stats_done = sem("stats_done")
        moments_ready = sem("moments_ready")
        var_ready = sem("var_ready")
        rstd_ready = sem("rstd_ready")
        xn_ready = sem("xn_ready")
        x_bo_ready = sem("x_bo_ready")
        xr_hi = sem("xr_hi")
        xr_ready = sem("xr_ready")
        xt_done = sem("xt_done")
        xt_hi = sem("xt_hi")
        xt_ready = sem("xt_ready")
        k_done = sem("k_done")
        k_t1_ready = sem("k_t1_ready")
        k_exp = sem("k_exp")
        k_ready = sem("k_ready")
        k_hi = sem("k_hi")
        k_lo = sem("k_lo")
        q_done = sem("q_done")
        q_exp = sem("q_exp")
        q_min = sem("q_min")
        q_ready = sem("q_ready")
        q_hi = sem("q_hi")
        q_lo = sem("q_lo")
        m_done = sem("m_done")
        m_hi = sem("m_hi")
        m_lo = sem("m_lo")
        ksum_done = sem("ksum_done")
        ksum_ready = sem("ksum_ready")
        p_done = sem("p_done")
        p_ready = sem("p_ready")
        p_hi = sem("p_hi")
        p_lo = sem("p_lo")
        c_done = sem("c_done")
        rz_ready = sem("rz_ready")
        attn_ready = sem("attn_ready")
        route_exp = sem("route_exp")
        route_step = sem("route_step")
        route_ready = sem("route_ready")
        normed_stored = [sem(f"normed_stored{i}") for i in range(2)]
        attn_stored = [sem(f"attn_stored{i}") for i in range(2)]
        rows_loaded = [sem(f"rows_loaded{i}") for i in range(2)]
        acc_loaded = [sem(f"acc_loaded{i}") for i in range(2)]
        fx_done = sem("fx_done")
        fx_hi = sem("fx_hi")
        fx_ready = sem("fx_ready")
        up_done = sem("up_done")
        silu_ready = sem("silu_ready")
        weighted = sem("weighted")
        ht_done = sem("ht_done")
        ht_hi = sem("ht_hi")
        ht_ready = sem("ht_ready")
        down_done = sem("down_done")
        f_ready = sem("f_ready")
        out_stored = [sem(f"out_stored{i}") for i in range(2)]

        def wait(eng, s, value):
            if isinstance(value, int) and value <= 0:
                return
            eng.wait_ge(s, value)

        def bare(eng):
            eng.sem_inc(waits_met, 1)

        def later(at, d):
            m, par = at
            return m + (par + d) // 2, (par + d) % 2

        def idx(at):
            return 2 * at[0] + at[1]

        def split3(dst, pairs, start=True, stop=True):
            n = 3 * len(pairs)
            k = 0
            for ah, al, bh, bl in pairs:
                for a, b in ((ah, bh), (ah, bl), (al, bh)):
                    last = nc.tensor.matmul(dst, a, b, start=start and k == 0, stop=stop and k == n - 1)
                    k += 1
            return last

        def attention_rounds(eng, body):
            body((-1, 1), False, False, True)
            body((0, 0), False, True, True)
            body((0, 1), True, True, True)
            body((1, 0), True, True, True)
            with eng.Fori(1, (B - 2) // 2) as k:
                body((k, 1), True, True, True)
                body((k + 1, 0), True, True, True)
            body(((B - 1) // 2, 1), True, True, False)
            body((B // 2, 0), True, False, False)

        ROUTE_STEPS = 20

        def ffn_rounds(eng, unit):
            for r in range(2 * NG):
                unit(0, r, True, False)
            with eng.Fori(1, NT // 2 - 1) as k:
                for r in range(2 * NG):
                    unit(k, r, False, False)
            for r in range(2 * NG):
                unit(NT // 2 - 1, r, False, True)

        block = ctx.enter_context(nc.Block())

        @block.sync
        def _(sp):
            def load_x(at):
                c = idx(at)
                wait(sp, xn_ready, c - 1)
                wait(sp, x_bo_ready, c - 1)
                sp.dma_start(x_in[:, at[1]], batch_of(x_rows, c)).then_inc(x_loaded[at[1]], 16)

            def load_expert(at):
                c = idx(at)
                dst = we_raw[:, at[1]]
                if isinstance(c, int) and c < 2:
                    wait(sp, expert_lo, SH)
                else:
                    wait(sp, expert_lo, SH + c - 1)
                for kd in range(KD):
                    sp.dma_start(dst[:, kd * I:(kd + 1) * I],
                                 expert_up[bass.ds(c, 1), kd * P:(kd + 1) * P, :].rearrange("o d i -> (o d) i")
                                 ).then_inc(expert_loaded[at[1]], 16)
                sp.dma_start(dst[:, UPW:], expert_down[bass.ds(c, 1)].rearrange("o i d -> (o i) d")
                             ).then_inc(expert_loaded[at[1]], 16)

            load_x((0, 0))
            for i, w in enumerate((Wk, Wq, Wo, Wv)):
                sp.dma_start(w_raw[:, i], w.rearrange("(c p) d -> p c d", p=P)).then_inc(setup_loads[i], 16)
                if i == 0:
                    sp.dma_start(gate_raw[:, :], gate).then_inc(bias_loaded, 16)
            sp.dma_start(bk1_all[:, 0:D], bk.partition_broadcast(P)).then_inc(bias_loaded, 16)
            sp.dma_start(bo_all[:, :], bo.partition_broadcast(P)).then_inc(bias_loaded, 16)
            sp.dma_start(bq_col[:, :], bq.rearrange("(c p) -> p c", p=P), allow_slow_non_contiguous=True).then_inc(bias_loaded, 16)
            sp.dma_start(bv_col[:, :], bv.rearrange("(c p) -> p c", p=P), allow_slow_non_contiguous=True).then_inc(bias_loaded, 16)
            load_x((0, 1))
            for j in range(SH):
                wait(sp, expert_lo, j - 1)
                dst = we_raw[:, j % 2]
                for kd in range(KD):
                    sp.dma_start(dst[:, kd * I:(kd + 1) * I], shared_up[kd * P:(kd + 1) * P, j * I:(j + 1) * I]
                                 ).then_inc(shared_loaded[j % 2], 16)
                sp.dma_start(dst[:, UPW:], shared_down[j * I:(j + 1) * I, :]).then_inc(shared_loaded[j % 2], 16)

            def body(at, before, now, after):
                if now:
                    load_expert(at)
                if before:
                    b = later(at, -1)
                    wait(sp, attn_ready, SUB * (idx(b) + 1))
                    sp.dma_start(batch_of(partial_b, idx(b)), attn_out[:, b[1]]).then_inc(attn_stored[b[1]], 16)
                if now:
                    wait(sp, route_ready, idx(at) + 1)
                    sp.dma_start(batch_of(normed_b, idx(at)), xn[:, at[1]]).then_inc(normed_stored[at[1]], 16)

            body((0, 0), False, True, True)
            load_x((1, 0))
            body((0, 1), True, True, True)
            load_x((1, 1))
            body((1, 0), True, True, True)
            load_x((2, 0))
            with sp.Fori(1, (B - 4) // 2) as k:
                body((k, 1), True, True, True)
                load_x((k + 1, 1))
                body((k + 1, 0), True, True, True)
                load_x((k + 2, 0))
            m = (B - 4) // 2
            body((m, 1), True, True, True)
            load_x((m + 1, 1))
            body((m + 1, 0), True, True, True)
            body((m + 1, 1), True, True, False)
            body((m + 2, 0), True, False, False)

            for par in range(2):
                sp.wait_ge(normed_stored[par], 16 * (B // 2))
                sp.wait_ge(attn_stored[par], 16 * (B // 2))

            def load_rows(at):
                j = idx(at)
                wait(sp, weighted, N_GROUP * (j - 1))
                sp.dma_start(f_rows[:, at[1]], tile_of(normed_t, j)).then_inc(rows_loaded[at[1]], 16)

            def load_acc(at):
                j = idx(at)
                wait(sp, f_ready, j - 1)
                sp.dma_start(f_acc[:, at[1]], tile_of(partial_t, j)).then_inc(acc_loaded[at[1]], 16)

            def store_tile(at):
                j = idx(at)
                wait(sp, f_ready, j + 1)
                sp.dma_start(tile_of(out_rows, j), f_out[:, at[1]]).then_inc(out_stored[at[1]], 16)

            for par in range(2):
                load_rows((0, par))
                load_acc((0, par))
            with sp.Fori(0, NT // 2 - 1) as k:
                for par in range(2):
                    load_rows((k + 1, par))
                    store_tile((k, par))
                    load_acc((k + 1, par))
            for par in range(2):
                store_tile((NT // 2 - 1, par))
            for par in range(2):
                sp.wait_ge(out_stored[par], 16 * (NT // 2))

        @block.gpsimd
        def _(pool):
            nc.gpsimd.memset(ident[:, :], 1.0).then_inc(const_step, 1)
            nc.gpsimd.memset(lower[:, :, :], 1.0).then_inc(const_step, 1)
            pool.wait_ge(const_step, 2)
            nc.gpsimd.affine_select(out=ident[:, :], in_=ident[:, :], compare_op=ALU.is_equal, fill=0.0, base=0,
                                    pattern=[[-1, P]], channel_multiplier=1).then_inc(consts_made, 1)
            nc.gpsimd.affine_select(out=lower[:, :, :], in_=lower[:, :, :], compare_op=ALU.is_gt, fill=0.0, base=0,
                                    pattern=[[1, N_GROUP], [-1, N_GROUP]], channel_multiplier=0
                                    ).then_inc(consts_made, 1)
            nc.gpsimd.iota(expert_iota[:, :], pattern=[[1, E]], base=0, channel_multiplier=0).then_inc(consts_made, 1)
            nc.gpsimd.memset(minus_half[:, :], -0.5).then_inc(consts_made, 1)
            nc.gpsimd.memset(ones_r[:, :].bitcast(F32), 1.0).then_inc(consts_made, 1)

            def split_expert(slot, par, loaded, count):
                pool.wait_ge(loaded, count)
                hi = we_h[:, bass.ds(slot, 1), :].rearrange("p o w -> p (o w)")
                lo = we_l[:, bass.ds(slot, 1), :].rearrange("p o w -> p (o w)")
                bare(pool)
                nc.gpsimd.tensor_copy(hi, we_raw[:, par]).then_inc(expert_hi, 1)
                return hi, lo

            def rest_expert(hi, lo, par, value):
                pool.wait_ge(expert_hi, value)
                nc.gpsimd.tensor_tensor(lo, we_raw[:, par], hi.bitcast(F32), ALU.subtract).then_inc(expert_lo, 1)

            def moments(at):
                c = idx(at)
                pool.wait_ge(moments_ready, c + 1)
                bare(pool)
                nc.gpsimd.tensor_scalar(var_eps[:, :], mean_var[:, at[1], :, 1], LN_EPS, None, ALU.add
                                        ).then_inc(var_ready, 1)
                pool.wait_ge(var_ready, c + 1)
                nc.gpsimd.tensor_tensor(rstd[:, at[1]], var_eps[:, :], minus_half[:, :], ALU.pow
                                        ).then_inc(rstd_ready, 1)

            def residual(at):
                c = idx(at)
                wait(pool, x_loaded[at[1]], 16 * (at[0] + 1))
                wait(pool, attn_ready, SUB * (c - 1))
                nc.gpsimd.tensor_tensor(x_bo[:, at[1]], x_in[:, at[1]],
                                        bo_all[:, :].unsqueeze(1).to_broadcast([P, SUB, D]), ALU.add
                                        ).then_inc(x_bo_ready, 1)

            def split_rows(at):
                c = idx(at)
                wait(pool, xn_ready, c + 1)
                wait(pool, m_done, c)
                bare(pool)
                nc.gpsimd.tensor_copy(xr_h[:, :, :], xn[:, at[1], :, 0:D]).then_inc(xr_hi, 1)
                pool.wait_ge(xr_hi, c + 1)
                nc.gpsimd.tensor_tensor(xr_l[:, :, :], xn[:, at[1], :, 0:D], xr_h[:, :, :].bitcast(F32),
                                        ALU.subtract).then_inc(xr_ready, 1)

            def body(at, before, now, after):
                if after:
                    moments(later(at, 1))
                if now:
                    c = idx(at)
                    pool.wait_ge(k_hi, c + 1)
                    nc.gpsimd.tensor_tensor(k_l[:, :, :], k_f[:, :, :], k_h[:, :, :].bitcast(F32),
                                            ALU.subtract).then_inc(k_lo, 1)
                if after:
                    if not now:
                        pool.wait_ge(bias_loaded, 16 * 5)
                    residual(later(at, 1))
                if now:
                    par = at[1]
                    slot = idx(at)
                    hi, lo = split_expert(slot, par, expert_loaded[par], 48 * (at[0] + 1))
                    rest_expert(hi, lo, par, SH + slot + 1)
                if after:
                    split_rows(later(at, 1))
                if not now and not before:
                    for j in range(SH):
                        hi, lo = split_expert(E + j, j % 2, shared_loaded[j % 2], 48 * (j // 2 + 1))
                        rest_expert(hi, lo, j % 2, j + 1)

            attention_rounds(pool, body)

        @block.scalar
        def _(act):
            for i, (dst, w) in enumerate(((wkg_h[:, :, 0:D], 0), (wqT_h[:, :, :], 1))):
                act.wait_ge(turned, w + 1)
                nc.scalar.copy(dst, bank[w][:, :].rearrange("p (c d) -> p c d", c=KD)).then_inc(turned_hi, 1)
            act.wait_ge(turned, 3)
            nc.scalar.copy(wkg_h[:, :, D:ROW], bank[3][:, 0:KD * E].rearrange("p (c e) -> p c e", c=KD)
                           ).then_inc(turned_hi, 1)
            act.wait_ge(turned, 4)
            nc.scalar.copy(woT[:, :, :], bank[2][:, :].rearrange("p (c d) -> p c d", c=KD)).then_inc(wo_copied, 1)
            act.wait_ge(folded, 1)
            nc.scalar.copy(wvo_h[:, :, :], bank[0][:, :].rearrange("p (c d) -> p c d", c=KD)).then_inc(folded_hi, 1)

            def body(at, before, now, after):
                c = idx(at)
                if now:
                    act.wait_ge(k_t1_ready, SUB * (c + 1))
                    wait(act, k_lo, c)
                    nc.scalar.activation(k_f[:, :, :], k_t1[:, :, 0:D], ACT.Exp, bias=minus_one[:, 0:1]
                                         ).then_inc(k_exp, 1)
                if before:
                    act.wait_ge(p_ready, c)
                    wait(act, c_done, SUB * (c - 1))
                    nc.scalar.copy(p_h[:, :, :], p_f[:, :, :]).then_inc(p_hi, 1)
                if now:
                    act.wait_ge(k_ready, c + 1)
                    wait(act, ksum_done, c)
                    nc.scalar.copy(k_h[:, :, :], k_f[:, :, :]).then_inc(k_hi, 1)
                    for h in range(KD):
                        act.wait_ge(q_done, KD * c + h + 1)
                        wait(act, q_lo, c)
                        nc.scalar.activation(q_f[:, h, :], bank[2 + h][:, :], ACT.Exp, bias=bq_col[:, h:h + 1]
                                             ).then_inc(q_exp, 1)
                    nc.scalar.activation(r_exp[:, :, :], k_t1[:, :, D:ROW], ACT.Exp, scale=-1.0
                                         ).then_inc(route_exp, 1)
                    act.wait_ge(q_ready, KD * (c + 1))
                    wait(act, c_done, SUB * c)
                    nc.scalar.copy(q_h[:, :, :], q_f[:, :, :]).then_inc(q_hi, 1)
                if after:
                    act.wait_ge(xt_done, c + 2)
                    wait(act, q_done, KD * (c + 1))
                    for h in range(KD):
                        nc.scalar.copy(xt_h[:, h, :], bank[4 + h][:, :]).then_inc(xt_hi, 1)
                if now:
                    act.wait_ge(m_done, c + 1)
                    wait(act, p_done, c)
                    nc.scalar.copy(m_h[:, :, :], bank[6][:, :].rearrange("p (c d) -> p c d", c=KD)
                                   ).then_inc(m_hi, 1)

            attention_rounds(act, body)

            def turn_rows(at):
                act.wait_ge(fx_done, idx(at) + 1)
                wait(act, up_done, NG * (idx(at) - 1))
                nc.scalar.copy(fx_h[:, at[1]], bank[4][:, 0:D].rearrange("p (c t) -> p c t", c=KD)
                               ).then_inc(fx_hi, 1)

            def silu(u, r):
                act.wait_ge(up_done, u + 1)
                wait(act, ht_done, u - 1)
                nc.scalar.activation(hid[:, r % 2], bank[r % 2][:, :].rearrange("p (e i) -> p e i", e=GE), ACT.Silu
                                     ).then_inc(silu_ready, 1)

            def hidden_hi(u, r):
                act.wait_ge(ht_done, u + 1)
                wait(act, down_done, u - 1)
                nc.scalar.copy(ht_h[:, r % 2], bank[2 + r % 2][:, :].rearrange("p (e t) -> p e t", e=GE)
                               ).then_inc(ht_hi, 1)

            turn_rows((0, 0))

            def unit(k, r, first, last):
                u = 2 * NG * k + r
                silu(u, r)
                if r % NG == 2 and not (last and r // NG == 1):
                    turn_rows(later((k, r // NG), 1))
                if not (first and r == 0):
                    hidden_hi(u - 1, r + 1)

            ffn_rounds(act, unit)
            hidden_hi(NG * NT - 1, 2 * NG - 1)

        @block.vector
        def _(dve):
            nc.vector.memset(minus_one[:, :], -1.0).then_inc(bias_ready, 1)
            nc.vector.memset(p_f[:, :, D + 1:PW], 0.0).then_inc(bias_ready, 1)
            nc.vector.memset(bk1_all[:, D:ROW], 0.0).then_inc(bias_ready, 1)
            dve.wait_ge(bias_loaded, 16 * 5)
            nc.vector.tensor_scalar(bk1_all[:, 0:D], bk1_all[:, 0:D], 1.0, None, ALU.add).then_inc(bias_ready, 1)
            nc.vector.tensor_scalar(bq1_col[:, :], bq_col[:, :], 1.0, None, ALU.add).then_inc(bias_ready, 1)
            for c in range(KD):
                nc.vector.tensor_copy(bv_wide[:, c, :], bv_col[:, c:c + 1].to_broadcast([P, P])).then_inc(bias_ready, 1)
            for i, (dst, hi, src) in enumerate((
                    (wkg_l[:, :, 0:D], wkg_h[:, :, 0:D], bank[0][:, :].rearrange("p (c d) -> p c d", c=KD)),
                    (wqT_l[:, :, :], wqT_h[:, :, :], bank[1][:, :].rearrange("p (c d) -> p c d", c=KD)),
                    (wkg_l[:, :, D:ROW], wkg_h[:, :, D:ROW],
                     bank[3][:, 0:KD * E].rearrange("p (c e) -> p c e", c=KD)))):
                dve.wait_ge(turned_hi, i + 1)
                nc.vector.tensor_tensor(dst, src, hi.bitcast(F32), ALU.subtract).then_inc(turned_lo, 1)
            dve.wait_ge(folded_hi, 1)
            nc.vector.tensor_tensor(wvo_l[:, :, :], bank[0][:, :].rearrange("p (c d) -> p c d", c=KD),
                                    wvo_h[:, :, :].bitcast(F32), ALU.subtract).then_inc(folded_lo, 1)
            dve.wait_ge(folded, 2)
            nc.vector.tensor_copy(bvo_all[:, :], bank[1][:, 0:D]).then_inc(bvo_ready, 1)

            def statistics(at):
                c = idx(at)
                dve.wait_ge(x_loaded[at[1]], 16 * (at[0] + 1))
                for s in range(SUB):
                    last = nc.vector.bn_stats(stats[:, s], x_in[:, at[1], s])
                last.then_inc(stats_done, 1)
                dve.wait_ge(stats_done, c + 1)
                bare(dve)
                for s in range(SUB):
                    last = nc.vector.bn_aggr(mean_var[:, at[1], s], stats[:, s])
                last.then_inc(moments_ready, 1)

            def normalise(at):
                c = idx(at)
                dve.wait_ge(rstd_ready, c + 1)
                wait(dve, normed_stored[at[1]], 16 * at[0])
                wait(dve, xr_ready, c - 1)
                for s in range(SUB):
                    last = nc.vector.tensor_scalar(xn[:, at[1], s, 0:D], x_in[:, at[1], s],
                                                   mean_var[:, at[1], s, 0:1], rstd[:, at[1], s:s + 1],
                                                   ALU.subtract, ALU.mult)
                last.then_inc(xn_ready, 1)

            def route(at):
                c = idx(at)
                steps = [0]

                def step(ins, n=1):
                    steps[0] += n
                    ins.then_inc(route_step, n)

                def after_steps():
                    dve.wait_ge(route_step, ROUTE_STEPS * c + steps[0])

                V = nc.vector
                dve.wait_ge(route_exp, c + 1)
                step(V.tensor_scalar(r_den[:, :, :], r_exp[:, :, :], 1.0, None, ALU.add))
                after_steps()
                step(V.reciprocal(score[:, :, :], r_den[:, :, :]))
                after_steps()
                g4 = score[:, :, :].rearrange("p s (g e) -> p (s g) e", g=N_GROUP)
                V.tensor_tensor(g_hi[:, :, :], g4[:, :, 0:2], g4[:, :, 2:4], ALU.max)
                step(V.tensor_tensor(g_lo[:, :, :], g4[:, :, 0:2], g4[:, :, 2:4], ALU.min))
                after_steps()
                V.tensor_tensor(g_top[:, :], g_hi[:, :, 0], g_hi[:, :, 1], ALU.max)
                V.tensor_tensor(g_mid[:, :], g_hi[:, :, 0], g_hi[:, :, 1], ALU.min)
                step(V.tensor_tensor(g_low[:, :], g_lo[:, :, 0], g_lo[:, :, 1], ALU.max))
                after_steps()
                step(V.tensor_tensor(g_second[:, :], g_mid[:, :], g_low[:, :], ALU.max))
                after_steps()
                step(V.tensor_tensor(g_score[:, :, :].rearrange("p s g -> p (s g)"), g_top[:, :], g_second[:, :],
                                     ALU.add))
                after_steps()
                mine = g_score[:, :, :].unsqueeze(3).to_broadcast([P, SUB, N_GROUP, N_GROUP])
                other = g_score[:, :, :].unsqueeze(2).to_broadcast([P, SUB, N_GROUP, N_GROUP])
                V.tensor_tensor(g_gt[:, :, :, :], other, mine, ALU.is_gt)
                step(V.tensor_tensor(g_ge[:, :, :, :], other, mine, ALU.is_ge))
                after_steps()
                step(V.tensor_tensor(g_tie[:, :, :, :], g_ge[:, :, :, :],
                                     lower[:, :, :].unsqueeze(1).to_broadcast([P, SUB, N_GROUP, N_GROUP]), ALU.mult))
                after_steps()
                step(V.tensor_tensor(g_beats[:, :, :, :], g_gt[:, :, :, :], g_tie[:, :, :, :], ALU.max))
                after_steps()
                step(V.tensor_reduce(g_rank[:, :, :], g_beats[:, :, :, :], AX_X, ALU.add))
                after_steps()
                step(V.tensor_scalar(g_in[:, :, :], g_rank[:, :, :], 2.0, None, ALU.is_lt))
                after_steps()
                step(V.tensor_tensor(masked[:, :, :].rearrange("p s (g e) -> p (s g) e", g=N_GROUP), g4,
                                     g_in[:, :, :].rearrange("p s g -> p (s g)").unsqueeze(2).to_broadcast(
                                         [P, SUB * N_GROUP, GE]), ALU.mult))
                after_steps()
                bare(dve)
                for s in range(SUB):
                    last = V.max(top8[:, s], masked[:, s])
                step(last)
                after_steps()
                bare(dve)
                for s in range(SUB):
                    last = V.max_index(top8_at[:, s], top8[:, s], masked[:, s])
                step(last)
                after_steps()
                step(V.tensor_tensor(hit[:, :, :, :],
                                     expert_iota[:, :].unsqueeze(1).unsqueeze(3).to_broadcast([P, SUB, E, 4]),
                                     top8_at[:, :, 0:4].unsqueeze(2).to_broadcast([P, SUB, E, 4]), ALU.is_equal))
                after_steps()
                step(V.tensor_reduce(chosen[:, :, :], hit[:, :, :, :], AX_X, ALU.add))
                after_steps()
                step(V.tensor_tensor(w_raw4[:, :, :], chosen[:, :, :], score[:, :, :], ALU.mult))
                after_steps()
                step(V.tensor_reduce(w_sum[:, :], w_raw4[:, :, :], AX_X, ALU.add))
                after_steps()
                step(V.tensor_scalar(w_sum_eps[:, :], w_sum[:, :], SUM_EPS, None, ALU.add))
                after_steps()
                step(V.reciprocal(w_rsum[:, :], w_sum_eps[:, :]))
                after_steps()
                assert steps[0] == ROUTE_STEPS, steps[0]
                V.scalar_tensor_tensor(out=xn[:, at[1], :, D:ROW], in0=w_raw4[:, :, :], scalar=ROUTED_SCALING,
                                       in1=w_rsum[:, :].unsqueeze(2).to_broadcast([P, SUB, E]),
                                       op0=ALU.mult, op1=ALU.mult).then_inc(route_ready, 1)

            def body(at, before, now, after):
                c = idx(at)
                V = nc.vector
                if after:
                    statistics(later(at, 1))
                    if not now:
                        dve.wait_ge(consts_made, 5)
                        normalise(later(at, 1))
                if now:
                    for s in range(SUB):
                        dve.wait_ge(k_done, SUB * c + s + 1)
                        wait(dve, route_exp, c)
                        V.tensor_tensor(k_t1[:, s], bank[s % 2][:, 0:ROW], bk1_all[:, :], ALU.add
                                        ).then_inc(k_t1_ready, 1)
                if before:
                    dve.wait_ge(p_done, c)
                    if not now:
                        dve.wait_ge(bvo_ready, 1)
                    wait(dve, ksum_ready, c)
                    wait(dve, p_hi, c - 1)
                    for h in range(KD):
                        last = V.scalar_tensor_tensor(out=p_f[:, h, 0:D], in0=bvo_all[:, :], scalar=ksum[:, h:h + 1],
                                                      in1=bank[7][:, h * D:(h + 1) * D], op0=ALU.mult, op1=ALU.add)
                    last.then_inc(p_ready, 1)
                    dve.wait_ge(p_hi, c)
                    V.tensor_tensor(p_l[:, :, :], p_f[:, :, :], p_h[:, :, :].bitcast(F32), ALU.subtract
                                    ).then_inc(p_lo, 1)
                if now:
                    dve.wait_ge(k_exp, c + 1)
                    V.scalar_tensor_tensor(out=k_f[:, :, :], in0=k_f[:, :, :], scalar=1.0, in1=k_t1[:, :, 0:D],
                                           op0=ALU.min, op1=ALU.max).then_inc(k_ready, 1)
                    for h in range(KD):
                        dve.wait_ge(q_exp, KD * c + h + 1)
                        V.tensor_scalar(q_f[:, h], q_f[:, h], 1.0, None, ALU.min).then_inc(q_min, 1)
                    for h in range(KD):
                        dve.wait_ge(q_min, KD * c + h + 1)
                        V.scalar_tensor_tensor(out=q_f[:, h], in0=bank[2 + h][:, :], scalar=bq1_col[:, h:h + 1],
                                               in1=q_f[:, h], op0=ALU.add, op1=ALU.max).then_inc(q_ready, 1)
                    if after:
                        normalise(later(at, 1))
                if before:
                    b = later(at, -1)
                    wait(dve, attn_stored[b[1]], 16 * b[0])
                    wait(dve, x_bo_ready, c)
                    for s in range(SUB):
                        dve.wait_ge(c_done, SUB * (c - 1) + s + 1)
                        V.reciprocal(rz[:, s:s + 1], bank[s % 2][:, D:D + 1]).then_inc(rz_ready, 1)
                        dve.wait_ge(rz_ready, SUB * (c - 1) + s + 1)
                        V.scalar_tensor_tensor(out=attn_out[:, b[1], s], in0=bank[s % 2][:, 0:D],
                                               scalar=rz[:, s:s + 1], in1=x_bo[:, b[1], s],
                                               op0=ALU.mult, op1=ALU.add).then_inc(attn_ready, 1)
                if now:
                    dve.wait_ge(q_hi, c + 1)
                    V.tensor_tensor(q_l[:, :, :], q_f[:, :, :], q_h[:, :, :].bitcast(F32), ALU.subtract
                                    ).then_inc(q_lo, 1)
                if after:
                    for h in range(KD):
                        dve.wait_ge(xt_hi, KD * (c + 1) + h + 1)
                        V.tensor_tensor(xt_l[:, h], bank[4 + h][:, :], xt_h[:, h].bitcast(F32), ALU.subtract
                                        ).then_inc(xt_ready, 1)
                if now:
                    route(at)
                    dve.wait_ge(m_hi, c + 1)
                    V.tensor_tensor(m_l[:, :, :], bank[6][:, :].rearrange("p (c d) -> p c d", c=KD),
                                    m_h[:, :, :].bitcast(F32), ALU.subtract).then_inc(m_lo, 1)
                    dve.wait_ge(ksum_done, c + 1)
                    sums = bank[1][:, 508:512].rearrange("p (h two) -> p h two", two=2)[:, :, 0]
                    V.tensor_copy(ksum[:, :], sums)
                    V.tensor_scalar(p_f[:, :, D], sums, Z_EPS, None, ALU.add).then_inc(ksum_ready, 1)

            attention_rounds(dve, body)

            V = nc.vector

            def turn_rows(at):
                dve.wait_ge(fx_hi, idx(at) + 1)
                V.tensor_tensor(fx_l[:, at[1]], bank[4][:, 0:D].rearrange("p (c t) -> p c t", c=KD),
                                fx_h[:, at[1]].bitcast(F32), ALU.subtract).then_inc(fx_ready, 1)

            def weigh(k, r):
                g, par = r % NG, r // NG
                if g == 0:
                    dve.wait_ge(rows_loaded[par], 16 * (k + 1))
                if g < N_GROUP:
                    dve.wait_ge(silu_ready, 2 * NG * k + r + 1)
                    V.tensor_tensor(hidw[:, r % 2], hid[:, r % 2],
                                    f_rows[:, par, D + g * GE:D + (g + 1) * GE].unsqueeze(2).to_broadcast(
                                        [P, GE, I]), ALU.mult).then_inc(weighted, 1)

            def hidden_lo(u, r):
                dve.wait_ge(ht_hi, u + 1)
                V.tensor_tensor(ht_l[:, r % 2], bank[2 + r % 2][:, :].rearrange("p (e t) -> p e t", e=GE),
                                ht_h[:, r % 2].bitcast(F32), ALU.subtract).then_inc(ht_ready, 1)

            def finish(at):
                j = idx(at)
                dve.wait_ge(acc_loaded[at[1]], 16 * (at[0] + 1))
                dve.wait_ge(down_done, NG * (j + 1))
                wait(dve, out_stored[at[1]], 16 * at[0])
                V.tensor_tensor(f_out[:, at[1]], bank[6 + at[1]][:, 0:D], f_acc[:, at[1]], ALU.add
                                ).then_inc(f_ready, 1)

            turn_rows((0, 0))

            def unit(k, r, first, last):
                u = 2 * NG * k + r
                weigh(k, r)
                if r % NG == 2 and not (last and r // NG == 1):
                    turn_rows(later((k, r // NG), 1))
                if not (first and r == 0):
                    hidden_lo(u - 1, r + 1)
                if r % NG == 3 and not (first and r == 3):
                    finish(later((k, r // NG), -1))

            ffn_rounds(dve, unit)
            hidden_lo(NG * NT - 1, 2 * NG - 1)
            finish((NT // 2 - 1, 1))

        @block.tensor
        def _(pe):
            T_ = nc.tensor
            pe.wait_ge(consts_made, 1)

            def turn_weight(w, b):
                pe.wait_ge(setup_loads[w], 16)
                for r in range(KD):
                    for c in range(KD):
                        last = T_.transpose(bank[b][:, c * D + r * P:c * D + (r + 1) * P],
                                            w_raw[:, w, r, c * P:(c + 1) * P], ident[:, :])
                last.then_inc(turned, 1)

            turn_weight(0, 0)
            turn_weight(1, 1)
            pe.wait_ge(bias_loaded, 16 * 5)
            for c in range(KD):
                last = T_.transpose(bank[3][:, c * E:(c + 1) * E], gate_raw[:, c * P:(c + 1) * P], ident[0:E, 0:E])
            last.then_inc(turned, 1)
            turn_weight(2, 2)
            pe.wait_ge(setup_loads[3], 16)
            pe.wait_ge(wo_copied, 1)
            pe.wait_ge(turned_lo, 2)
            for h in range(KD):
                for m in range(KD):
                    last = T_.matmul(bank[0][:, h * D:(h + 1) * D], w_raw[:, 3, m, h * P:(h + 1) * P], woT[:, m, :],
                                     start=(m == 0), stop=(m == KD - 1))
            last.then_inc(folded, 1)
            pe.wait_ge(bias_ready, 7)
            for m in range(KD):
                last = T_.matmul(bank[1][:, 0:D], bv_wide[:, m, :], woT[:, m, :], start=(m == 0), stop=(m == KD - 1))
            last.then_inc(folded, 1)
            pe.wait_ge(folded_lo, 1)
            pe.wait_ge(bvo_ready, 1)
            pe.wait_ge(turned_lo, 3)

            def body(at, before, now, after):
                c = idx(at)
                if now:
                    pe.wait_ge(xt_ready, KD * (c + 1))
                    for s in range(SUB):
                        if s < 2:
                            wait(pe, ksum_ready, c)
                        else:
                            pe.wait_ge(k_t1_ready, SUB * c + s - 1)
                        cols = slice(s * P, (s + 1) * P)
                        split3(bank[s % 2][:, 0:ROW],
                               [(xt_h[:, h, cols], xt_l[:, h, cols], wkg_h[:, h, :], wkg_l[:, h, :])
                                for h in range(KD)]).then_inc(k_done, 1)
                if before:
                    pe.wait_ge(m_lo, c)
                    wait(pe, p_ready, c - 1)
                    for h in range(KD):
                        cols = slice(h * P, (h + 1) * P)
                        last = split3(bank[7][:, h * D:(h + 1) * D],
                                      [(m_h[:, d, cols], m_l[:, d, cols], wvo_h[:, d, :], wvo_l[:, d, :])
                                       for d in range(KD)])
                    last.then_inc(p_done, 1)
                if now:
                    for h in range(KD):
                        wait(pe, q_ready, KD * (c - 1) + h + 1)
                        cols = slice(h * P, (h + 1) * P)
                        split3(bank[2 + h][:, :],
                               [(wqT_h[:, d, cols], wqT_l[:, d, cols], xt_h[:, d, :], xt_l[:, d, :])
                                for d in range(KD)]).then_inc(q_done, 1)
                if before:
                    pe.wait_ge(p_lo, c)
                    pe.wait_ge(q_lo, c)
                    for s in range(SUB):
                        if s < 2:
                            if now:
                                pe.wait_ge(k_t1_ready, SUB * c + s + 3)
                            else:
                                pe.wait_ge(ksum_ready, c)
                        else:
                            pe.wait_ge(attn_ready, SUB * (c - 1) + s - 1)
                        cols = slice(s * P, (s + 1) * P)
                        split3(bank[s % 2][:, 0:PW],
                               [(q_h[:, d, cols], q_l[:, d, cols], p_h[:, d, :], p_l[:, d, :])
                                for d in range(KD)]).then_inc(c_done, 1)
                if after:
                    n = later(at, 1)
                    pe.wait_ge(xn_ready, c + 2)
                    wait(pe, xt_ready, KD * (c + 1))
                    for s in range(SUB):
                        for h in range(KD):
                            last = T_.transpose(bank[4 + h][:, s * P:(s + 1) * P], xn[:, n[1], s, h * P:(h + 1) * P],
                                                ident[:, :])
                    last.then_inc(xt_done, 1)
                if now:
                    pe.wait_ge(xr_ready, c + 1)
                    pe.wait_ge(k_lo, c + 1)
                    wait(pe, m_lo, c)
                    for h in range(KD):
                        cols = slice(h * P, (h + 1) * P)
                        last = split3(bank[6][:, h * D:(h + 1) * D],
                                      [(xr_h[:, s, cols], xr_l[:, s, cols], k_h[:, s, :], k_l[:, s, :])
                                       for s in range(SUB)])
                    last.then_inc(m_done, 1)
                    pe.wait_ge(k_t1_ready, SUB * (c + 1))
                    wait(pe, attn_ready, SUB * c)
                    for h in range(KD):
                        cols = slice(h * P, (h + 1) * P)
                        for n, kk in enumerate((k_h, k_l)):
                            for s in range(SUB):
                                last = T_.matmul(bank[1][:, 508 + 2 * h:510 + 2 * h], kk[:, s, cols], ones_r[:, :],
                                                 start=(n == 0 and s == 0), stop=(n == 1 and s == SUB - 1))
                    last.then_inc(ksum_done, 1)

            attention_rounds(pe, body)

            pe.wait_ge(attn_ready, SUB * B)
            pe.wait_ge(expert_lo, NE)

            def turn_rows(at):
                j = idx(at)
                pe.wait_ge(rows_loaded[at[1]], 16 * (at[0] + 1))
                wait(pe, fx_ready, j)
                for h in range(KD):
                    last = T_.transpose(bank[4][:, h * P:(h + 1) * P], f_rows[:, at[1], h * P:(h + 1) * P],
                                        ident[:, :])
                last.then_inc(fx_done, 1)

            def up(u, k, r):
                g, par = r % NG, r // NG
                if g == 0:
                    pe.wait_ge(fx_ready, 2 * k + par + 1)
                wait(pe, silu_ready, u - 1)
                mov = [[w[:, g * GE:(g + 1) * GE, h * I:(h + 1) * I] for w in (we_h, we_l)] for h in range(KD)]
                split3(bank[r % 2][:, :].rearrange("p (e i) -> p e i", e=GE),
                       [(fx_h[:, par, h], fx_l[:, par, h], mov[h][0], mov[h][1])
                        for h in range(KD)]).then_inc(up_done, 1)

            def turn_hidden(k, r):
                u = 2 * NG * k + r
                g = r % NG
                if g < N_GROUP:
                    pe.wait_ge(weighted, N_GROUP * (2 * k + r // NG) + g + 1)
                else:
                    pe.wait_ge(silu_ready, u + 1)
                wait(pe, ht_ready, u - 1)
                src = hidw if g < N_GROUP else hid
                for e in range(GE):
                    last = T_.transpose(bank[2 + r % 2][:, e * P:(e + 1) * P], src[:, r % 2, e, :], ident[:, :])
                last.then_inc(ht_done, 1)

            def down(k, r):
                u = 2 * NG * k + r
                g, par = r % NG, (r // NG) % 2
                pe.wait_ge(ht_ready, u + 1)
                if g == 0:
                    wait(pe, f_ready, 2 * k + r // NG - 1)
                split3(bank[6 + par][:, 0:D],
                       [(ht_h[:, r % 2, e], ht_l[:, r % 2, e], we_h[:, g * GE + e, UPW:], we_l[:, g * GE + e, UPW:])
                        for e in range(GE)], start=(g == 0), stop=(g == NG - 1)).then_inc(down_done, 1)

            turn_rows((0, 0))

            def unit(k, r, first, last):
                u = 2 * NG * k + r
                up(u, k, r)
                if r % NG == 1 and not (last and r // NG == 1):
                    turn_rows(later((k, r // NG), 1))
                if not (first and r < 1):
                    turn_hidden(k, r - 1)
                if not (first and r < 2):
                    down(k, r - 2)

            ffn_rounds(pe, unit)
            k = NT // 2 - 1
            turn_hidden(k, 2 * NG - 1)
            down(k, 2 * NG - 2)
            down(k, 2 * NG - 1)


_INS = ['L0_attn_x', 'L0_attn_Wq', 'L0_attn_bq', 'L0_attn_Wk', 'L0_attn_bk', 'L0_attn_Wv', 'L0_attn_bv', 'L0_attn_Wo',
        'L0_attn_bo', 'L0_ffn_gate_weight', 'L0_ffn_expert_up', 'L0_ffn_expert_down', 'L0_ffn_shared_up',
        'L0_ffn_shared_down']
_OUTS = [((16, 512, 256), 'float32')]


def kernel(**inputs):
    import numpy as _np
    import concourse.bacc as _bacc
    from concourse import mybir as _mybir
    from concourse.bass_utils import run_bass_kernel_spmd as _run

    nc = _bacc.Bacc("TRN2", target_bir_lowering=False, num_devices=1)
    arrays, args = {}, []
    for name in _INS:
        a = _np.ascontiguousarray(inputs[name])
        arrays[f"in_{name}_dram"] = a
        args.append(nc.dram_tensor(f"in_{name}_dram", a.shape, _mybir.dt.from_np(a.dtype), kind="ExternalInput").ap())
    for i, (shape, dtype) in enumerate(_OUTS):
        dt = _mybir.dt.from_np(_np.dtype(dtype))
        args.append(nc.dram_tensor(f"out_{i}_dram", shape, dt, kind="ExternalOutput").ap())
    attention_and_routed_ffn(nc, *args)
    r = _run(nc, [arrays], core_ids=[0])
    got = tuple(r.results[0][f"out_{i}_dram"] for i in range(len(_OUTS)))
    return got[0]
```

```python
from contextlib import ExitStack

import concourse.bass as bass
from concourse import mybir

F32 = mybir.dt.float32
F32R = mybir.dt.float32r
U32 = mybir.dt.uint32
ALU = mybir.AluOpType
ACT = mybir.ActivationFunctionType
AX_X = mybir.AxisListType.X

P = 128
N_GROUP = 4
ROUTED_SCALING = 2.5
LN_EPS = 1e-5
Z_EPS = 1e-6
SUM_EPS = 1e-20


def attention_and_routed_ffn(
    nc: bass.Bass,
    x: bass.AP,
    Wq: bass.AP,
    bq: bass.AP,
    Wk: bass.AP,
    bk: bass.AP,
    Wv: bass.AP,
    bv: bass.AP,
    Wo: bass.AP,
    bo: bass.AP,
    gate: bass.AP,
    expert_up: bass.AP,
    expert_down: bass.AP,
    shared_up: bass.AP,
    shared_down: bass.AP,
    out: bass.AP,
):
    B, S, D = x.shape
    E, _, I = expert_up.shape
    T = B * S
    KD = D // P
    SUB = S // P
    GE = E // N_GROUP
    SH = shared_up.shape[1] // I
    NE = E + SH
    ROW = D + E
    NT = T // P
    NG = NE // GE
    REGION = T + P
    TILES = 2 * NT + N_GROUP
    SPARE = P * N_GROUP
    SLOTS = N_GROUP * REGION + SPARE
    PAIR = 2 * SUB
    assert KD == 2 and SUB == 4 and GE == 4 and SH == 4 and B % 4 == 0 and I == P and B == E

    x_rows = x.rearrange("b (s p) d -> b p s d", p=P)
    out_rows = out.rearrange("b (s p) d -> (b s) p d", p=P)
    normed = nc.dram_tensor("normed_rows", (T, ROW), F32, kind="Internal").ap()
    partial = nc.dram_tensor("attention_rows", (T, D), F32, kind="Internal").ap()
    normed_b = normed.rearrange("(b s p) r -> b p s r", s=SUB, p=P)
    by_group = nc.dram_tensor("rows_by_group", (SLOTS, ROW), F32, kind="Internal").ap()
    routed = nc.dram_tensor("routed_rows", (TILES * P, D), F32, kind="Internal").ap()
    routed_t = routed.rearrange("(t p) d -> t p d", p=P)
    x_tiles = x.rearrange("b (s p) d -> (b s) p d", p=P)
    partial_b = partial.rearrange("(b s p) d -> b p s d", s=SUB, p=P)
    normed_t = normed.rearrange("(t p) r -> t p r", p=P)
    partial_t = partial.rearrange("(t p) d -> t p d", p=P)

    def batch_of(view, index):
        return view[bass.ds(index, 1)].rearrange("o p s d -> (o p) s d")

    def tile_of(view, index):
        return view[bass.ds(index, 1)].rearrange("o p d -> (o p) d")

    with ExitStack() as ctx:
        def sb(name, shape, dt=F32):
            return ctx.enter_context(nc.sbuf_tensor(name, shape, dt))

        def sem(name):
            return ctx.enter_context(nc.semaphore(name))

        bank = [ctx.enter_context(nc.psum_tensor(f"bank{i}", [P, 512], F32)) for i in range(8)]

        CONSTS = 11
        ident = sb("ident", [P, P])
        ones_r = sb("ones_r", [P, 2], F32R)
        lower = sb("lower", [P, N_GROUP, N_GROUP])
        earlier = sb("earlier", [P, P], F32R)
        ones_wide = sb("ones_wide", [P, P], F32R)
        region_i = sb("region_i", [P, N_GROUP], U32)
        region = sb("region", [P, N_GROUP])
        pad_i = sb("pad_i", [P, N_GROUP], U32)
        pad_first = sb("pad_first", [P, N_GROUP])
        step128_i = sb("step128_i", [P, NT], U32)
        step128 = sb("step128", [P, NT])
        tile_i = sb("tile_i", [1, TILES], U32)
        tile_no = sb("tile_no", [1, TILES])
        zero_rows = sb("zero_rows", [P, ROW])
        expert_iota = sb("expert_iota", [P, E], U32)
        minus_half = sb("minus_half", [P, SUB])
        minus_one = sb("minus_one", [P, 1])
        bv_col = sb("bv_col", [P, KD])
        bq_col = sb("bq_col", [P, KD])
        bq1_col = sb("bq1_col", [P, KD])
        bk1_all = sb("bk1_all", [P, ROW])
        bvo_all = sb("bvo_all", [P, D])
        ebo_h = sb("ebo_h", [1, D], F32R)
        ebo_l = sb("ebo_l", [1, D], F32R)
        wqT_h = sb("wqT_h", [P, KD, D], F32R)
        wqT_l = sb("wqT_l", [P, KD, D], F32R)
        wkg_h = sb("wkg_h", [P, KD, ROW], F32R)
        wkg_l = sb("wkg_l", [P, KD, ROW], F32R)
        wvo_h = sb("wvo_h", [P, KD, D], F32R)
        wvo_l = sb("wvo_l", [P, KD, D], F32R)
        UPW = KD * I
        we_h = sb("we_h", [P, NE, UPW + D], F32R)
        we_l = sb("we_l", [P, NE, UPW + D], F32R)
        we_raw = sb("we_raw", [P, 2, UPW + D])
        x_in = sb("x_in", [P, 2, SUB, D])
        stats = sb("stats", [P, SUB, 6])
        mean_var = sb("mean_var", [P, 2, SUB, 2])
        var_eps = sb("var_eps", [P, SUB])
        rstd = sb("rstd", [P, 2, SUB])
        mean_neg = sb("mean_neg", [P, SUB])
        shift_neg = sb("shift_neg", [P, 2, SUB])
        xn = sb("xn", [P, 4, SUB, ROW])
        xr_h = sb("xr_h", [P, SUB, D], F32R)
        xr_l = sb("xr_l", [P, SUB, D], F32R)
        xt_h = sb("xt_h", [P, KD, S], F32R)
        xt_l = sb("xt_l", [P, KD, S], F32R)
        k_t1 = sb("k_t1", [P, SUB, ROW])
        k_f = sb("k_f", [P, SUB, D])
        k_h = sb("k_h", [P, SUB, D], F32R)
        k_l = sb("k_l", [P, SUB, D], F32R)
        q_f = sb("q_f", [P, KD, S])
        q_t1 = sb("q_t1", [P, KD, S])
        q_h = sb("q_h", [P, KD, S], F32R)
        q_l = sb("q_l", [P, KD, S], F32R)
        m_h = sb("m_h", [P, KD, D], F32R)
        m_l = sb("m_l", [P, KD, D], F32R)
        ksum = sb("ksum", [P, KD])
        PW = D + 2
        p_f = sb("p_f", [P, KD, PW])
        p_h = sb("p_h", [P, KD, PW], F32R)
        p_l = sb("p_l", [P, KD, PW], F32R)
        rz = sb("rz", [P, SUB])
        attn_out = sb("attn_out", [P, 2, SUB, D])
        GP = PAIR * N_GROUP
        r_exp = sb("r_exp", [P, PAIR, E])
        r_den = sb("r_den", [P, PAIR, E])
        score = sb("score", [P, PAIR, E])
        g_hi = sb("g_hi", [P, GP, 2])
        g_lo = sb("g_lo", [P, GP, 2])
        g_top = sb("g_top", [P, GP])
        g_mid = sb("g_mid", [P, GP])
        g_low = sb("g_low", [P, GP])
        g_second = sb("g_second", [P, GP])
        g_score = sb("g_score", [P, PAIR, N_GROUP])
        g_work = sb("g_work", [P, 4, PAIR, N_GROUP, N_GROUP])
        g_rank = sb("g_rank", [P, PAIR, N_GROUP])
        g_in = sb("g_in", [P, PAIR, N_GROUP])
        g_in_r = sb("g_in_r", [P, PAIR, N_GROUP], F32R)
        run = [sb(f"run{i}", [P, 4 + PAIR, N_GROUP]) for i in range(3)]
        run_all = sb("run_all", [P, 1 + PAIR, N_GROUP], F32R)
        top8 = sb("top8", [P, PAIR, 8])
        top8_at = sb("top8_at", [P, PAIR, 8], U32)
        fourth = sb("fourth", [P, PAIR])
        w_raw4 = sb("w_raw4", [P, PAIR, E])
        w_sum = sb("w_sum", [P, PAIR])
        w_sum_eps = sb("w_sum_eps", [P, PAIR])
        w_rsum = sb("w_rsum", [P, PAIR])
        slot = sb("slot", [P, PAIR, N_GROUP])
        slot_in = sb("slot_in", [P, PAIR, N_GROUP])
        slot_out = sb("slot_out", [P, PAIR, N_GROUP])
        slot_first = sb("slot_first", [P, PAIR])
        slot_last = sb("slot_last", [P, PAIR])
        slots_now = sb("slots_now", [P, 2, PAIR], U32)
        slots_all = sb("slots_all", [P, 2, NT])
        rows_all = sb("rows_all", [P, 2, NT], U32)
        slots_tile = sb("slots_tile", [P, 2, 2], U32)
        count = sb("count", [P, N_GROUP])
        pad_f = sb("pad_f", [P, N_GROUP])
        pad_at = sb("pad_at", [P, N_GROUP], U32)
        n_tiles = sb("n_tiles", [P, N_GROUP])
        tile_end = sb("tile_end", [1, N_GROUP])
        jump = sb("jump", [P, N_GROUP])
        tile_row = sb("tile_row", [1, TILES], U32)
        tile_expert = sb("tile_expert", [1, TILES], U32)
        fourth_min = sb("fourth_min", [P, 2])
        fourth_all = sb("fourth_all", [1, 1])
        dense = sb("dense", [1, 1], U32)
        def reused(t, shape, at=0, partitions=P):
            names = " ".join("abcd"[:len(t.shape) - 1])
            flat = t[tuple(slice(None) for _ in t.shape)].rearrange(f"p {names} -> p ({names})")
            size = 1
            for n in shape:
                size *= n
            names = " ".join("abcd"[:len(shape)])
            return flat[0:partitions, at:at + size].rearrange(f"p ({names}) -> p {names}",
                                                              **dict(zip("abcd", shape)))

        w_raw = reused(attn_out, (4, KD, D))
        woT = reused(q_t1, (KD, D))
        gate_raw = reused(q_t1, (1, D), KD * D, E)[:, 0]
        bv_wide = reused(q_t1, (KD, P), (KD + 1) * D)
        earlier_f = reused(k_f, (1, P))[:, 0]
        ones_wide_f = reused(k_f, (1, P), P)[:, 0]
        bo_all = reused(q_f, (1, D))[:, 0]
        ebo_f = reused(q_f, (1, D), D, 1)[:, 0]
        masked = reused(r_den, (PAIR, E))
        chosen = reused(r_den, (PAIR, E))
        hit = reused(g_work, (PAIR, E, 4))
        g_gt, g_ge, g_tie, g_beats = [reused(g_work, (PAIR, N_GROUP, N_GROUP), i * PAIR * N_GROUP * N_GROUP)
                                      for i in range(4)]
        shift = reused(q_t1, (N_GROUP - 1, 2, NT))
        over = reused(k_f, (N_GROUP, NT))
        jumped = reused(q_f, (1, TILES), 0, 1)[:, 0]
        group_f = reused(q_f, (1, TILES), TILES, 1)[:, 0]
        past = reused(k_t1, (N_GROUP, TILES), 0, 1)
        jumps = reused(k_t1, (N_GROUP, TILES), N_GROUP * TILES, 1)
        f_rows = reused(k_t1, (4, ROW))
        f_acc = reused(x_in, (8, D))[:, 0:2]
        f_out = reused(x_in, (8, D))[:, 2:4]
        f_x = reused(x_in, (8, D))[:, 4:6]
        f_y = reused(x_in, (8, D))[:, 6:8]
        f_got = reused(attn_out, (2, 4, D))
        fx_h = reused(xt_h, (2, KD, P))
        fx_l = reused(xt_l, (2, KD, P))
        hid = reused(k_f, (2, GE, I))
        hidw = reused(q_f, (2, GE, I))
        ht_h = reused(q_h, (2, GE, P))
        ht_l = reused(q_l, (2, GE, P))

        def sems(*names):
            return [sem(n) for n in names]

        setup_loads = [sem(f"setup_load{i}") for i in range(4)]
        bias_loaded = sem("bias_loaded")
        shared_loaded = [sem(f"shared_loaded{i}") for i in range(2)]
        expert_loaded = [sem(f"expert_loaded{i}") for i in range(2)]
        spare_stored = sem("spare_stored")
        consts_made, const_step, waits_met, consts_cast, bias_ready = sems(
            "consts_made", "const_step", "waits_met", "consts_cast", "bias_ready")
        turned, turned_hi, turned_lo, wo_copied = sems("turned", "turned_hi", "turned_lo", "wo_copied")
        folded, folded_hi, folded_lo, bvo_ready, ebo_step = sems(
            "folded", "folded_hi", "folded_lo", "bvo_ready", "ebo_step")
        expert_hi, expert_lo = sems("expert_hi", "expert_lo")
        x_loaded = [sem(f"x_loaded{i}") for i in range(2)]
        stats_done, moments_ready, var_ready, var_done, rstd_ready, xn_ready = sems(
            "stats_done", "moments_ready", "var_ready", "var_done", "rstd_ready", "xn_ready")
        xr_hi, xr_ready, xt_done, xt_hi, xt_ready = sems("xr_hi", "xr_ready", "xt_done", "xt_hi", "xt_ready")
        k_done, k_t1_ready, k_exp, k_ready, k_hi, k_lo = sems(
            "k_done", "k_t1_ready", "k_exp", "k_ready", "k_hi", "k_lo")
        q_done, q_exp, q_ready, q_hi, q_lo = sems("q_done", "q_exp", "q_ready", "q_hi", "q_lo")
        m_done, m_hi, m_lo, ksum_done, ksum_ready = sems("m_done", "m_hi", "m_lo", "ksum_done", "ksum_ready")
        p_done, p_ready, p_hi, p_lo = sems("p_done", "p_ready", "p_hi", "p_lo")
        c_done, rz_ready, attn_ready = sems("c_done", "rz_ready", "attn_ready")
        route_exp, front_step, front_ready, rank_done, rank_read, back_step, route_ready = sems(
            "route_exp", "front_step", "front_ready", "rank_done", "rank_read", "back_step", "route_ready")
        normed_stored = [sem(f"normed_stored{i}") for i in range(4)]
        attn_stored = [sem(f"attn_stored{i}") for i in range(2)]
        scattered = [sem(f"scattered{i}") for i in range(4)]
        counted, plan_step, pad_ready, padded, fourth_turned, plan_ready, rows_known = sems(
            "counted", "plan_step", "pad_ready", "padded", "fourth_turned", "plan_ready", "rows_known")
        rows_loaded = [sem(f"rows_loaded{i}") for i in range(4)]
        acc_loaded = [sem(f"acc_loaded{i}") for i in range(2)]
        got_loaded = [sem(f"got_loaded{i}") for i in range(2)]
        slots_copied = sem("slots_copied")
        fx_done, fx_hi, fx_ready = sems("fx_done", "fx_hi", "fx_ready")
        up_done, silu_ready, weighted = sems("up_done", "silu_ready", "weighted")
        ht_done, ht_hi, ht_ready, down_done = sems("ht_done", "ht_hi", "ht_ready", "down_done")
        y_ready = sem("y_ready")
        y_stored = [sem(f"y_stored{i}") for i in range(2)]
        sums_made, sum_ready, f_ready = sems("sums_made", "sum_ready", "f_ready")
        out_stored = [sem(f"out_stored{i}") for i in range(2)]

        def wait(eng, s, value):
            if isinstance(value, int) and value <= 0:
                return
            eng.wait_ge(s, value)

        def bare(eng):
            eng.sem_inc(waits_met, 1)

        def later(at, d):
            k, r = at
            return k + (r + d) // 4, (r + d) % 4

        def idx(at):
            return 4 * at[0] + at[1]

        def half(at):
            return 2 * at[0] + at[1] // 2

        def pair_later(at, d):
            k, par = at
            return k + (par + d) // 2, (par + d) % 2

        def pair_idx(at):
            return 2 * at[0] + at[1]

        def split3(dst, pairs, start=True, stop=True):
            n = 3 * len(pairs)
            k = 0
            for ah, al, bh, bl in pairs:
                for a, b in ((ah, bh), (ah, bl), (al, bh)):
                    last = nc.tensor.matmul(dst, a, b, start=start and k == 0, stop=stop and k == n - 1)
                    k += 1
            return last

        def attention_rounds(eng, body):
            body((-1, 3), False, False, True)
            body((0, 0), False, True, True)
            body((0, 1), True, True, True)
            body((0, 2), True, True, True)
            with eng.Fori(1, B // 4) as k:
                body((k - 1, 3), True, True, True)
                body((k, 0), True, True, True)
                body((k, 1), True, True, True)
                body((k, 2), True, True, True)
            body((B // 4 - 1, 3), True, True, False)
            body((B // 4, 0), True, False, False)

        UNITS = TILES + NT
        assert TILES % 4 == 0 and NT % 4 == 0

        class Step:
            def __init__(self, k, r, near=None):
                self.k, self.r, self.par = k, r, r % 2
                self.u = 4 * k + r
                self.near = self.u if near is None else near

            def kind(self, d):
                n = self.near + d
                return None if n < 0 or n >= UNITS else "routed" if n < TILES else "shared"

            def fours(self, d=0):
                return self.k + (self.r + d) // 4

            def twos(self, d=0):
                return 2 * self.k + (self.r + d) // 2

        def sparse_steps(eng, step):
            for n in range(4):
                step(Step(0, n))
            with eng.Fori(1, TILES // 4 - 1) as k:
                for r in range(4):
                    step(Step(k, r, TILES // 2))
            for n in range(TILES - 4, TILES + 8):
                step(Step(n // 4, n % 4))
            with eng.Fori(TILES // 4 + 2, UNITS // 4 - 1) as k:
                for r in range(4):
                    step(Step(k, r, TILES + 16))
            for n in range(UNITS - 4, UNITS + 4):
                step(Step(n // 4, n % 4))

        def dense_rounds(eng, unit):
            for r in range(2 * NG):
                unit(0, r, True, False)
            with eng.Fori(1, NT // 2 - 1) as k:
                for r in range(2 * NG):
                    unit(k, r, False, False)
            for r in range(2 * NG):
                unit(NT // 2 - 1, r, False, True)

        def either(eng, sparse_path, dense_path):
            eng.wait_ge(plan_ready, 1)
            is_dense = eng.value_load(dense[0:1, 0:1], min_val=0, max_val=1)
            with eng.If(is_dense == 0):
                sparse_path()
            with eng.Else():
                dense_path()

        FRONT_STEPS = 19
        BACK_STEPS = 2
        FAR = float(1 << 17)
        assert SLOTS < FAR

        block = ctx.enter_context(nc.Block())

        @block.sync
        def _(sp):
            def load_x(at):
                c = idx(at)
                wait(sp, xn_ready, c - 1)
                sp.dma_start(x_in[:, at[1] % 2], batch_of(x_rows, c)).then_inc(x_loaded[at[1] % 2], 16)

            def load_expert(at):
                c, par = idx(at), at[1] % 2
                dst = we_raw[:, par]
                wait(sp, expert_lo, SH + c - 1)
                for kd in range(KD):
                    sp.dma_start(dst[:, kd * I:(kd + 1) * I],
                                 expert_up[bass.ds(c, 1), kd * P:(kd + 1) * P, :].rearrange("o d i -> (o d) i")
                                 ).then_inc(expert_loaded[par], 16)
                sp.dma_start(dst[:, UPW:], expert_down[bass.ds(c, 1)].rearrange("o i d -> (o i) d")
                             ).then_inc(expert_loaded[par], 16)

            load_x((0, 0))
            for i, w in enumerate((Wk, Wq, Wo, Wv)):
                sp.dma_start(w_raw[:, i], w.rearrange("(c p) d -> p c d", p=P)).then_inc(setup_loads[i], 16)
                if i == 0:
                    sp.dma_start(gate_raw[:, :], gate).then_inc(bias_loaded, 16)
            sp.dma_start(bk1_all[:, 0:D], bk.partition_broadcast(P)).then_inc(bias_loaded, 16)
            sp.dma_start(bo_all[:, :], bo.partition_broadcast(P)).then_inc(bias_loaded, 16)
            sp.dma_start(bq_col[:, :], bq.rearrange("(c p) -> p c", p=P), allow_slow_non_contiguous=True
                         ).then_inc(bias_loaded, 16)
            sp.dma_start(bv_col[:, :], bv.rearrange("(c p) -> p c", p=P), allow_slow_non_contiguous=True
                         ).then_inc(bias_loaded, 16)
            load_x((0, 1))
            for j in range(SH):
                wait(sp, expert_lo, j - 1)
                dst = we_raw[:, j % 2]
                for kd in range(KD):
                    sp.dma_start(dst[:, kd * I:(kd + 1) * I], shared_up[kd * P:(kd + 1) * P, j * I:(j + 1) * I]
                                 ).then_inc(shared_loaded[j % 2], 16)
                sp.dma_start(dst[:, UPW:], shared_down[j * I:(j + 1) * I, :]).then_inc(shared_loaded[j % 2], 16)
            sp.wait_ge(consts_made, CONSTS)
            for g in range(N_GROUP):
                at = N_GROUP * REGION + g * P
                sp.dma_start(by_group[at:at + P, :], zero_rows[:, :]).then_inc(spare_stored, 16)

            def round_(at, before, now, more_x):
                if now:
                    load_expert(at)
                if more_x:
                    load_x(later(at, 3))
                if before:
                    b = later(at, -1)
                    wait(sp, attn_ready, SUB * (idx(b) + 1))
                    sp.dma_start(batch_of(partial_b, idx(b)), attn_out[:, b[1] % 2]
                                 ).then_inc(attn_stored[b[1] % 2], 16)
                    if at[1] % 2 == 0:
                        for d in (-2, -1):
                            b = later(at, d)
                            wait(sp, route_ready, half(at))
                            sp.dma_start(batch_of(normed_b, idx(b)), xn[:, b[1]]).then_inc(normed_stored[b[1]], 16)

            load_x((0, 2))
            round_((0, 0), False, True, True)
            round_((0, 1), True, True, True)
            round_((0, 2), True, True, True)
            with sp.Fori(1, B // 4 - 1) as k:
                round_((k - 1, 3), True, True, True)
                round_((k, 0), True, True, True)
                round_((k, 1), True, True, True)
                round_((k, 2), True, True, True)
            m = B // 4 - 1
            round_((m - 1, 3), True, True, True)
            round_((m, 0), True, True, True)
            for at in ((m, 1), (m, 2), (m, 3)):
                round_(at, True, True, False)
            round_((m + 1, 0), True, False, False)

            for r in range(4):
                sp.wait_ge(normed_stored[r], 16 * (B // 4))
            for par in range(2):
                sp.wait_ge(attn_stored[par], 16 * (B // 2))

            def load_rows(view, j, par):
                sp.dma_start(f_rows[:, par], tile_of(view, j)).then_inc(rows_loaded[par], 16)

            def load_rest(j, par):
                sp.dma_start(f_acc[:, par], tile_of(partial_t, j)).then_inc(acc_loaded[par], 16)
                sp.dma_start(f_x[:, par], tile_of(x_tiles, j)).then_inc(acc_loaded[par], 16)

            def store_out(j, par):
                wait(sp, f_ready, j + 1)
                sp.dma_start(tile_of(out_rows, j), f_out[:, par]).then_inc(out_stored[par], 16)

            def sparse_path():
                for r in range(4):
                    sp.wait_ge(scattered[r], 2 * SUB * 16 * (B // 4))
                sp.wait_ge(padded, 16 * N_GROUP)
                sp.wait_ge(spare_stored, 16 * N_GROUP)

                def tile_at(u):
                    return sp.value_load(tile_row[0:1, bass.ds(u, 1)], min_val=0, max_val=SLOTS - P)

                def load_unit(s, d):
                    u, r = s.u + d, (s.r + d) % 4
                    if s.kind(d) == "routed":
                        first_row = tile_at(u)
                        wait(sp, weighted, u - 3)
                        bare(sp)
                        sp.dma_start(f_rows[:, r], by_group[bass.ds(first_row, P), :]
                                     ).then_inc(rows_loaded[r], 16)
                    elif s.kind(d) == "shared":
                        if s.kind(d - 4) == "routed":
                            wait(sp, weighted, u - 3)
                        else:
                            wait(sp, fx_done, u - 3)
                        bare(sp)
                        sp.dma_start(f_rows[:, r], tile_of(normed_t, u - TILES)).then_inc(rows_loaded[r], 16)

                def step(s):
                    if s.near == 0:
                        for d in range(3):
                            load_unit(s, d)
                    load_unit(s, 3)
                    if s.kind(-3) == "routed":
                        par = 1 - s.par
                        sp.wait_ge(y_ready, s.u - 2)
                        bare(sp)
                        sp.dma_start(tile_of(routed_t, s.u - 3), f_y[:, par]).then_inc(y_stored[par], 16)
                    if s.kind(-3) == "shared":
                        sp.wait_ge(f_ready, s.u - TILES - 2)
                        bare(sp)
                        sp.dma_start(tile_of(out_rows, s.u - TILES - 3), f_out[:, 1 - s.par]
                                     ).then_inc(out_stored[1 - s.par], 16)
                    if s.kind(0) == "shared":
                        wait(sp, sum_ready, s.u - TILES - 1)
                        bare(sp)
                        load_rest(s.u - TILES, s.par)

                sparse_steps(sp, step)

            def dense_path():
                for par in range(2):
                    load_rows(normed_t, par, par)
                    load_rest(par, par)
                with sp.Fori(0, NT // 2 - 1) as k:
                    for par in range(2):
                        wait(sp, weighted, N_GROUP * (2 * k + par + 1))
                        load_rows(normed_t, 2 * k + par + 2, par)
                        store_out(2 * k + par, par)
                        load_rest(2 * k + par + 2, par)
                for par in range(2):
                    store_out(NT - 2 + par, par)

            either(sp, sparse_path, dense_path)
            for par in range(2):
                sp.wait_ge(out_stored[par], 16 * (NT // 2))

        @block.gpsimd
        def _(pool):
            G = nc.gpsimd
            for t in (ident, earlier_f, ones_wide_f):
                G.memset(t[:, :], 1.0).then_inc(const_step, 1)
            G.memset(lower[:, :, :], 1.0).then_inc(const_step, 1)
            pool.wait_ge(const_step, 4)
            G.affine_select(out=ident[:, :], in_=ident[:, :], compare_op=ALU.is_equal, fill=0.0, base=0,
                            pattern=[[-1, P]], channel_multiplier=1).then_inc(consts_made, 1)
            G.affine_select(out=earlier_f[:, :], in_=earlier_f[:, :], compare_op=ALU.is_gt, fill=0.0, base=0,
                            pattern=[[1, P]], channel_multiplier=-1).then_inc(consts_made, 1)
            G.affine_select(out=lower[:, :, :], in_=lower[:, :, :], compare_op=ALU.is_gt, fill=0.0, base=0,
                            pattern=[[1, N_GROUP], [-1, N_GROUP]], channel_multiplier=0).then_inc(consts_made, 1)
            for t, step, chan in ((expert_iota, 1, 0), (region_i, REGION, 0), (pad_i, REGION, 1), (step128_i, P, 0),
                                  (tile_i, 1, 0)):
                G.iota(t[:, :], pattern=[[step, t.shape[1]]], base=0, channel_multiplier=chan
                       ).then_inc(consts_made, 1)
            G.memset(minus_half[:, :], -0.5).then_inc(consts_made, 1)
            G.memset(ones_r[:, :].bitcast(F32), 1.0).then_inc(consts_made, 1)
            G.memset(zero_rows[:, :], 0.0).then_inc(consts_made, 1)

            def expert_rest(slot, par, value):
                pool.wait_ge(expert_hi, value)
                hi = we_h[:, bass.ds(slot, 1), :].rearrange("p o w -> p (o w)")
                lo = we_l[:, bass.ds(slot, 1), :].rearrange("p o w -> p (o w)")
                G.tensor_tensor(lo, we_raw[:, par], hi.bitcast(F32), ALU.subtract).then_inc(expert_lo, 1)

            def moments(at):
                c = idx(at)
                pool.wait_ge(moments_ready, c + 1)
                bare(pool)
                G.tensor_scalar(var_eps[:, :], mean_var[:, at[1] % 2, :, 1], LN_EPS, None, ALU.add
                                ).then_inc(var_ready, 1)
                G.tensor_scalar(mean_neg[:, :], mean_var[:, at[1] % 2, :, 0], -1.0, None, ALU.mult
                                ).then_inc(var_ready, 1)
                wait(pool, xn_ready, c - 1)
                pool.wait_ge(var_ready, 2 * (c + 1))
                G.tensor_tensor(rstd[:, at[1] % 2], var_eps[:, :], minus_half[:, :], ALU.pow
                                ).then_inc(var_done, 1)
                pool.wait_ge(var_done, c + 1)
                G.tensor_tensor(shift_neg[:, at[1] % 2], mean_neg[:, :], rstd[:, at[1] % 2], ALU.mult
                                ).then_inc(rstd_ready, 1)

            def scatter(at, subs):
                pool.wait_ge(route_ready, half(at) + 1)
                bare(pool)
                for s in subs:
                    for first_or_second in range(2):
                        t = (at[1] % 2) * SUB + s
                        G.indirect_dma_start(
                            out=by_group[:, :], in_=xn[:, at[1], s, :], in_offset=None,
                            out_offset=bass.IndirectOffsetOnAxis(ap=slots_now[:, first_or_second, t:t + 1], axis=0)
                        ).then_inc(scattered[at[1]], 16)

            def body(at, before, now, after):
                c = idx(at)
                if after:
                    moments(later(at, 1))
                if not now and not before:
                    for j in range(SH):
                        expert_rest(E + j, j % 2, j + 1)
                if now:
                    pool.wait_ge(xr_hi, c + 1)
                    G.tensor_tensor(xr_l[:, :, :], xn[:, at[1], :, 0:D], xr_h[:, :, :].bitcast(F32),
                                    ALU.subtract).then_inc(xr_ready, 1)
                two_back = not (isinstance(at[0], int) and c < 2)
                if two_back:
                    scatter(later(at, -2), (0, 1))
                if now:
                    pool.wait_ge(q_hi, c + 1)
                    G.tensor_tensor(q_l[:, :, :], q_f[:, :, :], q_h[:, :, :].bitcast(F32), ALU.subtract
                                    ).then_inc(q_lo, 1)
                if two_back:
                    scatter(later(at, -2), (2, 3))
                if now:
                    expert_rest(c, at[1] % 2, SH + c + 1)

            attention_rounds(pool, body)
            scatter((B // 4 - 1, 3), range(SUB))
            pool.wait_ge(pad_ready, 1)
            for r in range(4):
                pool.wait_ge(scattered[r], 2 * SUB * 16 * (B // 4))
            for g in range(N_GROUP):
                G.indirect_dma_start(out=by_group[:, :], in_=zero_rows[:, :], in_offset=None,
                                     out_offset=bass.IndirectOffsetOnAxis(ap=pad_at[:, g:g + 1], axis=0)
                                     ).then_inc(padded, 16)

            def sparse_path():
                pool.wait_ge(rows_known, 1)
                for par in range(2):
                    pool.wait_ge(attn_stored[par], 16 * (B // 2))
                    pool.wait_ge(y_stored[par], 16 * (TILES // 2))

                def gather(v, par):
                    wait(pool, sums_made, v - 1)
                    bare(pool)
                    G.tensor_copy(slots_tile[:, par, :], rows_all[:, :, bass.ds(v, 1)].rearrange("p f o -> p (f o)")
                                  ).then_inc(slots_copied, 1)
                    pool.wait_ge(slots_copied, v + 1)
                    bare(pool)
                    for f in range(2):
                        G.indirect_dma_start(
                            out=f_got[:, par, f, :], out_offset=None, in_=routed[:, :],
                            in_offset=bass.IndirectOffsetOnAxis(ap=slots_tile[:, par, f:f + 1], axis=0)
                        ).then_inc(got_loaded[par], 16)

                for par in range(2):
                    gather(par, par)
                with pool.Fori(1, NT // 2) as k:
                    for par in range(2):
                        gather(2 * k + par, par)

            either(pool, sparse_path, lambda: None)

        @block.scalar
        def _(act):
            A = nc.scalar
            for i, (dst, w) in enumerate(((wkg_h[:, :, 0:D], 0), (wqT_h[:, :, :], 1))):
                act.wait_ge(turned, w + 1)
                A.copy(dst, bank[w][:, :].rearrange("p (c d) -> p c d", c=KD)).then_inc(turned_hi, 1)
            act.wait_ge(turned, 3)
            A.copy(wkg_h[:, :, D:ROW], bank[3][:, 0:KD * E].rearrange("p (c e) -> p c e", c=KD)
                   ).then_inc(turned_hi, 1)
            act.wait_ge(turned, 4)
            A.copy(woT[:, :, :], bank[2][:, :].rearrange("p (c d) -> p c d", c=KD)).then_inc(wo_copied, 1)
            act.wait_ge(folded, 1)
            A.copy(wvo_h[:, :, :], bank[0][:, :].rearrange("p (c d) -> p c d", c=KD)).then_inc(folded_hi, 1)

            def expert_high(slot, par, loaded, value):
                act.wait_ge(loaded, value)
                A.copy(we_h[:, bass.ds(slot, 1), :].rearrange("p o w -> p (o w)"), we_raw[:, par]
                       ).then_inc(expert_hi, 1)

            def normalise(at):
                c, par = idx(at), at[1] % 2
                act.wait_ge(rstd_ready, c + 1)
                wait(act, normed_stored[at[1]], 16 * at[0])
                wait(act, scattered[at[1]], 2 * SUB * 16 * at[0])
                wait(act, xr_ready, c - 3)
                for s in range(SUB):
                    last = A.activation(xn[:, at[1], s, 0:D], x_in[:, par, s], ACT.Identity,
                                        bias=shift_neg[:, par, s:s + 1], scale=rstd[:, par, s:s + 1])
                last.then_inc(xn_ready, 1)

            def body(at, before, now, after):
                c, par = idx(at), at[1] % 2
                if now:
                    act.wait_ge(xn_ready, c + 1)
                    wait(act, m_done, c)
                    wait(act, xr_ready, c)
                    A.copy(xr_h[:, :, :], xn[:, at[1], :, 0:D]).then_inc(xr_hi, 1)
                    act.wait_ge(k_t1_ready, SUB * (c + 1))
                    wait(act, k_lo, c)
                    A.activation(k_f[:, :, :], k_t1[:, :, 0:D], ACT.Exp, bias=minus_one[:, 0:1]).then_inc(k_exp, 1)
                if before:
                    act.wait_ge(p_ready, c)
                    wait(act, c_done, SUB * (c - 1))
                    A.copy(p_h[:, :, :], p_f[:, :, :]).then_inc(p_hi, 1)

                def q_exponential(h):
                    act.wait_ge(q_done, KD * c + h + 1)
                    wait(act, q_lo, c)
                    A.activation(q_f[:, h, :], bank[2 + h][:, :], ACT.Exp, bias=bq_col[:, h:h + 1])
                    A.activation(q_t1[:, h, :], bank[2 + h][:, :], ACT.Identity, bias=bq1_col[:, h:h + 1]
                                 ).then_inc(q_exp, 1)

                if now:
                    q_exponential(0)
                    act.wait_ge(k_ready, c + 1)
                    wait(act, ksum_done, c)
                    A.copy(k_h[:, :, :], k_f[:, :, :]).then_inc(k_hi, 1)
                    q_exponential(1)
                    if par == 0:
                        wait(act, front_step, FRONT_STEPS * (half(at) - 1) + 1)
                    A.activation(r_exp[:, par * SUB:(par + 1) * SUB, :], k_t1[:, :, D:ROW], ACT.Exp, scale=-1.0
                                 ).then_inc(route_exp, 1)
                if after:
                    normalise(later(at, 1))
                if before:
                    b = later(at, -1)
                    wait(act, attn_stored[b[1] % 2], 16 * half(b))
                    for s in range(SUB):
                        act.wait_ge(rz_ready, SUB * (c - 1) + s + 1)
                        A.activation(attn_out[:, b[1] % 2, s], bank[s][:, 0:D], ACT.Copy, scale=rz[:, s:s + 1]
                                     ).then_inc(attn_ready, 1)
                if after:
                    act.wait_ge(xt_done, c + 2)
                    wait(act, q_done, KD * (c + 1))
                    for h in range(KD):
                        A.copy(xt_h[:, h, :], bank[4 + h][:, :]).then_inc(xt_hi, 1)
                if now:
                    act.wait_ge(q_ready, KD * (c + 1))
                    wait(act, c_done, SUB * c)
                    A.copy(q_h[:, :, :], q_f[:, :, :]).then_inc(q_hi, 1)
                    expert_high(c, par, expert_loaded[par], 48 * (half(at) + 1))
                    act.wait_ge(m_done, c + 1)
                    wait(act, p_done, c)
                    A.copy(m_h[:, :, :], bank[6][:, :].rearrange("p (c d) -> p c d", c=KD)).then_inc(m_hi, 1)
                if not now and not before:
                    for j in range(SH):
                        expert_high(E + j, j % 2, shared_loaded[j % 2], 48 * (j // 2 + 1))

            attention_rounds(act, body)

            def turn_rows(n, par):
                act.wait_ge(fx_done, n + 1)
                A.copy(fx_h[:, par], bank[4 + par][:, 0:D].rearrange("p (c t) -> p c t", c=KD)).then_inc(fx_hi, 1)

            def silu(u, par):
                act.wait_ge(up_done, u + 1)
                wait(act, ht_done, u - 1)
                A.activation(hid[:, par], bank[par][:, :].rearrange("p (e i) -> p e i", e=GE), ACT.Silu
                             ).then_inc(silu_ready, 1)

            def hidden_hi(u, par):
                act.wait_ge(ht_done, u + 1)
                wait(act, down_done, u - 1)
                A.copy(ht_h[:, par], bank[2 + par][:, :].rearrange("p (e t) -> p e t", e=GE)).then_inc(ht_hi, 1)

            def sparse_path():
                def step(s):
                    if s.near == 0:
                        turn_rows(0, 0)
                    if s.kind(0):
                        silu(s.u, s.par)
                    if s.kind(1):
                        wait(act, up_done, s.u)
                        turn_rows(s.u + 1, 1 - s.par)
                    if s.kind(-1):
                        hidden_hi(s.u - 1, 1 - s.par)
                    if s.kind(-2) == "routed":
                        act.wait_ge(down_done, s.u - 1)
                        wait(act, y_stored[s.par], 16 * s.twos(-2))
                        A.copy(f_y[:, s.par], bank[6 + s.par][:, 0:D]).then_inc(y_ready, 1)

                sparse_steps(act, step)

            def dense_path():
                turn_rows(0, 0)

                def unit(k, r, first, last):
                    u = 2 * NG * k + r
                    silu(u, r % 2)
                    if r % NG == 2 and not (last and r // NG == 1):
                        j = 2 * k + r // NG
                        wait(act, up_done, NG * j)
                        turn_rows(j + 1, 1 - r // NG)
                    if not (first and r == 0):
                        hidden_hi(u - 1, (r + 1) % 2)

                dense_rounds(act, unit)
                hidden_hi(NG * NT - 1, 1)

            either(act, sparse_path, dense_path)

        @block.vector
        def _(dve):
            V = nc.vector
            V.memset(minus_one[:, :], -1.0).then_inc(bias_ready, 1)
            V.memset(p_f[:, :, D + 1:PW], 0.0).then_inc(bias_ready, 1)
            V.memset(bk1_all[:, D:ROW], 0.0).then_inc(bias_ready, 1)
            for t in run:
                V.memset(t[:, :, :], 0.0).then_inc(bias_ready, 1)
            V.memset(run_all[:, :, :].bitcast(F32), 0.0).then_inc(bias_ready, 1)
            V.memset(fourth[:, :], 1.0).then_inc(bias_ready, 1)
            dve.wait_ge(bias_loaded, 16 * 5)
            V.tensor_scalar(bk1_all[:, 0:D], bk1_all[:, 0:D], 1.0, None, ALU.add).then_inc(bias_ready, 1)
            V.tensor_scalar(bq1_col[:, :], bq_col[:, :], 1.0, None, ALU.add).then_inc(bias_ready, 1)
            for c in range(KD):
                V.tensor_copy(bv_wide[:, c, :], bv_col[:, c:c + 1].to_broadcast([P, P])).then_inc(bias_ready, 1)
            V.tensor_scalar(ebo_f[:, :], bo_all[0:1, :], Z_EPS, None, ALU.mult).then_inc(ebo_step, 1)
            dve.wait_ge(ebo_step, 1)
            V.tensor_copy(ebo_h[:, :], ebo_f[:, :]).then_inc(ebo_step, 1)
            dve.wait_ge(ebo_step, 2)
            V.tensor_tensor(ebo_l[:, :], ebo_f[:, :], ebo_h[:, :].bitcast(F32), ALU.subtract).then_inc(ebo_step, 1)
            for i, (dst, hi, src) in enumerate((
                    (wkg_l[:, :, 0:D], wkg_h[:, :, 0:D], bank[0][:, :].rearrange("p (c d) -> p c d", c=KD)),
                    (wqT_l[:, :, :], wqT_h[:, :, :], bank[1][:, :].rearrange("p (c d) -> p c d", c=KD)),
                    (wkg_l[:, :, D:ROW], wkg_h[:, :, D:ROW],
                     bank[3][:, 0:KD * E].rearrange("p (c e) -> p c e", c=KD)))):
                dve.wait_ge(turned_hi, i + 1)
                V.tensor_tensor(dst, src, hi.bitcast(F32), ALU.subtract).then_inc(turned_lo, 1)
            dve.wait_ge(folded_hi, 1)
            V.tensor_tensor(wvo_l[:, :, :], bank[0][:, :].rearrange("p (c d) -> p c d", c=KD),
                            wvo_h[:, :, :].bitcast(F32), ALU.subtract).then_inc(folded_lo, 1)
            dve.wait_ge(folded, 2)
            V.tensor_tensor(bvo_all[:, :], bank[1][:, 0:D], bo_all[:, :], ALU.add).then_inc(bvo_ready, 1)

            def row_statistics(at, s):
                c, par = idx(at), at[1] % 2
                dve.wait_ge(x_loaded[par], 16 * (half(at) + 1))
                V.bn_stats(stats[:, s], x_in[:, par, s]).then_inc(stats_done, 1)

            def statistics(at):
                c, par = idx(at), at[1] % 2
                dve.wait_ge(stats_done, SUB * (c + 1))
                wait(dve, rstd_ready, c - 1)
                bare(dve)
                for s in range(SUB):
                    last = V.bn_aggr(mean_var[:, par, s], stats[:, s])
                last.then_inc(moments_ready, 1)

            def steps_of(semaphore, base, start=0):
                n = [start]

                def step(ins):
                    n[0] += 1
                    ins.then_inc(semaphore, 1)

                def after():
                    dve.wait_ge(semaphore, base + n[0])

                return step, after, n

            ROUTE_STEPS = (2, 4, 4, 2, 2, 2, 3)
            assert sum(ROUTE_STEPS) == FRONT_STEPS

            def route_part(pair, part):
                start = sum(ROUTE_STEPS[:part])
                step, after, n = steps_of(front_step, FRONT_STEPS * pair, start)
                if part > 0:
                    after()
                return step, after, n

            def route_scores(pair):
                step, after, n = route_part(pair, 0)
                dve.wait_ge(route_exp, 2 * pair + 2)
                step(V.tensor_scalar(r_den[:, :, :], r_exp[:, :, :], 1.0, None, ALU.add))
                after()
                step(V.reciprocal(score[:, :, :], r_den[:, :, :]))
                assert n[0] == sum(ROUTE_STEPS[:1]), n[0]

            def route_group_scores(pair):
                step, after, n = route_part(pair, 1)
                g4 = score[:, :, :].rearrange("p s (g e) -> p (s g) e", g=N_GROUP)
                V.tensor_tensor(g_hi[:, :, :], g4[:, :, 0:2], g4[:, :, 2:4], ALU.max)
                step(V.tensor_tensor(g_lo[:, :, :], g4[:, :, 0:2], g4[:, :, 2:4], ALU.min))
                after()
                V.tensor_tensor(g_top[:, :], g_hi[:, :, 0], g_hi[:, :, 1], ALU.max)
                V.tensor_tensor(g_mid[:, :], g_hi[:, :, 0], g_hi[:, :, 1], ALU.min)
                step(V.tensor_tensor(g_low[:, :], g_lo[:, :, 0], g_lo[:, :, 1], ALU.max))
                after()
                step(V.tensor_tensor(g_second[:, :], g_mid[:, :], g_low[:, :], ALU.max))
                after()
                step(V.tensor_tensor(g_score[:, :, :].rearrange("p s g -> p (s g)"), g_top[:, :], g_second[:, :],
                                     ALU.add))
                assert n[0] == sum(ROUTE_STEPS[:2]), n[0]

            def route_group_ranks(pair):
                step, after, n = route_part(pair, 2)
                wide = [P, PAIR, N_GROUP, N_GROUP]
                mine = g_score[:, :, :].unsqueeze(3).to_broadcast(wide)
                other = g_score[:, :, :].unsqueeze(2).to_broadcast(wide)
                V.tensor_tensor(g_gt[:, :, :, :], other, mine, ALU.is_gt)
                step(V.tensor_tensor(g_ge[:, :, :, :], other, mine, ALU.is_ge))
                after()
                step(V.tensor_tensor(g_tie[:, :, :, :], g_ge[:, :, :, :],
                                     lower[:, :, :].unsqueeze(1).to_broadcast(wide), ALU.mult))
                after()
                step(V.tensor_tensor(g_beats[:, :, :, :], g_gt[:, :, :, :], g_tie[:, :, :, :], ALU.max))
                after()
                step(V.tensor_reduce(g_rank[:, :, :], g_beats[:, :, :, :], AX_X, ALU.add))
                assert n[0] == sum(ROUTE_STEPS[:3]), n[0]

            def route_groups(pair):
                step, after, n = route_part(pair, 3)
                g4 = score[:, :, :].rearrange("p s (g e) -> p (s g) e", g=N_GROUP)
                wait(dve, rank_done, pair)
                V.tensor_scalar(g_in[:, :, :], g_rank[:, :, :], 2.0, None, ALU.is_lt)
                V.tensor_scalar(run[0][:, 5:, :], g_rank[:, 1:, :], 2.0, None, ALU.is_lt)
                V.scalar_tensor_tensor(out=run[0][:, 4, :], in0=g_rank[:, 0, :], scalar=2.0,
                                       in1=run_all[:, PAIR, :].bitcast(F32), op0=ALU.is_lt, op1=ALU.add)
                V.tensor_copy(run_all[:, 0, :], run_all[:, PAIR, :].bitcast(F32))
                step(V.tensor_scalar(g_in_r[:, :, :], g_rank[:, :, :], 2.0, None, ALU.is_lt))
                after()
                V.tensor_tensor(run[1][:, 4:, :], run[0][:, 4:, :], run[0][:, 3:3 + PAIR, :], ALU.add)
                step(V.tensor_tensor(masked[:, :, :].rearrange("p s (g e) -> p (s g) e", g=N_GROUP), g4,
                                     g_in[:, :, :].rearrange("p s g -> p (s g)").unsqueeze(2).to_broadcast(
                                         [P, PAIR * N_GROUP, GE]), ALU.mult))
                assert n[0] == sum(ROUTE_STEPS[:4]), n[0]

            def route_top(pair):
                step, after, n = route_part(pair, 4)
                step(V.tensor_tensor(run[2][:, 4:, :], run[1][:, 4:, :], run[1][:, 2:2 + PAIR, :], ALU.add))
                after()
                bare(dve)
                for s in range(PAIR):
                    last = V.max(top8[:, s], masked[:, s])
                step(last)
                V.tensor_tensor(run_all[:, 1:, :], run[2][:, 4:, :], run[2][:, 0:PAIR, :], ALU.add
                                ).then_inc(front_ready, 1)
                assert n[0] == sum(ROUTE_STEPS[:5]), n[0]

            def route_experts(pair):
                step, after, n = route_part(pair, 5)
                bare(dve)
                for s in range(PAIR):
                    last = V.max_index(top8_at[:, s], top8[:, s], masked[:, s])
                step(last)
                after()
                V.tensor_tensor(fourth[:, :], fourth[:, :], top8[:, :, 3], ALU.min)
                step(V.tensor_tensor(hit[:, :, :, :],
                                     expert_iota[:, :].unsqueeze(1).unsqueeze(3).to_broadcast([P, PAIR, E, 4]),
                                     top8_at[:, :, 0:4].unsqueeze(2).to_broadcast([P, PAIR, E, 4]), ALU.is_equal))
                assert n[0] == sum(ROUTE_STEPS[:6]), n[0]

            def route_weights(pair):
                step, after, n = route_part(pair, 6)
                step(V.tensor_reduce(chosen[:, :, :], hit[:, :, :, :], AX_X, ALU.add))
                after()
                step(V.tensor_tensor(w_raw4[:, :, :], chosen[:, :, :], score[:, :, :], ALU.mult))
                after()
                step(V.tensor_reduce(w_sum[:, :], w_raw4[:, :, :], AX_X, ALU.add))
                assert n[0] == sum(ROUTE_STEPS[:7]), n[0]

            def read_slots(pair):
                dve.wait_ge(rank_done, pair + 1)
                V.tensor_tensor(slot[:, :, :], bank[7][:, 0:GP].rearrange("p (s g) -> p s g", g=N_GROUP),
                                region[:, :].unsqueeze(1).to_broadcast([P, PAIR, N_GROUP]), ALU.add
                                ).then_inc(rank_read, 1)

            def route_back(at, pair):
                step, after, n = steps_of(back_step, BACK_STEPS * pair)
                dve.wait_ge(rank_read, pair + 1)
                dve.wait_ge(front_step, FRONT_STEPS * (pair + 1))
                V.tensor_scalar(w_sum_eps[:, :], w_sum[:, :], SUM_EPS, None, ALU.add)
                V.tensor_tensor(slot_in[:, :, :], slot[:, :, :], g_in[:, :, :], ALU.mult)
                step(V.scalar_tensor_tensor(out=slot_out[:, :, :], in0=g_in[:, :, :], scalar=-FAR, in1=slot[:, :, :],
                                            op0=ALU.mult, op1=ALU.add))
                after()
                V.reciprocal(w_rsum[:, :], w_sum_eps[:, :])
                V.tensor_reduce(slot_last[:, :], slot_in[:, :, :], AX_X, ALU.max)
                step(V.tensor_reduce(slot_first[:, :], slot_out[:, :, :], AX_X, ALU.min))
                after()
                for r in range(2):
                    b = later(at, r - 2)
                    wait(dve, scattered[b[1]], 2 * SUB * 16 * (b[0] + 1))
                V.scalar_tensor_tensor(
                    out=xn[:, at[1]:at[1] + 2, :, D:ROW].rearrange("p b s e -> p (b s) e"), in0=w_raw4[:, :, :],
                    scalar=ROUTED_SCALING, in1=w_rsum[:, :].unsqueeze(2).to_broadcast([P, PAIR, E]),
                    op0=ALU.mult, op1=ALU.mult)
                V.tensor_scalar(slots_now[:, 0, :], slot_first[:, :], FAR, None, ALU.add)
                V.tensor_copy(slots_now[:, 1, :], slot_last[:, :]).then_inc(route_ready, 1)
                dve.wait_ge(route_ready, pair + 1)
                V.tensor_copy(slots_all[:, :, bass.ds(PAIR * pair, PAIR)], slots_now[:, :, :])
                assert n[0] == BACK_STEPS, n[0]

            def body(at, before, now, after):
                c = idx(at)
                even = at[1] % 2 == 0
                pair = half(at)
                if after and not now:
                    for s in range(SUB):
                        row_statistics(later(at, 1), s)
                    statistics(later(at, 1))
                    dve.wait_ge(consts_made, CONSTS)
                    V.tensor_copy(earlier[:, :], earlier_f[:, :])
                    V.tensor_copy(ones_wide[:, :], ones_wide_f[:, :])
                    V.tensor_copy(region[:, :], region_i[:, :])
                    V.tensor_copy(pad_first[:, :], pad_i[:, :])
                    V.tensor_copy(step128[:, :], step128_i[:, :])
                    V.tensor_copy(tile_no[:, :], tile_i[:, :]).then_inc(consts_cast, 1)
                    dve.wait_ge(consts_cast, 1)
                for s in range(SUB):
                    if now:
                        dve.wait_ge(k_done, SUB * c + s + 1)
                        wait(dve, route_exp, c)
                        V.tensor_tensor(k_t1[:, s], bank[s % 2][:, 0:ROW], bk1_all[:, :], ALU.add
                                        ).then_inc(k_t1_ready, 1)
                        if after:
                            row_statistics(later(at, 1), s)
                    if before and even:
                        (route_groups, route_top, route_experts, route_weights)[s](pair - 1)
                if now and after:
                    statistics(later(at, 1))
                if before:
                    dve.wait_ge(p_done, c)
                    if not now:
                        dve.wait_ge(bvo_ready, 1)
                    wait(dve, ksum_ready, c)
                    wait(dve, p_hi, c - 1)
                    for h in range(KD):
                        last = V.scalar_tensor_tensor(out=p_f[:, h, 0:D], in0=bvo_all[:, :], scalar=ksum[:, h:h + 1],
                                                      in1=bank[7][:, h * D:(h + 1) * D], op0=ALU.mult, op1=ALU.add)
                    last.then_inc(p_ready, 1)
                if now:
                    dve.wait_ge(k_exp, c + 1)
                    V.scalar_tensor_tensor(out=k_f[:, :, :], in0=k_f[:, :, :], scalar=1.0, in1=k_t1[:, :, 0:D],
                                           op0=ALU.min, op1=ALU.max).then_inc(k_ready, 1)
                if before:
                    dve.wait_ge(p_hi, c)
                    V.tensor_tensor(p_l[:, :, :], p_f[:, :, :], p_h[:, :, :].bitcast(F32), ALU.subtract
                                    ).then_inc(p_lo, 1)
                if before and even:
                    read_slots(pair - 1)

                def q_elu(h):
                    dve.wait_ge(q_exp, KD * c + h + 1)
                    V.scalar_tensor_tensor(out=q_f[:, h], in0=q_f[:, h], scalar=1.0, in1=q_t1[:, h],
                                           op0=ALU.min, op1=ALU.max).then_inc(q_ready, 1)

                if now:
                    q_elu(0)
                if before and even:
                    route_back(later(at, -2), pair - 1)
                if now:
                    dve.wait_ge(k_hi, c + 1)
                    V.tensor_tensor(k_l[:, :, :], k_f[:, :, :], k_h[:, :, :].bitcast(F32), ALU.subtract
                                    ).then_inc(k_lo, 1)
                    q_elu(1)
                if before:
                    for s in range(SUB):
                        dve.wait_ge(c_done, SUB * (c - 1) + s + 1)
                        wait(dve, attn_ready, SUB * (c - 2) + s + 1)
                        V.reciprocal(rz[:, s:s + 1], bank[s][:, D:D + 1]).then_inc(rz_ready, 1)
                if now and not even:
                    route_scores(pair)
                if after:
                    for h in range(KD):
                        dve.wait_ge(xt_hi, KD * (c + 1) + h + 1)
                        V.tensor_tensor(xt_l[:, h], bank[4 + h][:, :], xt_h[:, h].bitcast(F32), ALU.subtract
                                        ).then_inc(xt_ready, 1)
                if now:
                    if not even:
                        route_group_scores(pair)
                        route_group_ranks(pair)
                    dve.wait_ge(m_hi, c + 1)
                    V.tensor_tensor(m_l[:, :, :], bank[6][:, :].rearrange("p (c d) -> p c d", c=KD),
                                    m_h[:, :, :].bitcast(F32), ALU.subtract).then_inc(m_lo, 1)
                    dve.wait_ge(ksum_done, c + 1)
                    sums = bank[1][:, 508:512].rearrange("p (h two) -> p h two", two=2)[:, :, 0]
                    V.tensor_copy(ksum[:, :], sums)
                    V.tensor_scalar(p_f[:, :, D], sums, Z_EPS, None, ALU.add).then_inc(ksum_ready, 1)

            attention_rounds(dve, body)

            step, after, _ = steps_of(plan_step, 0)
            dve.wait_ge(counted, 1)
            V.tensor_reduce(fourth_min[:, 0:1], fourth[:, :], AX_X, ALU.min)
            step(V.tensor_copy(count[:, :], bank[1][:, 0:N_GROUP]))
            after()
            step(V.tensor_tensor(pad_f[:, :], count[:, :], pad_first[:, :], ALU.add))
            V.tensor_copy(bv_wide[:, 0, :], fourth_min[:, 0:1].to_broadcast([P, P])).then_inc(fourth_turned, 1)
            step(V.tensor_tensor(over[:, :, :], count[:, :].unsqueeze(2).to_broadcast([P, N_GROUP, NT]),
                                 step128[:, :].unsqueeze(1).to_broadcast([P, N_GROUP, NT]), ALU.is_gt))
            after()
            V.tensor_copy(pad_at[:, :], pad_f[:, :]).then_inc(pad_ready, 1)
            step(V.tensor_reduce(n_tiles[:, :], over[:, :, :], AX_X, ALU.add))
            after()
            V.tensor_scalar(jump[:, :], n_tiles[:, :], -float(P), float(REGION), ALU.mult, ALU.add)
            step(V.tensor_copy(tile_end[:, 0:1], n_tiles[0:1, 0:1]))
            for g in range(1, N_GROUP):
                after()
                step(V.tensor_tensor(tile_end[:, g:g + 1], tile_end[:, g - 1:g], n_tiles[0:1, g:g + 1], ALU.add))
            after()
            step(V.tensor_tensor(past[:, :, :], tile_no[:, :].unsqueeze(1).to_broadcast([1, N_GROUP, TILES]),
                                 tile_end[:, :].unsqueeze(2).to_broadcast([1, N_GROUP, TILES]), ALU.is_ge))
            after()
            step(V.tensor_tensor(jumps[:, :, :], past[:, :, :],
                                 jump[0:1, :].unsqueeze(2).to_broadcast([1, N_GROUP, TILES]), ALU.mult))
            V.tensor_reduce(group_f[:, :], past[:, 0:N_GROUP - 1, :].rearrange("p g t -> p t g"), AX_X, ALU.add)
            after()
            step(V.tensor_reduce(jumped[:, :], jumps[:, :, :].rearrange("p g t -> p t g"), AX_X, ALU.add))
            after()
            V.scalar_tensor_tensor(out=tile_row[:, :], in0=tile_no[:, :], scalar=float(P), in1=jumped[:, :],
                                   op0=ALU.mult, op1=ALU.add)
            V.tensor_scalar(tile_expert[:, :], group_f[:, :], float(GE), None, ALU.mult)
            dve.wait_ge(fourth_turned, 2)
            step(V.tensor_reduce(fourth_all[:, :], bank[0][0:1, 0:P], AX_X, ALU.min))
            after()
            V.tensor_scalar(dense[:, :], fourth_all[:, :], 0.0, None, ALU.is_equal).then_inc(plan_ready, 1)

            step_, after_ = step, after

            def turn_rows(n, par):
                dve.wait_ge(fx_hi, n + 1)
                V.tensor_tensor(fx_l[:, par], bank[4 + par][:, 0:D].rearrange("p (c t) -> p c t", c=KD),
                                fx_h[:, par].bitcast(F32), ALU.subtract).then_inc(fx_ready, 1)

            def weigh(par, rows_par, first):
                V.tensor_tensor(hidw[:, par], hid[:, par],
                                f_rows[:, rows_par, bass.ds(first, GE)].unsqueeze(2).to_broadcast([P, GE, I]),
                                ALU.mult).then_inc(weighted, 1)

            def hidden_lo(u, par):
                dve.wait_ge(ht_hi, u + 1)
                V.tensor_tensor(ht_l[:, par], bank[2 + par][:, :].rearrange("p (e t) -> p e t", e=GE),
                                ht_h[:, par].bitcast(F32), ALU.subtract).then_inc(ht_ready, 1)

            def sparse_path():
                def gather_sums(s):
                    par, k = s.par, s.twos(-2) - TILES // 2
                    dve.wait_ge(acc_loaded[par], 32 * (k + 1))
                    V.tensor_tensor(f_acc[:, par], f_acc[:, par], f_x[:, par], ALU.add)
                    dve.wait_ge(got_loaded[par], 32 * (k + 1))
                    V.tensor_tensor(f_got[:, par, 2, :], f_got[:, par, 0, :], f_got[:, par, 1, :], ALU.add
                                    ).then_inc(sums_made, 1)

                def add_sums(s):
                    dve.wait_ge(sums_made, s.u - TILES - 1)
                    V.tensor_tensor(f_got[:, s.par, 3, :], f_acc[:, s.par], f_got[:, s.par, 2, :], ALU.add
                                    ).then_inc(sum_ready, 1)

                def finish(s):
                    v, par = s.u - 3 - TILES, 1 - s.par
                    dve.wait_ge(sum_ready, v + 1)
                    dve.wait_ge(down_done, s.u - 2)
                    wait(dve, out_stored[par], 16 * (s.twos(-3) - TILES // 2))
                    V.tensor_tensor(f_out[:, par], bank[6 + par][:, 0:D], f_got[:, par, 3, :], ALU.add
                                    ).then_inc(f_ready, 1)

                def step(s):
                    if s.near == 0:
                        turn_rows(0, 0)
                    if s.kind(-3) == "shared":
                        finish(s)
                    if s.kind(1):
                        turn_rows(s.u + 1, 1 - s.par)
                    if s.kind(0) == "routed":
                        first = dve.value_load(tile_expert[0:1, bass.ds(s.u, 1)], min_val=0, max_val=E - GE)
                        dve.wait_ge(silu_ready, s.u + 1)
                        weigh(s.par, s.r, first + D)
                    if s.kind(-1):
                        hidden_lo(s.u - 1, 1 - s.par)
                    if s.kind(-2) == "shared":
                        gather_sums(s)
                        add_sums(s)

                for g in range(N_GROUP - 1):
                    step_(V.tensor_scalar(shift[:, g], slots_all[:, :, :], float((g + 1) * REGION),
                                          jump[:, g:g + 1], ALU.is_ge, ALU.mult))
                after_()
                for g in range(N_GROUP - 1):
                    step_(V.tensor_tensor(slots_all[:, :, :], slots_all[:, :, :], shift[:, g], ALU.subtract))
                    after_()
                V.tensor_copy(rows_all[:, :, :], slots_all[:, :, :]).then_inc(rows_known, 1)
                sparse_steps(dve, step)

            def dense_path():
                def finish(k, par, j):
                    dve.wait_ge(acc_loaded[par], 32 * (k + 1))
                    V.tensor_tensor(f_acc[:, par], f_acc[:, par], f_x[:, par], ALU.add).then_inc(sums_made, 1)
                    dve.wait_ge(sums_made, j + 1)
                    dve.wait_ge(down_done, NG * (j + 1))
                    wait(dve, out_stored[par], 16 * k)
                    V.tensor_tensor(f_out[:, par], bank[6 + par][:, 0:D], f_acc[:, par], ALU.add
                                    ).then_inc(f_ready, 1)

                turn_rows(0, 0)

                def unit(k, r, first, last):
                    u = 2 * NG * k + r
                    g, par = r % NG, r // NG
                    if g < N_GROUP:
                        dve.wait_ge(silu_ready, u + 1)
                        weigh(r % 2, par, D + g * GE)
                    if g == 2 and not (last and par == 1):
                        turn_rows(2 * k + par + 1, 1 - par)
                    if not (first and r == 0):
                        hidden_lo(u - 1, (r + 1) % 2)
                    if g == 3 and not (first and r == 3):
                        j = 2 * k + par - 1
                        finish(k - 1 + par, 1 - par, j)

                dense_rounds(dve, unit)
                hidden_lo(NG * NT - 1, 1)
                finish(NT // 2 - 1, 1, NT - 1)

            either(dve, sparse_path, dense_path)

        @block.tensor
        def _(pe):
            T_ = nc.tensor
            pe.wait_ge(consts_made, 1)

            def turn_weight(w, b):
                pe.wait_ge(setup_loads[w], 16)
                for r in range(KD):
                    for c in range(KD):
                        last = T_.transpose(bank[b][:, c * D + r * P:c * D + (r + 1) * P],
                                            w_raw[:, w, r, c * P:(c + 1) * P], ident[:, :])
                last.then_inc(turned, 1)

            turn_weight(0, 0)
            turn_weight(1, 1)
            pe.wait_ge(bias_loaded, 16 * 5)
            for c in range(KD):
                last = T_.transpose(bank[3][:, c * E:(c + 1) * E], gate_raw[:, c * P:(c + 1) * P], ident[0:E, 0:E])
            last.then_inc(turned, 1)
            turn_weight(2, 2)
            pe.wait_ge(setup_loads[3], 16)
            pe.wait_ge(wo_copied, 1)
            pe.wait_ge(turned_lo, 2)
            for h in range(KD):
                for m in range(KD):
                    last = T_.matmul(bank[0][:, h * D:(h + 1) * D], w_raw[:, 3, m, h * P:(h + 1) * P], woT[:, m, :],
                                     start=(m == 0), stop=(m == KD - 1))
            last.then_inc(folded, 1)
            pe.wait_ge(bias_ready, 12)
            for m in range(KD):
                last = T_.matmul(bank[1][:, 0:D], bv_wide[:, m, :], woT[:, m, :], start=(m == 0), stop=(m == KD - 1))
            last.then_inc(folded, 1)
            pe.wait_ge(folded_lo, 1)
            pe.wait_ge(bvo_ready, 1)
            pe.wait_ge(turned_lo, 3)
            pe.wait_ge(ebo_step, 3)

            def body(at, before_, now, after):
                c = idx(at)
                even = at[1] % 2 == 0
                if now:
                    pe.wait_ge(xt_ready, KD * (c + 1))
                    for s in range(SUB):
                        if s < 2:
                            wait(pe, attn_ready, SUB * (c - 1))
                            wait(pe, ksum_ready, c)
                        else:
                            pe.wait_ge(k_t1_ready, SUB * c + s - 1)
                        cols = slice(s * P, (s + 1) * P)
                        split3(bank[s % 2][:, 0:ROW],
                               [(xt_h[:, h, cols], xt_l[:, h, cols], wkg_h[:, h, :], wkg_l[:, h, :])
                                for h in range(KD)]).then_inc(k_done, 1)
                if before_:
                    pe.wait_ge(m_lo, c)
                    wait(pe, p_ready, c - 1)
                    wait(pe, rank_read, half(at) - 1 if even else half(at))
                    for h in range(KD):
                        cols = slice(h * P, (h + 1) * P)
                        dst = bank[7][:, h * D:(h + 1) * D]
                        one = ones_wide[0:1, :]
                        T_.matmul(dst, one, ebo_h[:, :], start=True, stop=False)
                        T_.matmul(dst, one, ebo_l[:, :], start=False, stop=False)
                        last = split3(dst, [(m_h[:, d, cols], m_l[:, d, cols], wvo_h[:, d, :], wvo_l[:, d, :])
                                            for d in range(KD)], start=False)
                    last.then_inc(p_done, 1)
                if now:
                    for h in range(KD):
                        wait(pe, q_exp, KD * (c - 1) + h + 1)
                        cols = slice(h * P, (h + 1) * P)
                        split3(bank[2 + h][:, :],
                               [(wqT_h[:, d, cols], wqT_l[:, d, cols], xt_h[:, d, :], xt_l[:, d, :])
                                for d in range(KD)]).then_inc(q_done, 1)
                if before_ and even:
                    pe.wait_ge(front_ready, half(at))
                    pe.wait_ge(p_ready, c)
                    pe.wait_ge(consts_cast, 1)
                    T_.matmul(bank[7][:, 0:GP], earlier[:, :], g_in_r[:, :, :].rearrange("p s g -> p (s g)"),
                              start=True, stop=False)
                    T_.matmul(bank[7][:, 0:GP], ones_wide[:, :],
                              run_all[:, 0:PAIR, :].rearrange("p s g -> p (s g)"), start=False, stop=True
                              ).then_inc(rank_done, 1)
                if before_:
                    pe.wait_ge(p_lo, c)
                    pe.wait_ge(q_lo, c)
                    for s in range(SUB):
                        if s == 0:
                            pe.wait_ge(k_t1_ready, SUB * (c + 1) if now else SUB * c)
                        elif s == 2:
                            pe.wait_ge(q_exp, KD * (c + 1) if now else KD * c)
                        cols = slice(s * P, (s + 1) * P)
                        split3(bank[s][:, 0:PW],
                               [(q_h[:, d, cols], q_l[:, d, cols], p_h[:, d, :], p_l[:, d, :])
                                for d in range(KD)]).then_inc(c_done, 1)
                if after:
                    n = later(at, 1)
                    pe.wait_ge(xn_ready, c + 2)
                    wait(pe, xt_ready, KD * (c + 1))
                    for s in range(SUB):
                        for h in range(KD):
                            last = T_.transpose(bank[4 + h][:, s * P:(s + 1) * P], xn[:, n[1], s, h * P:(h + 1) * P],
                                                ident[:, :])
                    last.then_inc(xt_done, 1)
                if now:
                    pe.wait_ge(xr_ready, c + 1)
                    pe.wait_ge(k_lo, c + 1)
                    wait(pe, m_lo, c)
                    for h in range(KD):
                        cols = slice(h * P, (h + 1) * P)
                        last = split3(bank[6][:, h * D:(h + 1) * D],
                                      [(xr_h[:, s, cols], xr_l[:, s, cols], k_h[:, s, :], k_l[:, s, :])
                                       for s in range(SUB)])
                    last.then_inc(m_done, 1)
                    if before_:
                        pe.wait_ge(attn_ready, SUB * (c - 1) + 2)
                    for h in range(KD):
                        cols = slice(h * P, (h + 1) * P)
                        for n, kk in enumerate((k_h, k_l)):
                            for s in range(SUB):
                                last = T_.matmul(bank[1][:, 508 + 2 * h:510 + 2 * h], kk[:, s, cols], ones_r[:, :],
                                                 start=(n == 0 and s == 0), stop=(n == 1 and s == SUB - 1))
                    last.then_inc(ksum_done, 1)

            attention_rounds(pe, body)

            pe.wait_ge(attn_ready, SUB * B)
            T_.matmul(bank[1][:, 0:N_GROUP], ones_wide[:, :], run_all[:, PAIR, :], start=True, stop=True
                      ).then_inc(counted, 1)
            pe.wait_ge(fourth_turned, 1)
            T_.transpose(bank[0][:, 0:P], bv_wide[:, 0, :], ident[:, :]).then_inc(fourth_turned, 1)
            pe.wait_ge(expert_lo, NE)

            def turn_rows(buf, par, count_):
                pe.wait_ge(rows_loaded[buf], count_)
                for h in range(KD):
                    last = T_.transpose(bank[4 + par][:, h * P:(h + 1) * P], f_rows[:, buf, h * P:(h + 1) * P],
                                        ident[:, :])
                last.then_inc(fx_done, 1)

            def up(u, par, rows_par, first):
                wait(pe, silu_ready, u - 1)
                mov = [[w[:, bass.ds(first, GE), h * I:(h + 1) * I] for w in (we_h, we_l)] for h in range(KD)]
                split3(bank[par][:, :].rearrange("p (e i) -> p e i", e=GE),
                       [(fx_h[:, rows_par, h], fx_l[:, rows_par, h], mov[h][0], mov[h][1])
                        for h in range(KD)]).then_inc(up_done, 1)

            def turn_hidden(u, par, src):
                wait(pe, ht_ready, u - 1)
                for e in range(GE):
                    last = T_.transpose(bank[2 + par][:, e * P:(e + 1) * P], src[:, par, e, :], ident[:, :])
                last.then_inc(ht_done, 1)

            def down(u, par, y_par, first, start, stop):
                pe.wait_ge(ht_ready, u + 1)

                def moving(w, e):
                    return w[:, bass.ds(first + e, 1), UPW:].rearrange("p o d -> p (o d)")

                split3(bank[6 + y_par][:, 0:D],
                       [(ht_h[:, par, e], ht_l[:, par, e], moving(we_h, e), moving(we_l, e)) for e in range(GE)],
                       start=start, stop=stop).then_inc(down_done, 1)

            def sparse_path():
                def first_expert(s, d):
                    if s.kind(d) == "shared":
                        return E
                    return pe.value_load(tile_expert[0:1, bass.ds(s.u + d, 1)], min_val=0, max_val=E - GE)

                def step(s):
                    if s.near == 0:
                        turn_rows(0, 0, 16)
                    if s.kind(0):
                        first = first_expert(s, 0)
                        pe.wait_ge(fx_ready, s.u + 1)
                        up(s.u, s.par, s.par, first)
                    if s.kind(1):
                        wait(pe, fx_ready, s.u)
                        turn_rows((s.r + 1) % 4, 1 - s.par, 16 * (s.fours(1) + 1))
                    if s.kind(-1):
                        if s.kind(-1) == "routed":
                            pe.wait_ge(weighted, s.u)
                        else:
                            pe.wait_ge(silu_ready, s.u)
                        turn_hidden(s.u - 1, 1 - s.par, hidw if s.kind(-1) == "routed" else hid)
                    if s.kind(-2):
                        first = first_expert(s, -2)
                        if s.kind(-4) == "shared":
                            pe.wait_ge(f_ready, s.u - 3 - TILES)
                        else:
                            wait(pe, y_ready, s.u - 3)
                        down(s.u - 2, s.par, s.par, first, True, True)

                sparse_steps(pe, step)

            def dense_path():
                turn_rows(0, 0, 16)

                def unit(k, r, first, last):
                    u = 2 * NG * k + r
                    g, par = r % NG, r // NG
                    if g == 0:
                        pe.wait_ge(fx_ready, 2 * k + par + 1)
                    up(u, r % 2, par, g * GE)
                    if g == 1 and not (last and par == 1):
                        wait(pe, fx_ready, 2 * k + par)
                        turn_rows(1 - par, 1 - par, 16 * (k + 1 + par))
                    if not (first and r < 1):
                        turn(k, r - 1)
                    if not (first and r < 2):
                        fold(k, r - 2)

                def turn(k, r):
                    u = 2 * NG * k + r
                    g = r % NG
                    if g < N_GROUP:
                        pe.wait_ge(weighted, N_GROUP * (2 * k + r // NG) + g + 1)
                    else:
                        pe.wait_ge(silu_ready, u + 1)
                    turn_hidden(u, r % 2, hidw if g < N_GROUP else hid)

                def fold(k, r):
                    g, par = r % NG, (r // NG) % 2
                    if g == 0:
                        wait(pe, f_ready, 2 * k + r // NG - 1)
                    down(2 * NG * k + r, r % 2, par, g * GE, g == 0, g == NG - 1)

                dense_rounds(pe, unit)
                k = NT // 2 - 1
                turn(k, 2 * NG - 1)
                fold(k, 2 * NG - 2)
                fold(k, 2 * NG - 1)

            either(pe, sparse_path, dense_path)


_INS = ['L0_attn_x', 'L0_attn_Wq', 'L0_attn_bq', 'L0_attn_Wk', 'L0_attn_bk', 'L0_attn_Wv', 'L0_attn_bv', 'L0_attn_Wo',
        'L0_attn_bo', 'L0_ffn_gate_weight', 'L0_ffn_expert_up', 'L0_ffn_expert_down', 'L0_ffn_shared_up',
        'L0_ffn_shared_down']
_OUTS = [((16, 512, 256), 'float32')]


def kernel(**inputs):
    import numpy as _np
    import concourse.bacc as _bacc
    from concourse import mybir as _mybir
    from concourse.bass_utils import run_bass_kernel_spmd as _run

    nc = _bacc.Bacc("TRN2", target_bir_lowering=False, num_devices=1)
    arrays, args = {}, []
    for name in _INS:
        a = _np.ascontiguousarray(inputs[name])
        arrays[f"in_{name}_dram"] = a
        args.append(nc.dram_tensor(f"in_{name}_dram", a.shape, _mybir.dt.from_np(a.dtype), kind="ExternalInput").ap())
    for i, (shape, dtype) in enumerate(_OUTS):
        dt = _mybir.dt.from_np(_np.dtype(dtype))
        args.append(nc.dram_tensor(f"out_{i}_dram", shape, dt, kind="ExternalOutput").ap())
    attention_and_routed_ffn(nc, *args)
    r = _run(nc, [arrays], core_ids=[0])
    got = tuple(r.results[0][f"out_{i}_dram"] for i in range(len(_OUTS)))
    return got[0]
```

```python
from contextlib import ExitStack

import concourse.bass as bass
from concourse import mybir

F32 = mybir.dt.float32
F32R = mybir.dt.float32r
U32 = mybir.dt.uint32
ALU = mybir.AluOpType
ACT = mybir.ActivationFunctionType
AX_X = mybir.AxisListType.X

P = 128
N_GROUP = 4
ROUTED_SCALING = 2.5
LN_EPS = 1e-5
Z_EPS = 1e-6
SUM_EPS = 1e-20


def attention_and_routed_ffn(
    nc: bass.Bass,
    x: bass.AP,
    Wq: bass.AP,
    bq: bass.AP,
    Wk: bass.AP,
    bk: bass.AP,
    Wv: bass.AP,
    bv: bass.AP,
    Wo: bass.AP,
    bo: bass.AP,
    gate: bass.AP,
    expert_up: bass.AP,
    expert_down: bass.AP,
    shared_up: bass.AP,
    shared_down: bass.AP,
    out: bass.AP,
):
    B, S, D = x.shape
    E, _, I = expert_up.shape
    T = B * S
    KD = D // P
    SUB = S // P
    GE = E // N_GROUP
    SH = shared_up.shape[1] // I
    NE = E + SH
    ROW = D + E
    NT = T // P
    NG = NE // GE
    UR = 2 * P
    REGION = T + UR
    ROUTED = 2 * T // UR + N_GROUP
    SHARED = T // UR
    SPARE = UR * N_GROUP
    SLOTS = N_GROUP * REGION + SPARE
    PAIR = 2 * SUB
    assert KD == 2 and SUB == 4 and GE == 4 and SH == 4 and B % 4 == 0 and I == P and B == E

    x_rows = x.rearrange("b (s p) d -> b p s d", p=P)
    out_rows = out.rearrange("b (s p) d -> (b s) p d", p=P)
    normed = nc.dram_tensor("normed_rows", (T, ROW), F32, kind="Internal").ap()
    partial = nc.dram_tensor("attention_rows", (T, D), F32, kind="Internal").ap()
    normed_b = normed.rearrange("(b s p) r -> b p s r", s=SUB, p=P)
    by_group = nc.dram_tensor("rows_by_group", (SLOTS, ROW), F32, kind="Internal").ap()
    routed = nc.dram_tensor("routed_rows", (ROUTED * UR, D), F32, kind="Internal").ap()
    routed_u = routed.rearrange("(u s p) d -> u p s d", s=2, p=P)
    x_tiles = x.rearrange("b (s p) d -> (b s) p d", p=P)
    partial_b = partial.rearrange("(b s p) d -> b p s d", s=SUB, p=P)
    normed_t = normed.rearrange("(t p) r -> t p r", p=P)
    normed_u = normed.rearrange("(u s p) r -> u p s r", s=2, p=P)
    partial_u = partial.rearrange("(u s p) d -> u p s d", s=2, p=P)
    x_u = x.rearrange("b (u s p) d -> (b u) p s d", s=2, p=P)
    out_u = out.rearrange("b (u s p) d -> (b u) p s d", s=2, p=P)
    partial_t = partial.rearrange("(t p) d -> t p d", p=P)

    def batch_of(view, index):
        return view[bass.ds(index, 1)].rearrange("o p s d -> (o p) s d")

    def tile_of(view, index):
        return view[bass.ds(index, 1)].rearrange("o p d -> (o p) d")

    with ExitStack() as ctx:
        def sb(name, shape, dt=F32):
            return ctx.enter_context(nc.sbuf_tensor(name, shape, dt))

        def sem(name):
            return ctx.enter_context(nc.semaphore(name))

        bank = [ctx.enter_context(nc.psum_tensor(f"bank{i}", [P, 512], F32)) for i in range(8)]

        CONSTS = 8
        ident = sb("ident", [P, P])
        lower = sb("lower", [P, N_GROUP, N_GROUP])
        earlier = sb("earlier", [P, P], F32R)
        ones_wide = sb("ones_wide", [P, P], F32R)
        region_i = sb("region_i", [P, N_GROUP], U32)
        region = sb("region", [P, N_GROUP])
        unit_rows_i = sb("unit_rows_i", [P, SHARED], U32)
        unit_rows = sb("unit_rows", [P, SHARED])
        unit_i = sb("unit_i", [1, ROUTED], U32)
        unit_no = sb("unit_no", [1, ROUTED])
        zero_rows = sb("zero_rows", [P, ROW])
        minus_half = sb("minus_half", [P, SUB])
        minus_one = sb("minus_one", [P, 1])
        bv_col = sb("bv_col", [P, KD])
        kb = sb("kb", [2, ROW], F32R)
        qb = sb("qb", [2, D], F32R)
        PW = D + 2
        bo_all = sb("bo_all", [96, D])
        bias_all = sb("bias_all", [96, PW])
        ksum_rows = sb("ksum_rows", [96, D], F32R)
        bias_rows = sb("bias_rows", [96, PW], F32R)
        wqT_h = sb("wqT_h", [P, KD, D], F32R)
        wqT_l = sb("wqT_l", [P, KD, D], F32R)
        wkg_h = sb("wkg_h", [P, KD, ROW], F32R)
        wkg_l = sb("wkg_l", [P, KD, ROW], F32R)
        wvo_h = sb("wvo_h", [P, KD, D], F32R)
        wvo_l = sb("wvo_l", [P, KD, D], F32R)
        UPW = KD * I
        we_h = sb("we_h", [P, NE, UPW + D], F32R)
        we_l = sb("we_l", [P, NE, UPW + D], F32R)
        we_raw = sb("we_raw", [P, 2, UPW + D])
        x_in = sb("x_in", [P, 2, SUB, D])
        stats = sb("stats", [P, SUB, 6])
        mean_var = sb("mean_var", [P, 2, SUB, 2])
        var_eps = sb("var_eps", [P, SUB])
        rstd = sb("rstd", [P, 2, SUB])
        mean_neg = sb("mean_neg", [P, SUB])
        shift_neg = sb("shift_neg", [P, 2, SUB])
        xn = sb("xn", [P, 4, SUB, ROW])
        xr_h = sb("xr_h", [P, SUB, D], F32R)
        xr_l = sb("xr_l", [P, SUB, D], F32R)
        xt_h = sb("xt_h", [P, KD, S], F32R)
        xt_l = sb("xt_l", [P, KD, S], F32R)
        k_f = sb("k_f", [P, SUB, D])
        k_h = sb("k_h", [P, SUB, D], F32R)
        k_l = sb("k_l", [P, SUB, D], F32R)
        q_f = sb("q_f", [P, KD, S])
        q_h = sb("q_h", [P, KD, S], F32R)
        q_l = sb("q_l", [P, KD, S], F32R)
        m_h = sb("m_h", [P, KD, D], F32R)
        m_l = sb("m_l", [P, KD, D], F32R)
        p_h = sb("p_h", [P, KD, PW], F32R)
        p_l = sb("p_l", [P, KD, PW], F32R)
        rz = sb("rz", [P, SUB])
        work = sb("work", [P, 4 * ROW])
        attn_out = sb("attn_out", [P, 2, SUB, D])
        GP = PAIR * N_GROUP
        r_exp = sb("r_exp", [P, PAIR, E])
        r_den = sb("r_den", [P, PAIR, E])
        score = sb("score", [P, PAIR, E])
        g_hi = sb("g_hi", [P, GP, 2])
        g_lo = sb("g_lo", [P, GP, 2])
        g_top = sb("g_top", [P, GP])
        g_mid = sb("g_mid", [P, GP])
        g_low = sb("g_low", [P, GP])
        g_second = sb("g_second", [P, GP])
        g_score = sb("g_score", [P, PAIR, N_GROUP])
        g_work = sb("g_work", [P, 4, PAIR, N_GROUP, N_GROUP])
        g_rank = sb("g_rank", [P, PAIR, N_GROUP])
        g_in = sb("g_in", [P, PAIR, N_GROUP])
        g_in_r = sb("g_in_r", [P, PAIR, N_GROUP], F32R)
        run = [sb(f"run{i}", [P, 4 + PAIR, N_GROUP]) for i in range(3)]
        run_all = sb("run_all", [P, 1 + PAIR, N_GROUP], F32R)
        top8 = sb("top8", [P, PAIR, 8])
        fourth = sb("fourth", [P, PAIR])
        w_raw4 = sb("w_raw4", [P, PAIR, E])
        w_sum = sb("w_sum", [P, PAIR])
        w_sum_eps = sb("w_sum_eps", [P, PAIR])
        w_rsum = sb("w_rsum", [P, PAIR])
        slot = sb("slot", [P, PAIR, N_GROUP])
        slot_in = sb("slot_in", [P, PAIR, N_GROUP])
        slot_out = sb("slot_out", [P, PAIR, N_GROUP])
        slot_first = sb("slot_first", [P, PAIR])
        slot_last = sb("slot_last", [P, PAIR])
        slots_now = sb("slots_now", [P, 2, PAIR], U32)
        slots_all = sb("slots_all", [P, 2, NT])
        rows_all = sb("rows_all", [P, 2, NT], U32)
        rows_now = sb("rows_now", [P, 2, 4], U32)
        counts = sb("counts", [P, 2 * N_GROUP])
        pad_f = sb("pad_f", [1, N_GROUP])
        pad_at = sb("pad_at", [1, N_GROUP], U32)
        n_units = sb("n_units", [P, 2 * N_GROUP])
        unit_end = sb("unit_end", [1, 2 * N_GROUP])
        jump = sb("jump", [P, N_GROUP])
        unit_row = sb("unit_row", [1, ROUTED], U32)
        rows_stage = sb("rows_stage", [1, ROUTED], U32)
        unit_expert = sb("unit_expert", [1, ROUTED], U32)
        fourth_min = sb("fourth_min", [P, 2])
        fourth_all = sb("fourth_all", [1, 1])
        dense = sb("dense", [1, 1], U32)
        def reused(t, shape, at=0, partitions=P):
            names = " ".join("abcd"[:len(t.shape) - 1])
            flat = t[tuple(slice(None) for _ in t.shape)].rearrange(f"p {names} -> p ({names})")
            size = 1
            for n in shape:
                size *= n
            names = " ".join("abcd"[:len(shape)])
            return flat[0:partitions, at:at + size].rearrange(f"p ({names}) -> p {names}",
                                                              **dict(zip("abcd", shape)))

        w_raw = reused(attn_out, (4, KD, D))
        woT = reused(work, (KD, D))
        gate_raw = reused(work, (1, D), KD * D, E)[:, 0]
        bv_wide = reused(work, (KD, P), (KD + 1) * D)
        bk_row = reused(k_f, (1, ROW), 2 * P, 2)[:, 0]
        bq_row = reused(k_f, (1, D), 2 * P + ROW, 2)[:, 0]
        kb_h, kb_l = [reused(k_l, (1, ROW), i * ROW, 2)[:, 0] for i in range(2)]
        qb_h, qb_l = [reused(k_h, (1, D), i * D, 2)[:, 0] for i in range(2)]
        eb_all = reused(q_f, (1, PW), 0, 96)[:, 0]
        bias_h, bias_l = [reused(p_h, (1, PW), i * PW, 96)[:, 0] for i in range(2)]
        eb_h, eb_l = [reused(q_l, (1, PW), i * PW, 96)[:, 0] for i in range(2)]
        earlier_f = reused(k_f, (1, P))[:, 0]
        ones_wide_f = reused(k_f, (1, P), P)[:, 0]
        masked = reused(r_den, (PAIR, E))
        marked = reused(g_work, (PAIR, E))
        g_gt, g_ge, g_tie, g_beats = [reused(g_work, (PAIR, N_GROUP, N_GROUP), i * PAIR * N_GROUP * N_GROUP)
                                      for i in range(4)]
        shift = reused(work, (N_GROUP - 1, 2, NT))
        over = reused(k_f, (2 * N_GROUP, SHARED))
        jumped = reused(q_f, (1, ROUTED), 0, 1)[:, 0]
        group_f = reused(q_f, (1, ROUTED), ROUTED, 1)[:, 0]
        past = reused(work, (2 * N_GROUP, ROUTED), 0, 1)
        jumps = reused(q_f, (N_GROUP, ROUTED), 4 * ROUTED, 1)
        ended, late_from, late = [reused(k_f, (1, ROUTED), 2 * N_GROUP * SHARED + i * ROUTED, 1)[:, 0] for i in range(3)]
        f_rows = reused(xn, (4, 2, ROW))
        f_acc = reused(xn, (2, 2, D), 8 * ROW)
        f_x = reused(xn, (2, 2, D), 8 * ROW + 4 * D)
        f_y = reused(x_in, (2, 2, D))
        f_out = reused(x_in, (2, 2, D), 4 * D)
        f_got = reused(attn_out, (2, 2, 2, D))
        fx_h = reused(xt_h, (2, KD, 2, P))
        fx_l = reused(xt_l, (2, KD, 2, P))
        hid = [reused(t, (2, GE, I)) for t in (k_f, we_raw)]
        hidw = [reused(t, (2, GE, I)) for t in (q_f, work)]
        ht_h = [reused(t, (2, GE, P)) for t in (q_h, k_h)]
        ht_l = [reused(t, (2, GE, P)) for t in (q_l, k_l)]

        def sems(*names):
            return [sem(n) for n in names]

        setup_loads = [sem(f"setup_load{i}") for i in range(4)]
        bias_loaded = sem("bias_loaded")
        shared_loaded = [sem(f"shared_loaded{i}") for i in range(2)]
        expert_loaded = [sem(f"expert_loaded{i}") for i in range(2)]
        zeros_stored = sem("zeros_stored")
        consts_made, const_step, waits_met, consts_cast = sems(
            "consts_made", "const_step", "waits_met", "consts_cast")
        turned, turned_hi, turned_lo, wo_copied = sems("turned", "turned_hi", "turned_lo", "wo_copied")
        folded, folded_hi, folded_lo, bv_ready, bias_step, row_biases, bias_rows_ready = sems(
            "folded", "folded_hi", "folded_lo", "bv_ready", "bias_step", "row_biases", "bias_rows_ready")
        expert_hi, expert_lo = sems("expert_hi", "expert_lo")
        x_loaded = [sem(f"x_loaded{i}") for i in range(2)]
        stats_done, moments_ready, var_ready, var_done, rstd_ready, xn_ready = sems(
            "stats_done", "moments_ready", "var_ready", "var_done", "rstd_ready", "xn_ready")
        xr_hi, xr_ready, xt_done, xt_hi, xt_ready = sems("xr_hi", "xr_ready", "xt_done", "xt_hi", "xt_ready")
        k_done, k_exp, k_ready, k_hi, k_lo = sems("k_done", "k_exp", "k_ready", "k_hi", "k_lo")
        q_done, q_exp, q_ready, q_hi, q_lo = sems("q_done", "q_exp", "q_ready", "q_hi", "q_lo")
        m_done, m_hi, m_lo, ksum_done, ksum_hi, ksum_ready = sems(
            "m_done", "m_hi", "m_lo", "ksum_done", "ksum_hi", "ksum_ready")
        p_done, p_hi, p_lo = sems("p_done", "p_hi", "p_lo")
        c_done, rz_ready, attn_ready = sems("c_done", "rz_ready", "attn_ready")
        front_step, front_ready, rank_done, rank_read, back_step, route_ready = sems(
            "front_step", "front_ready", "rank_done", "rank_read", "back_step", "route_ready")
        normed_stored = [sem(f"normed_stored{i}") for i in range(4)]
        attn_stored = [sem(f"attn_stored{i}") for i in range(2)]
        scattered = [sem(f"scattered{i}") for i in range(4)]
        counted, plan_step, pad_ready, fourth_turned, plan_ready, rows_known = sems(
            "counted", "plan_step", "pad_ready", "fourth_turned", "plan_ready", "rows_known")
        rows_loaded = [sem(f"rows_loaded{i}") for i in range(4)]
        acc_loaded = [sem(f"acc_loaded{i}") for i in range(2)]
        got_loaded = [sem(f"got_loaded{i}") for i in range(2)]
        slots_copied = sem("slots_copied")
        fx_done, fx_hi, fx_ready = sems("fx_done", "fx_hi", "fx_ready")
        up_done, silu_ready, weighted = sems("up_done", "silu_ready", "weighted")
        ht_done, ht_hi, ht_ready, down_done = sems("ht_done", "ht_hi", "ht_ready", "down_done")
        y_ready = sem("y_ready")
        y_stored = [sem(f"y_stored{i}") for i in range(2)]
        sums_made, sum_ready, f_ready = sems("sums_made", "sum_ready", "f_ready")
        out_stored = [sem(f"out_stored{i}") for i in range(2)]

        def wait(eng, s, value):
            if isinstance(value, int) and value <= 0:
                return
            eng.wait_ge(s, value)

        def bare(eng):
            eng.sem_inc(waits_met, 1)

        def later(at, d):
            k, r = at
            return k + (r + d) // 4, (r + d) % 4

        def idx(at):
            return 4 * at[0] + at[1]

        def half(at):
            return 2 * at[0] + at[1] // 2

        def pair_later(at, d):
            k, par = at
            return k + (par + d) // 2, (par + d) % 2

        def pair_idx(at):
            return 2 * at[0] + at[1]

        def split3(dst, pairs, start=True, stop=True):
            n = 3 * len(pairs)
            k = 0
            for ah, al, bh, bl in pairs:
                for a, b in ((ah, bh), (ah, bl), (al, bh)):
                    last = nc.tensor.matmul(dst, a, b, start=start and k == 0, stop=stop and k == n - 1)
                    k += 1
            return last

        def attention_rounds(eng, body):
            body((-1, 3), False, False, True)
            body((0, 0), False, True, True)
            body((0, 1), True, True, True)
            body((0, 2), True, True, True)
            with eng.Fori(1, B // 4) as k:
                body((k - 1, 3), True, True, True)
                body((k, 0), True, True, True)
                body((k, 1), True, True, True)
                body((k, 2), True, True, True)
            body((B // 4 - 1, 3), True, True, False)
            body((B // 4, 0), True, False, False)

        UNITS = ROUTED + SHARED
        assert ROUTED % 4 == 0 and SHARED % 4 == 0

        class Step:
            def __init__(self, k, r, near=None):
                self.k, self.r, self.par = k, r, r % 2
                self.u = 4 * k + r
                self.near = self.u if near is None else near

            def kind(self, d):
                n = self.near + d
                return None if n < 0 or n >= UNITS else "routed" if n < ROUTED else "shared"

            def fours(self, d=0):
                return self.k + (self.r + d) // 4

            def twos(self, d=0):
                return 2 * self.k + (self.r + d) // 2

        def sparse_steps(eng, step):
            for n in range(4):
                step(Step(0, n))
            with eng.Fori(1, ROUTED // 4 - 1) as k:
                for r in range(4):
                    step(Step(k, r, ROUTED // 2))
            for n in range(ROUTED - 4, ROUTED + 8):
                step(Step(n // 4, n % 4))
            with eng.Fori(ROUTED // 4 + 2, UNITS // 4 - 1) as k:
                for r in range(4):
                    step(Step(k, r, ROUTED + 16))
            for n in range(UNITS - 4, UNITS + 4):
                step(Step(n // 4, n % 4))

        def dense_rounds(eng, unit):
            for r in range(2 * NG):
                unit(0, r, True, False)
            with eng.Fori(1, NT // 2 - 1) as k:
                for r in range(2 * NG):
                    unit(k, r, False, False)
            for r in range(2 * NG):
                unit(NT // 2 - 1, r, False, True)

        def either(eng, sparse_path, dense_path):
            eng.wait_ge(plan_ready, 1)
            is_dense = eng.value_load(dense[0:1, 0:1], min_val=0, max_val=1)
            with eng.If(is_dense == 0):
                sparse_path()
            with eng.Else():
                dense_path()

        SCATTERS = 2 * SUB * 16
        ZEROS = 16 * N_GROUP
        FRONT_STEPS = 18
        BACK_STEPS = 2
        FAR = float(1 << 17)
        assert SLOTS < FAR

        def store_zeros(eng, first_row):
            eng.dma_start(by_group[bass.ds(first_row, UR), :].rearrange("(s p) r -> p s r", p=P),
                          zero_rows[:, :].unsqueeze(1).to_broadcast([P, 2, ROW])).then_inc(zeros_stored, 16)

        block = ctx.enter_context(nc.Block())

        @block.sync
        def _(sp):
            def load_x(at):
                c = idx(at)
                wait(sp, xn_ready, c - 1)
                sp.dma_start(x_in[:, at[1] % 2], batch_of(x_rows, c)).then_inc(x_loaded[at[1] % 2], 16)

            def load_expert(at):
                c, par = idx(at), at[1] % 2
                dst = we_raw[:, par]
                wait(sp, expert_lo, c - 1)
                for kd in range(KD):
                    sp.dma_start(dst[:, kd * I:(kd + 1) * I],
                                 expert_up[bass.ds(c, 1), kd * P:(kd + 1) * P, :].rearrange("o d i -> (o d) i")
                                 ).then_inc(expert_loaded[par], 16)
                sp.dma_start(dst[:, UPW:], expert_down[bass.ds(c, 1)].rearrange("o i d -> (o i) d")
                             ).then_inc(expert_loaded[par], 16)

            load_x((0, 0))

            def load_weights(i, w):
                sp.dma_start(w_raw[:, i], w.rearrange("(c p) d -> p c d", p=P)).then_inc(setup_loads[i], 16)

            load_weights(0, Wk)
            sp.dma_start(gate_raw[:, :], gate).then_inc(bias_loaded, 16)
            load_weights(1, Wq)
            sp.dma_start(bk_row[:, 0:D], bk.partition_broadcast(2)).then_inc(bias_loaded, 16)
            sp.dma_start(bo_all[:, :], bo.partition_broadcast(96)).then_inc(bias_loaded, 16)
            sp.dma_start(bq_row[:, :], bq.partition_broadcast(2)).then_inc(bias_loaded, 16)
            sp.dma_start(bv_col[:, :], bv.rearrange("(c p) -> p c", p=P), allow_slow_non_contiguous=True
                         ).then_inc(bias_loaded, 16)
            load_x((0, 1))
            load_weights(2, Wo)
            load_weights(3, Wv)
            sp.wait_ge(consts_made, CONSTS)
            for g in range(N_GROUP):
                store_zeros(sp, N_GROUP * REGION + g * UR)

            def round_(at, before, now, more_x, more_experts=True):
                if more_experts:
                    load_expert(later(at, 1))
                if more_x:
                    load_x(later(at, 3))
                if before:
                    b = later(at, -1)
                    wait(sp, attn_ready, SUB * (idx(b) + 1))
                    sp.dma_start(batch_of(partial_b, idx(b)), attn_out[:, b[1] % 2]
                                 ).then_inc(attn_stored[b[1] % 2], 16)
                    if at[1] % 2 == 0:
                        for d in (-2, -1):
                            b = later(at, d)
                            wait(sp, route_ready, half(at))
                            sp.dma_start(batch_of(normed_b, idx(b)), xn[:, b[1]]).then_inc(normed_stored[b[1]], 16)

            load_x((0, 2))
            load_expert((0, 0))
            round_((0, 0), False, True, True)
            round_((0, 1), True, True, True)
            round_((0, 2), True, True, True)
            with sp.Fori(1, B // 4 - 1) as k:
                round_((k - 1, 3), True, True, True)
                round_((k, 0), True, True, True)
                round_((k, 1), True, True, True)
                round_((k, 2), True, True, True)
            m = B // 4 - 1
            round_((m - 1, 3), True, True, True)
            round_((m, 0), True, True, True)
            for r in range(1, 4):
                round_((m, r), True, True, False, r < 3)
            for j in range(SH):
                sp.wait_ge(expert_lo, E + j - 1)
                dst = we_raw[:, j % 2]
                for kd in range(KD):
                    sp.dma_start(dst[:, kd * I:(kd + 1) * I], shared_up[kd * P:(kd + 1) * P, j * I:(j + 1) * I]
                                 ).then_inc(shared_loaded[j % 2], 16)
                sp.dma_start(dst[:, UPW:], shared_down[j * I:(j + 1) * I, :]).then_inc(shared_loaded[j % 2], 16)

            def store_last_rows():
                round_((m + 1, 0), True, False, False, False)

            def scratch_stored():
                for r in range(4):
                    sp.wait_ge(normed_stored[r], 16 * (B // 4))
                for par in range(2):
                    sp.wait_ge(attn_stored[par], 16 * (B // 2))

            def load_rows(view, j, par):
                sp.dma_start(f_rows[:, par, 0], tile_of(view, j)).then_inc(rows_loaded[par], 16)

            def load_rest(j, par):
                sp.dma_start(f_acc[:, par, 0], tile_of(partial_t, j)).then_inc(acc_loaded[par], 16)
                sp.dma_start(f_x[:, par, 0], tile_of(x_tiles, j)).then_inc(acc_loaded[par], 16)

            def store_out(j, par):
                wait(sp, f_ready, j + 1)
                sp.dma_start(tile_of(out_rows, j), f_out[:, par, 0]).then_inc(out_stored[par], 16)

            def sparse_path():
                for r in range(2):
                    sp.wait_ge(scattered[r], SCATTERS * (B // 4))

                def load_unit(s, d):
                    u, r = s.u + d, (s.r + d) % 4
                    if s.kind(d) == "routed":
                        first_row = sp.value_load(unit_row[0:1, bass.ds(u, 1)], min_val=0, max_val=SLOTS - UR)
                        stage = sp.value_load(rows_stage[0:1, bass.ds(u, 1)], min_val=1, max_val=2)
                        sp.wait_ge(scattered[2], SCATTERS * (stage + B // 4 - 2))
                        bare(sp)
                        sp.wait_ge(scattered[3], SCATTERS * (stage + B // 4 - 2))
                        bare(sp)
                        sp.wait_ge(zeros_stored, ZEROS * stage)
                        bare(sp)
                        wait(sp, weighted, 2 * (u - 3))
                        bare(sp)
                        sp.dma_start(f_rows[:, r],
                                     by_group[bass.ds(first_row, UR), :].rearrange("(s p) r -> p s r", p=P)
                                     ).then_inc(rows_loaded[r], 16)
                    elif s.kind(d) == "shared":
                        if s.near + d == ROUTED:
                            scratch_stored()
                        if s.kind(d - 4) == "routed":
                            wait(sp, weighted, 2 * (u - 3))
                        else:
                            wait(sp, fx_done, u - 3)
                        bare(sp)
                        sp.dma_start(f_rows[:, r], batch_of(normed_u, u - ROUTED)).then_inc(rows_loaded[r], 16)

                def step(s):
                    if s.near == 0:
                        for d in range(3):
                            load_unit(s, d)
                    load_unit(s, 3)
                    if s.near == 0:
                        store_last_rows()
                    if s.kind(-3) == "routed":
                        par = 1 - s.par
                        sp.wait_ge(y_ready, s.u - 2)
                        bare(sp)
                        sp.dma_start(batch_of(routed_u, s.u - 3), f_y[:, par]).then_inc(y_stored[par], 16)
                    if s.kind(-3) == "shared":
                        sp.wait_ge(f_ready, s.u - ROUTED - 2)
                        bare(sp)
                        sp.dma_start(batch_of(out_u, s.u - ROUTED - 3), f_out[:, 1 - s.par]
                                     ).then_inc(out_stored[1 - s.par], 16)
                    if s.kind(-1) == "shared":
                        v, par = s.u - ROUTED - 1, 1 - s.par
                        if s.near == ROUTED + 1:
                            for r in range(2, 4):
                                sp.wait_ge(scattered[r], SCATTERS * (B // 4))
                        wait(sp, f_ready, v - 1)
                        bare(sp)
                        sp.dma_start(f_acc[:, par], batch_of(partial_u, v)).then_inc(acc_loaded[par], 16)
                        sp.dma_start(f_x[:, par], batch_of(x_u, v)).then_inc(acc_loaded[par], 16)

                sparse_steps(sp, step)
                for par in range(2):
                    sp.wait_ge(out_stored[par], 16 * (SHARED // 2))

            def dense_path():
                store_last_rows()
                scratch_stored()
                for r in range(4):
                    sp.wait_ge(scattered[r], SCATTERS * (B // 4))
                for par in range(2):
                    load_rows(normed_t, par, par)
                    load_rest(par, par)
                with sp.Fori(0, NT // 2 - 1) as k:
                    for par in range(2):
                        wait(sp, weighted, N_GROUP * (2 * k + par + 1))
                        load_rows(normed_t, 2 * k + par + 2, par)
                        store_out(2 * k + par, par)
                        load_rest(2 * k + par + 2, par)
                for par in range(2):
                    store_out(NT - 2 + par, par)

                for par in range(2):
                    sp.wait_ge(out_stored[par], 16 * (NT // 2))

            either(sp, sparse_path, dense_path)
            for r in range(4):
                sp.wait_ge(scattered[r], SCATTERS * (B // 4))
            sp.wait_ge(zeros_stored, 2 * ZEROS)

        @block.gpsimd
        def _(pool):
            G = nc.gpsimd
            for t in (ident, earlier_f, ones_wide_f):
                G.memset(t[:, :], 1.0).then_inc(const_step, 1)
            G.memset(lower[:, :, :], 1.0).then_inc(const_step, 1)
            pool.wait_ge(const_step, 4)
            G.affine_select(out=ident[:, :], in_=ident[:, :], compare_op=ALU.is_equal, fill=0.0, base=0,
                            pattern=[[-1, P]], channel_multiplier=1).then_inc(consts_made, 1)
            G.affine_select(out=earlier_f[:, :], in_=earlier_f[:, :], compare_op=ALU.is_gt, fill=0.0, base=0,
                            pattern=[[1, P]], channel_multiplier=-1).then_inc(consts_made, 1)
            G.affine_select(out=lower[:, :, :], in_=lower[:, :, :], compare_op=ALU.is_gt, fill=0.0, base=0,
                            pattern=[[1, N_GROUP], [-1, N_GROUP]], channel_multiplier=0).then_inc(consts_made, 1)
            for t, step, chan in ((region_i, REGION, 0), (unit_rows_i, UR, 0),
                                  (unit_i, 1, 0)):
                G.iota(t[:, :], pattern=[[step, t.shape[1]]], base=0, channel_multiplier=chan
                       ).then_inc(consts_made, 1)
            G.memset(minus_half[:, :], -0.5).then_inc(consts_made, 1)
            G.memset(zero_rows[:, :], 0.0).then_inc(consts_made, 1)

            def moments(at):
                c = idx(at)
                pool.wait_ge(moments_ready, c + 1)
                bare(pool)
                G.tensor_scalar(var_eps[:, :], mean_var[:, at[1] % 2, :, 1], LN_EPS, None, ALU.add
                                ).then_inc(var_ready, 1)
                G.tensor_scalar(mean_neg[:, :], mean_var[:, at[1] % 2, :, 0], -1.0, None, ALU.mult
                                ).then_inc(var_ready, 1)
                wait(pool, xn_ready, c - 1)
                pool.wait_ge(var_ready, 2 * (c + 1))
                G.tensor_tensor(rstd[:, at[1] % 2], var_eps[:, :], minus_half[:, :], ALU.pow
                                ).then_inc(var_done, 1)
                pool.wait_ge(var_done, c + 1)
                G.tensor_tensor(shift_neg[:, at[1] % 2], mean_neg[:, :], rstd[:, at[1] % 2], ALU.mult
                                ).then_inc(rstd_ready, 1)

            def scatter(at, subs):
                pool.wait_ge(route_ready, half(at) + 1)
                bare(pool)
                for s in subs:
                    for first_or_second in range(2):
                        t = (at[1] % 2) * SUB + s
                        G.indirect_dma_start(
                            out=by_group[:, :], in_=xn[:, at[1], s, :], in_offset=None,
                            out_offset=bass.IndirectOffsetOnAxis(ap=slots_now[:, first_or_second, t:t + 1], axis=0)
                        ).then_inc(scattered[at[1]], 16)

            def body(at, before, now, after):
                c = idx(at)
                if after:
                    moments(later(at, 1))
                if now:
                    pool.wait_ge(xr_hi, c + 1)
                    G.tensor_tensor(xr_l[:, :, :], xn[:, at[1], :, 0:D], xr_h[:, :, :].bitcast(F32),
                                    ALU.subtract).then_inc(xr_ready, 1)
                two_back = not (isinstance(at[0], int) and c < 2)
                if two_back:
                    scatter(later(at, -2), (0, 1))
                if now:
                    pool.wait_ge(q_hi, c + 1)
                    G.tensor_tensor(q_l[:, :, :], q_f[:, :, :], q_h[:, :, :].bitcast(F32), ALU.subtract
                                    ).then_inc(q_lo, 1)
                if two_back:
                    scatter(later(at, -2), (2, 3))

            attention_rounds(pool, body)
            scatter((B // 4 - 1, 3), range(SUB))
            def sparse_path():
                pool.wait_ge(rows_known, 1)
                for par in range(2):
                    pool.wait_ge(attn_stored[par], 16 * (B // 2))
                    pool.wait_ge(y_stored[par], 16 * (ROUTED // 2))

                def gather(v, par):
                    wait(pool, sum_ready, v - 1)
                    bare(pool)
                    G.tensor_copy(rows_now[:, par, :].rearrange("p (f s) -> p f s", f=2),
                                  rows_all[:, :, bass.ds(2 * v, 2)]).then_inc(slots_copied, 1)
                    pool.wait_ge(slots_copied, v + 1)
                    bare(pool)
                    for f in range(2):
                        for s in range(2):
                            at = 2 * f + s
                            G.indirect_dma_start(
                                out=f_got[:, par, f, s, :], out_offset=None, in_=routed[:, :],
                                in_offset=bass.IndirectOffsetOnAxis(ap=rows_now[:, par, at:at + 1], axis=0)
                            ).then_inc(got_loaded[par], 16)

                for par in range(2):
                    gather(par, par)
                with pool.Fori(1, SHARED // 2) as k:
                    for par in range(2):
                        gather(2 * k + par, par)

            either(pool, sparse_path, lambda: None)

        @block.scalar
        def _(act):
            A = nc.scalar
            def normalise(at):
                c, par = idx(at), at[1] % 2
                act.wait_ge(rstd_ready, c + 1)
                wait(act, normed_stored[at[1]], 16 * at[0])
                wait(act, scattered[at[1]], SCATTERS * at[0])
                wait(act, xr_ready, c - 3)
                for s in range(SUB):
                    last = A.activation(xn[:, at[1], s, 0:D], x_in[:, par, s], ACT.Identity,
                                        bias=shift_neg[:, par, s:s + 1], scale=rstd[:, par, s:s + 1])
                last.then_inc(xn_ready, 1)

            normalise((0, 0))
            for i, (dst, w) in enumerate(((wkg_h[:, :, 0:D], 0), (wqT_h[:, :, :], 1))):
                act.wait_ge(turned, w + 1)
                A.copy(dst, bank[w][:, :].rearrange("p (c d) -> p c d", c=KD)).then_inc(turned_hi, 1)
            act.wait_ge(turned, 3)
            A.copy(wkg_h[:, :, D:ROW], bank[3][:, 0:KD * E].rearrange("p (c e) -> p c e", c=KD)
                   ).then_inc(turned_hi, 1)

            def expert_high(slot, par, loaded, value):
                act.wait_ge(loaded, value)
                A.copy(we_h[:, bass.ds(slot, 1), :].rearrange("p o w -> p (o w)"), we_raw[:, par]
                       ).then_inc(expert_hi, 1)

            def body(at, before, now, after):
                c, par = idx(at), at[1] % 2
                if now:
                    act.wait_ge(xn_ready, c + 1)
                    wait(act, m_done, c)
                    wait(act, xr_ready, c)
                    A.copy(xr_h[:, :, :], xn[:, at[1], :, 0:D]).then_inc(xr_hi, 1)
                    if par == 0:
                        wait(act, front_step, FRONT_STEPS * (half(at) - 1) + 1)
                    wait(act, k_lo, c)
                    for s in range(SUB):
                        act.wait_ge(k_done, SUB * c + s + 1)
                        A.activation(k_f[:, s, :], bank[s][:, 0:D], ACT.Exp, bias=minus_one[:, 0:1])
                        A.activation(r_exp[:, par * SUB + s, :], bank[s][:, D:ROW], ACT.Exp, scale=-1.0
                                     ).then_inc(k_exp, 1)
                    expert_high(c, par, expert_loaded[par], 48 * (half(at) + 1))
                if before and not now:
                    for j in range(2):
                        expert_high(E + j, j, shared_loaded[j], 48)
                if before:
                    act.wait_ge(p_done, c)
                    wait(act, c_done, SUB * (c - 1))
                    for h in range(KD):
                        A.copy(p_h[:, h, :], bank[7 - h][:, 0:PW]).then_inc(p_hi, 1)

                def q_exponential(h):
                    act.wait_ge(q_done, KD * c + h + 1)
                    wait(act, q_lo, c)
                    A.activation(q_f[:, h, :], bank[2 + h][:, :], ACT.Exp, bias=minus_one[:, 0:1]
                                 ).then_inc(q_exp, 1)

                if now:
                    q_exponential(0)
                    act.wait_ge(k_ready, SUB * (c + 1))
                    wait(act, m_done, c)
                    A.copy(k_h[:, :, :], k_f[:, :, :]).then_inc(k_hi, 1)
                    q_exponential(1)
                    if not before:
                        act.wait_ge(turned, 4)
                        A.copy(woT[:, :, :], bank[0][:, :].rearrange("p (c d) -> p c d", c=KD)).then_inc(wo_copied, 1)
                if after:
                    if now:
                        normalise(later(at, 1))
                if after:
                    act.wait_ge(xt_done, c + 2)
                    wait(act, q_done, KD * (c + 1))
                    for h in range(KD):
                        A.copy(xt_h[:, h, :], bank[4 + h][:, :]).then_inc(xt_hi, 1)
                if before:
                    b = later(at, -1)
                    wait(act, attn_stored[b[1] % 2], 16 * half(b))
                    for s in range(SUB):
                        act.wait_ge(rz_ready, SUB * (c - 1) + s + 1)
                        A.activation(attn_out[:, b[1] % 2, s], bank[s][:, 0:D], ACT.Copy, scale=rz[:, s:s + 1]
                                     ).then_inc(attn_ready, 1)
                if now:
                    act.wait_ge(q_ready, KD * (c + 1))
                    wait(act, c_done, SUB * c)
                    A.copy(q_h[:, :, :], q_f[:, :, :]).then_inc(q_hi, 1)
                    if not before:
                        act.wait_ge(folded, 1)
                        A.copy(wvo_h[:, :, :], bank[1][:, :].rearrange("p (c d) -> p c d", c=KD)
                               ).then_inc(folded_hi, 1)
                    act.wait_ge(ksum_done, c + 1)
                    A.copy(ksum_rows[0:64, :], bank[7][0:64, D:2 * D]).then_inc(ksum_hi, 1)
                    act.wait_ge(m_done, c + 1)
                    wait(act, p_done, c)
                    A.copy(m_h[:, :, :], bank[6][:, :].rearrange("p (c d) -> p c d", c=KD)).then_inc(m_hi, 1)
            attention_rounds(act, body)
            for j in range(2, SH):
                expert_high(E + j, j % 2, shared_loaded[j % 2], 48 * (j // 2 + 1))
            act.wait_ge(pad_ready, 1)
            for g in range(N_GROUP):
                store_zeros(act, act.value_load(pad_at[0:1, g:g + 1], min_val=0, max_val=SLOTS - UR))

            def silu(n, tile, par, bk):
                act.wait_ge(up_done, n + 1)
                A.activation(hid[par][:, tile], bank[bk][:, :].rearrange("p (e i) -> p e i", e=GE), ACT.Silu
                             ).then_inc(silu_ready, 1)

            def hidden_hi(n, tile, par):
                act.wait_ge(ht_done, n + 1)
                A.copy(ht_h[par][:, tile], bank[2 + tile][:, :].rearrange("p (e t) -> p e t", e=GE)
                       ).then_inc(ht_hi, 1)

            def sparse_path():
                def turn_rows(u, par):
                    act.wait_ge(fx_done, u + 1)
                    A.copy(fx_h[:, par], bank[4 + par][:, :].rearrange("p (c s t) -> p c s t", c=KD, s=2)
                           ).then_inc(fx_hi, 1)

                def step(s):
                    if s.near == 0:
                        turn_rows(0, 0)
                    if s.kind(0):
                        for tile in range(2):
                            if s.kind(-2) == "shared":
                                act.wait_ge(ht_ready, 2 * s.u - 3 + tile)
                            else:
                                wait(act, ht_done, 2 * s.u - 3 + tile)
                            silu(2 * s.u + tile, tile, s.par, tile)
                    if s.kind(1):
                        wait(act, up_done, 2 * s.u)
                        turn_rows(s.u + 1, 1 - s.par)
                    if s.kind(-1):
                        wait(act, down_done, s.u - 2)
                        for tile in range(2):
                            if s.kind(-1) == "routed":
                                hidden_hi(2 * s.u - 2 + tile, tile, 1 - s.par)
                            else:
                                act.wait_ge(silu_ready, 2 * s.u - 1 + tile)
                                A.copy(ht_h[1 - s.par][:, tile], hid[1 - s.par][:, tile]).then_inc(ht_hi, 1)
                    if s.kind(-2) == "routed":
                        act.wait_ge(down_done, s.u - 1)
                        wait(act, y_stored[s.par], 16 * s.twos(-2))
                        for tile in range(2):
                            last = A.copy(f_y[:, s.par, tile], bank[6 + tile][:, 0:D])
                        last.then_inc(y_ready, 1)

                sparse_steps(act, step)

            def dense_path():
                def turn_rows(n, par):
                    act.wait_ge(fx_done, n + 1)
                    A.copy(fx_h[:, par, :, 0], bank[4 + par][:, 0:D].rearrange("p (c t) -> p c t", c=KD)
                           ).then_inc(fx_hi, 1)

                turn_rows(0, 0)

                def unit(k, r, first, last):
                    u = 2 * NG * k + r
                    wait(act, ht_done, u - 1)
                    silu(u, r % 2, 0, r % 2)
                    if r % NG == 2 and not (last and r // NG == 1):
                        j = 2 * k + r // NG
                        wait(act, up_done, NG * j)
                        turn_rows(j + 1, 1 - r // NG)
                    if not (first and r == 0):
                        wait(act, down_done, u - 2)
                        hidden_hi(u - 1, (r + 1) % 2, 0)

                dense_rounds(act, unit)
                act.wait_ge(down_done, NG * NT - 2)
                hidden_hi(NG * NT - 1, 1, 0)

            either(act, sparse_path, dense_path)

        @block.vector
        def _(dve):
            V = nc.vector
            def steps_of(semaphore, base, start=0):
                n = [start]

                def step(ins):
                    n[0] += 1
                    ins.then_inc(semaphore, 1)

                def after():
                    dve.wait_ge(semaphore, base + n[0])

                return step, after, n

            step, after, _ = steps_of(bias_step, 0)
            step(V.memset(minus_one[:, :], -1.0))
            step(V.memset(bk_row[:, D:ROW], 0.0))
            for t, one in ((bias_all, 1.0), (eb_all, Z_EPS)):
                step(V.memset(t[:, D:D + 1], one))
                step(V.memset(t[:, D + 1:PW], 0.0))
            step(V.memset(ksum_rows[:, :].bitcast(F32), 1.0))
            for t in run:
                step(V.memset(t[:, :, :], 0.0))
            step(V.memset(run_all[:, :, :].bitcast(F32), 0.0))
            step(V.memset(fourth[:, :], 1.0))
            def row_statistics(at, s):
                c, par = idx(at), at[1] % 2
                dve.wait_ge(x_loaded[par], 16 * (half(at) + 1))
                V.bn_stats(stats[:, s], x_in[:, par, s]).then_inc(stats_done, 1)

            def statistics(at):
                c, par = idx(at), at[1] % 2
                dve.wait_ge(stats_done, SUB * (c + 1))
                wait(dve, rstd_ready, c - 1)
                bare(dve)
                for s in range(SUB):
                    last = V.bn_aggr(mean_var[:, par, s], stats[:, s])
                last.then_inc(moments_ready, 1)

            for s in range(SUB):
                row_statistics((0, 0), s)
            statistics((0, 0))
            dve.wait_ge(consts_made, CONSTS)
            V.tensor_copy(earlier[:, :], earlier_f[:, :])
            V.tensor_copy(ones_wide[:, :], ones_wide_f[:, :])
            V.tensor_copy(region[:, :], region_i[:, :])
            V.tensor_copy(unit_rows[:, :], unit_rows_i[:, :])
            V.tensor_copy(unit_no[:, :], unit_i[:, :]).then_inc(consts_cast, 1)
            dve.wait_ge(bias_loaded, 16 * 5)
            for c in range(KD):
                V.tensor_copy(bv_wide[:, c, :], bv_col[:, c:c + 1].to_broadcast([P, P])).then_inc(bv_ready, 1)
            after()
            step(V.tensor_scalar(bk_row[:, 0:D], bk_row[:, 0:D], 1.0, None, ALU.add))
            step(V.tensor_scalar(bq_row[:, :], bq_row[:, :], 1.0, None, ALU.add))
            step(V.tensor_scalar(eb_all[:, 0:D], bo_all[:, :], Z_EPS, None, ALU.mult))
            after()
            for hi, row in ((kb_h, bk_row), (qb_h, bq_row), (eb_h, eb_all)):
                step(V.tensor_copy(hi[:, :], row[:, :]))
            after()
            for lo, hi, row in ((kb_l, kb_h, bk_row), (qb_l, qb_h, bq_row), (eb_l, eb_h, eb_all)):
                step(V.tensor_tensor(lo[:, :], row[:, :], hi[:, :].bitcast(F32), ALU.subtract))
            dve.wait_ge(consts_made, 1)
            for dst, hi, at_ in ((kb, kb_h, 0), (qb, qb_h, 0), (bias_rows, eb_h, 64)):
                n = dst.shape[0]
                step(V.tensor_scalar(dst[:, :], hi[:, :].bitcast(F32), ident[0:n, at_:at_ + 1], None, ALU.mult))
            after()

            def add_row(dst, src, at_):
                return V.scalar_tensor_tensor(out=dst[:, :], in0=src[:, :].bitcast(F32),
                                              scalar=ident[0:dst.shape[0], at_:at_ + 1],
                                              in1=dst[:, :].bitcast(F32), op0=ALU.mult, op1=ALU.add)

            add_row(kb, kb_l, 1).then_inc(row_biases, 1)
            add_row(qb, qb_l, 1).then_inc(row_biases, 1)
            step(add_row(bias_rows, eb_l, 65))
            for i, (dst, hi, src) in enumerate((
                    (wkg_l[:, :, 0:D], wkg_h[:, :, 0:D], bank[0][:, :].rearrange("p (c d) -> p c d", c=KD)),
                    (wqT_l[:, :, :], wqT_h[:, :, :], bank[1][:, :].rearrange("p (c d) -> p c d", c=KD)),
                    (wkg_l[:, :, D:ROW], wkg_h[:, :, D:ROW],
                     bank[3][:, 0:KD * E].rearrange("p (c e) -> p c e", c=KD)))):
                dve.wait_ge(turned_hi, i + 1)
                V.tensor_tensor(dst, src, hi.bitcast(F32), ALU.subtract).then_inc(turned_lo, 1)
            def finish_weights():
                dve.wait_ge(folded_hi, 1)
                V.tensor_tensor(wvo_l[:, :, :], bank[1][:, :].rearrange("p (c d) -> p c d", c=KD),
                                wvo_h[:, :, :].bitcast(F32), ALU.subtract).then_inc(folded_lo, 1)
                dve.wait_ge(folded, 2)
                step(V.tensor_tensor(bias_all[:, 0:D], bank[0][0:96, 0:D], bo_all[:, :], ALU.add))
                after()
                step(V.tensor_copy(bias_h[:, :], bias_all[:, :]))
                after()
                step(V.tensor_tensor(bias_l[:, :], bias_all[:, :], bias_h[:, :].bitcast(F32), ALU.subtract))
                step(add_row(bias_rows, bias_h, 0))
                after()
                step(add_row(bias_rows, bias_h, 32))
                after()
                add_row(bias_rows, bias_l, 1).then_inc(bias_rows_ready, 1)

            def expert_rest(slot, par, value):
                dve.wait_ge(expert_hi, value)
                hi = we_h[:, bass.ds(slot, 1), :].rearrange("p o w -> p (o w)")
                lo = we_l[:, bass.ds(slot, 1), :].rearrange("p o w -> p (o w)")
                V.tensor_tensor(lo, we_raw[:, par], hi.bitcast(F32), ALU.subtract).then_inc(expert_lo, 1)

            ROUTE_STEPS = (2, 4, 4, 2, 2, 2, 2)
            assert sum(ROUTE_STEPS) == FRONT_STEPS

            def route_part(pair, part):
                start = sum(ROUTE_STEPS[:part])
                step, after, n = steps_of(front_step, FRONT_STEPS * pair, start)
                if part > 0:
                    after()
                return step, after, n

            def route_scores(pair):
                step, after, n = route_part(pair, 0)
                dve.wait_ge(k_exp, SUB * (2 * pair + 2))
                step(V.tensor_scalar(r_den[:, :, :], r_exp[:, :, :], 1.0, None, ALU.add))
                after()
                step(V.reciprocal(score[:, :, :], r_den[:, :, :]))
                assert n[0] == sum(ROUTE_STEPS[:1]), n[0]

            def route_group_scores(pair):
                step, after, n = route_part(pair, 1)
                g4 = score[:, :, :].rearrange("p s (g e) -> p (s g) e", g=N_GROUP)
                V.tensor_tensor(g_hi[:, :, :], g4[:, :, 0:2], g4[:, :, 2:4], ALU.max)
                step(V.tensor_tensor(g_lo[:, :, :], g4[:, :, 0:2], g4[:, :, 2:4], ALU.min))
                after()
                V.tensor_tensor(g_top[:, :], g_hi[:, :, 0], g_hi[:, :, 1], ALU.max)
                V.tensor_tensor(g_mid[:, :], g_hi[:, :, 0], g_hi[:, :, 1], ALU.min)
                step(V.tensor_tensor(g_low[:, :], g_lo[:, :, 0], g_lo[:, :, 1], ALU.max))
                after()
                step(V.tensor_tensor(g_second[:, :], g_mid[:, :], g_low[:, :], ALU.max))
                after()
                step(V.tensor_tensor(g_score[:, :, :].rearrange("p s g -> p (s g)"), g_top[:, :], g_second[:, :],
                                     ALU.add))
                assert n[0] == sum(ROUTE_STEPS[:2]), n[0]

            def route_group_ranks(pair):
                step, after, n = route_part(pair, 2)
                wide = [P, PAIR, N_GROUP, N_GROUP]
                mine = g_score[:, :, :].unsqueeze(3).to_broadcast(wide)
                other = g_score[:, :, :].unsqueeze(2).to_broadcast(wide)
                V.tensor_tensor(g_gt[:, :, :, :], other, mine, ALU.is_gt)
                step(V.tensor_tensor(g_ge[:, :, :, :], other, mine, ALU.is_ge))
                after()
                step(V.tensor_tensor(g_tie[:, :, :, :], g_ge[:, :, :, :],
                                     lower[:, :, :].unsqueeze(1).to_broadcast(wide), ALU.mult))
                after()
                step(V.tensor_tensor(g_beats[:, :, :, :], g_gt[:, :, :, :], g_tie[:, :, :, :], ALU.max))
                after()
                step(V.tensor_reduce(g_rank[:, :, :], g_beats[:, :, :, :], AX_X, ALU.add))
                assert n[0] == sum(ROUTE_STEPS[:3]), n[0]

            def route_groups(pair):
                step, after, n = route_part(pair, 3)
                g4 = score[:, :, :].rearrange("p s (g e) -> p (s g) e", g=N_GROUP)
                wait(dve, rank_done, pair)
                V.tensor_scalar(g_in[:, :, :], g_rank[:, :, :], 2.0, None, ALU.is_lt)
                V.tensor_scalar(run[0][:, 5:, :], g_rank[:, 1:, :], 2.0, None, ALU.is_lt)
                V.scalar_tensor_tensor(out=run[0][:, 4, :], in0=g_rank[:, 0, :], scalar=2.0,
                                       in1=run_all[:, PAIR, :].bitcast(F32), op0=ALU.is_lt, op1=ALU.add)
                V.tensor_copy(run_all[:, 0, :], run_all[:, PAIR, :].bitcast(F32))
                step(V.tensor_scalar(g_in_r[:, :, :], g_rank[:, :, :], 2.0, None, ALU.is_lt))
                after()
                V.tensor_tensor(run[1][:, 4:, :], run[0][:, 4:, :], run[0][:, 3:3 + PAIR, :], ALU.add)
                step(V.tensor_tensor(masked[:, :, :].rearrange("p s (g e) -> p (s g) e", g=N_GROUP), g4,
                                     g_in[:, :, :].rearrange("p s g -> p (s g)").unsqueeze(2).to_broadcast(
                                         [P, PAIR * N_GROUP, GE]), ALU.mult))
                assert n[0] == sum(ROUTE_STEPS[:4]), n[0]

            def route_top(pair):
                step, after, n = route_part(pair, 4)
                step(V.tensor_tensor(run[2][:, 4:, :], run[1][:, 4:, :], run[1][:, 2:2 + PAIR, :], ALU.add))
                after()
                bare(dve)
                for s in range(PAIR):
                    last = V.max(top8[:, s], masked[:, s])
                step(last)
                V.tensor_tensor(run_all[:, 1:, :], run[2][:, 4:, :], run[2][:, 0:PAIR, :], ALU.add
                                ).then_inc(front_ready, 1)
                assert n[0] == sum(ROUTE_STEPS[:5]), n[0]

            def route_experts(pair):
                step, after, n = route_part(pair, 5)
                V.tensor_tensor(fourth[:, :], fourth[:, :], top8[:, :, 3], ALU.min)
                step(V.memset(top8[:, :, 4:8], 9.0))
                after()
                bare(dve)
                for s in range(PAIR):
                    last = V.match_replace(out=marked[:, s], in_to_replace=top8[:, s], in_values=masked[:, s],
                                           imm_value=-1.0)
                step(last)
                assert n[0] == sum(ROUTE_STEPS[:6]), n[0]

            def route_weights(pair):
                step, after, n = route_part(pair, 6)
                step(V.scalar_tensor_tensor(out=w_raw4[:, :, :], in0=marked[:, :, :], scalar=0.0,
                                            in1=score[:, :, :], op0=ALU.is_lt, op1=ALU.mult))
                after()
                step(V.tensor_reduce(w_sum[:, :], w_raw4[:, :, :], AX_X, ALU.add))
                assert n[0] == sum(ROUTE_STEPS[:7]), n[0]

            def read_slots(pair):
                dve.wait_ge(rank_done, pair + 1)
                V.tensor_tensor(slot[:, :, :], bank[7][:, 0:GP].rearrange("p (s g) -> p s g", g=N_GROUP),
                                region[:, :].unsqueeze(1).to_broadcast([P, PAIR, N_GROUP]), ALU.add
                                ).then_inc(rank_read, 1)

            def route_back(at, pair):
                step, after, n = steps_of(back_step, BACK_STEPS * pair)
                dve.wait_ge(rank_read, pair + 1)
                dve.wait_ge(front_step, FRONT_STEPS * (pair + 1))
                V.tensor_scalar(w_sum_eps[:, :], w_sum[:, :], SUM_EPS, None, ALU.add)
                V.tensor_tensor(slot_in[:, :, :], slot[:, :, :], g_in[:, :, :], ALU.mult)
                step(V.scalar_tensor_tensor(out=slot_out[:, :, :], in0=g_in[:, :, :], scalar=-FAR, in1=slot[:, :, :],
                                            op0=ALU.mult, op1=ALU.add))
                after()
                V.reciprocal(w_rsum[:, :], w_sum_eps[:, :])
                V.tensor_reduce(slot_last[:, :], slot_in[:, :, :], AX_X, ALU.max)
                step(V.tensor_reduce(slot_first[:, :], slot_out[:, :, :], AX_X, ALU.min))
                after()
                for r in range(2):
                    b = later(at, r - 2)
                    wait(dve, scattered[b[1]], SCATTERS * (b[0] + 1))
                V.scalar_tensor_tensor(
                    out=xn[:, at[1]:at[1] + 2, :, D:ROW].rearrange("p b s e -> p (b s) e"), in0=w_raw4[:, :, :],
                    scalar=ROUTED_SCALING, in1=w_rsum[:, :].unsqueeze(2).to_broadcast([P, PAIR, E]),
                    op0=ALU.mult, op1=ALU.mult)
                V.tensor_scalar(slots_now[:, 0, :], slot_first[:, :], FAR, None, ALU.add)
                V.tensor_copy(slots_now[:, 1, :], slot_last[:, :]).then_inc(route_ready, 1)
                dve.wait_ge(route_ready, pair + 1)
                V.tensor_copy(slots_all[:, :, bass.ds(PAIR * pair, PAIR)], slots_now[:, :, :])
                assert n[0] == BACK_STEPS, n[0]

            def normalisers(c):
                for s in range(SUB):
                    dve.wait_ge(c_done, SUB * (c - 1) + s + 1)
                    wait(dve, attn_ready, SUB * (c - 2) + s + 1)
                    V.reciprocal(rz[:, s:s + 1], bank[s][:, D:D + 1]).then_inc(rz_ready, 1)

            def body(at, before, now, after):
                c = idx(at)
                even = at[1] % 2 == 0
                pair = half(at)
                for s in range(SUB):
                    if now and after:
                        row_statistics(later(at, 1), s)
                    if now:
                        dve.wait_ge(k_exp, SUB * c + s + 1)
                        V.scalar_tensor_tensor(out=k_f[:, s, :], in0=k_f[:, s, :], scalar=1.0,
                                               in1=bank[s][:, 0:D], op0=ALU.min, op1=ALU.max).then_inc(k_ready, 1)
                if now and after:
                    statistics(later(at, 1))
                if before and even:
                    route_top(pair - 1)
                if before and not now:
                    route_experts(pair - 1)
                    route_weights(pair - 1)
                if before:
                    for h in range(KD):
                        dve.wait_ge(p_hi, KD * (c - 1) + h + 1)
                        V.tensor_tensor(p_l[:, h, :], bank[7 - h][:, 0:PW], p_h[:, h, :].bitcast(F32), ALU.subtract
                                        ).then_inc(p_lo, 1)
                if before and not now:
                    expert_rest(E, 0, E + 1)
                if before and now and even:
                    route_experts(pair - 1)

                def q_elu(h):
                    dve.wait_ge(q_exp, KD * c + h + 1)
                    V.scalar_tensor_tensor(out=q_f[:, h], in0=q_f[:, h], scalar=1.0, in1=bank[2 + h][:, :],
                                           op0=ALU.min, op1=ALU.max).then_inc(q_ready, 1)

                if now:
                    if not even:
                        route_scores(pair)
                    q_elu(0)
                    if not even:
                        route_group_scores(pair)
                if before and even:
                    read_slots(pair - 1)
                    if now:
                        route_weights(pair - 1)
                if now:
                    q_elu(1)
                    dve.wait_ge(k_hi, c + 1)
                    V.tensor_tensor(k_l[:, :, :], k_f[:, :, :], k_h[:, :, :].bitcast(F32), ALU.subtract
                                    ).then_inc(k_lo, 1)
                if before and even:
                    route_back(later(at, -2), pair - 1)
                if before and not now:
                    expert_rest(E + 1, 1, E + 2)
                if before:
                    normalisers(c)
                if now:
                    if not even:
                        route_group_ranks(pair)
                    else:
                        expert_rest(c, at[1] % 2, c + 1)
                if after:
                    for h in range(KD):
                        dve.wait_ge(xt_hi, KD * (c + 1) + h + 1)
                        V.tensor_tensor(xt_l[:, h], bank[4 + h][:, :], xt_h[:, h].bitcast(F32), ALU.subtract
                                        ).then_inc(xt_ready, 1)
                if now:
                    if not even:
                        route_groups(pair)
                        expert_rest(c, at[1] % 2, c + 1)
                    if not before:
                        finish_weights()
                    dve.wait_ge(ksum_hi, c + 1)
                    V.tensor_tensor(ksum_rows[32:64, :], bank[7][32:64, D:2 * D], ksum_rows[32:64, :].bitcast(F32),
                                    ALU.subtract).then_inc(ksum_ready, 1)
                    dve.wait_ge(m_hi, c + 1)
                    V.tensor_tensor(m_l[:, :, :], bank[6][:, :].rearrange("p (c d) -> p c d", c=KD),
                                    m_h[:, :, :].bitcast(F32), ALU.subtract).then_inc(m_lo, 1)
            attention_rounds(dve, body)

            step, after, _ = steps_of(plan_step, 0)
            dve.wait_ge(counted, 1)
            dve.wait_ge(q_lo, B)
            V.tensor_reduce(fourth_min[:, 0:1], fourth[:, :], AX_X, ALU.min)
            V.tensor_copy(counts[:, 0:N_GROUP], bank[4][:, 0:N_GROUP])
            step(V.tensor_scalar(counts[:, N_GROUP:], bank[4][:, N_GROUP:2 * N_GROUP], 1.0 - UR, None, ALU.add))
            after()
            wide = [P, 2 * N_GROUP, SHARED]
            step(V.tensor_tensor(over[:, :, :], counts[:, :].unsqueeze(2).to_broadcast(wide),
                                 unit_rows[:, :].unsqueeze(1).to_broadcast(wide), ALU.is_gt))
            after()
            step(V.tensor_reduce(n_units[:, :], over[:, :, :], AX_X, ALU.add))
            step(V.tensor_tensor(pad_f[:, :], counts[0:1, 0:N_GROUP], region[0:1, :], ALU.add))
            V.tensor_copy(bv_wide[:, 0, :], fourth_min[:, 0:1].to_broadcast([P, P])).then_inc(fourth_turned, 1)
            after()
            V.tensor_copy(pad_at[:, :], pad_f[:, :]).then_inc(pad_ready, 1)
            V.tensor_scalar(jump[:, :], n_units[:, 0:N_GROUP], -float(UR), float(REGION), ALU.mult, ALU.add)
            step(V.tensor_copy(unit_end[:, 0:1], n_units[0:1, 0:1]))
            V.tensor_copy(unit_end[:, N_GROUP:N_GROUP + 1], n_units[0:1, N_GROUP:N_GROUP + 1])
            for g in range(1, N_GROUP):
                after()
                step(V.tensor_tensor(unit_end[:, g:g + 1], unit_end[:, g - 1:g], n_units[0:1, g:g + 1], ALU.add))
            after()
            step(V.tensor_tensor(unit_end[:, N_GROUP + 1:], unit_end[:, 0:N_GROUP - 1], n_units[0:1, N_GROUP + 1:],
                                 ALU.add))
            after()
            wide = [1, 2 * N_GROUP, ROUTED]
            step(V.tensor_tensor(past[:, :, :], unit_no[:, :].unsqueeze(1).to_broadcast(wide),
                                 unit_end[:, :].unsqueeze(2).to_broadcast(wide), ALU.is_ge))
            after()

            def per_unit(t, first, end):
                return t[:, first:end, :].rearrange("p g t -> p t g")

            step(V.tensor_tensor(jumps[:, :, :], past[:, 0:N_GROUP, :],
                                 jump[0:1, :].unsqueeze(2).to_broadcast([1, N_GROUP, ROUTED]), ALU.mult))
            V.tensor_reduce(group_f[:, :], per_unit(past, 0, N_GROUP - 1), AX_X, ALU.add)
            V.tensor_reduce(ended[:, :], per_unit(past, 0, N_GROUP), AX_X, ALU.add)
            step(V.tensor_reduce(late_from[:, :], per_unit(past, N_GROUP, 2 * N_GROUP), AX_X, ALU.add))
            after()
            step(V.tensor_tensor(late[:, :], late_from[:, :], ended[:, :], ALU.subtract))
            step(V.tensor_reduce(jumped[:, :], per_unit(jumps, 0, N_GROUP), AX_X, ALU.add))
            after()
            V.scalar_tensor_tensor(out=unit_row[:, :], in0=unit_no[:, :], scalar=float(UR), in1=jumped[:, :],
                                   op0=ALU.mult, op1=ALU.add)
            V.tensor_scalar(unit_expert[:, :], group_f[:, :], float(GE), None, ALU.mult)
            V.tensor_scalar(rows_stage[:, :], late[:, :], 1.0, None, ALU.add)
            dve.wait_ge(fourth_turned, 2)
            step(V.tensor_reduce(fourth_all[:, :], bank[5][0:1, 0:P], AX_X, ALU.min))
            after()
            V.tensor_scalar(dense[:, :], fourth_all[:, :], 0.0, None, ALU.is_equal).then_inc(plan_ready, 1)

            step_, after_ = step, after

            for j in range(2, SH):
                expert_rest(E + j, j % 2, E + j + 1)

            def weigh(n, tile, par, weights):
                dve.wait_ge(silu_ready, n + 1)
                V.tensor_tensor(hidw[par][:, tile], hid[par][:, tile],
                                weights.unsqueeze(2).to_broadcast([P, GE, I]), ALU.mult).then_inc(weighted, 1)

            def hidden_lo(n, tile, par):
                dve.wait_ge(ht_hi, n + 1)
                V.tensor_tensor(ht_l[par][:, tile], bank[2 + tile][:, :].rearrange("p (e t) -> p e t", e=GE),
                                ht_h[par][:, tile].bitcast(F32), ALU.subtract).then_inc(ht_ready, 1)

            def sparse_path():
                def turn_rows(u, par):
                    dve.wait_ge(fx_hi, u + 1)
                    V.tensor_tensor(fx_l[:, par], bank[4 + par][:, :].rearrange("p (c s t) -> p c s t", c=KD, s=2),
                                    fx_h[:, par].bitcast(F32), ALU.subtract).then_inc(fx_ready, 1)

                def sums(s):
                    v, par, k = s.u - 2 - ROUTED, s.par, s.twos(-2) - ROUTED // 2
                    dve.wait_ge(acc_loaded[par], 32 * (k + 1))
                    V.tensor_tensor(f_acc[:, par], f_acc[:, par], f_x[:, par], ALU.add)
                    dve.wait_ge(got_loaded[par], 64 * (k + 1))
                    V.tensor_tensor(f_got[:, par, 0], f_got[:, par, 0], f_got[:, par, 1], ALU.add
                                    ).then_inc(sums_made, 1)
                    dve.wait_ge(sums_made, v + 1)
                    V.tensor_tensor(f_acc[:, par], f_acc[:, par], f_got[:, par, 0], ALU.add
                                    ).then_inc(sum_ready, 1)

                def finish(s):
                    v, par = s.u - 3 - ROUTED, 1 - s.par
                    dve.wait_ge(sum_ready, v + 1)
                    dve.wait_ge(down_done, s.u - 2)
                    wait(dve, out_stored[par], 16 * (s.twos(-3) - ROUTED // 2))
                    for tile in range(2):
                        last = V.tensor_tensor(f_out[:, par, tile], bank[6 + tile][:, 0:D], f_acc[:, par, tile],
                                               ALU.add)
                    last.then_inc(f_ready, 1)

                def step(s):
                    if s.near == 0:
                        turn_rows(0, 0)
                    if s.kind(-3) == "shared":
                        finish(s)
                    if s.kind(1):
                        turn_rows(s.u + 1, 1 - s.par)
                    if s.kind(0) == "routed":
                        first = dve.value_load(unit_expert[0:1, bass.ds(s.u, 1)], min_val=0, max_val=E - GE)
                        for tile in range(2):
                            weigh(2 * s.u + tile, tile, s.par, f_rows[:, s.r, tile, bass.ds(first + D, GE)])
                    if s.kind(-1):
                        for tile in range(2):
                            if s.kind(-1) == "routed":
                                hidden_lo(2 * s.u - 2 + tile, tile, 1 - s.par)
                            else:
                                par = 1 - s.par
                                dve.wait_ge(ht_hi, 2 * s.u - 1 + tile)
                                V.tensor_tensor(ht_l[par][:, tile], hid[par][:, tile],
                                                ht_h[par][:, tile].bitcast(F32), ALU.subtract).then_inc(ht_ready, 1)
                    if s.kind(-2) == "shared":
                        sums(s)

                for g in range(N_GROUP - 1):
                    step_(V.tensor_scalar(shift[:, g], slots_all[:, :, :], float((g + 1) * REGION),
                                          jump[:, g:g + 1], ALU.is_ge, ALU.mult))
                after_()
                for g in range(N_GROUP - 1):
                    step_(V.tensor_tensor(slots_all[:, :, :], slots_all[:, :, :], shift[:, g], ALU.subtract))
                    after_()
                V.tensor_copy(rows_all[:, :, :], slots_all[:, :, :]).then_inc(rows_known, 1)
                sparse_steps(dve, step)

            def dense_path():
                def turn_rows(n, par):
                    dve.wait_ge(fx_hi, n + 1)
                    V.tensor_tensor(fx_l[:, par, :, 0], bank[4 + par][:, 0:D].rearrange("p (c t) -> p c t", c=KD),
                                    fx_h[:, par, :, 0].bitcast(F32), ALU.subtract).then_inc(fx_ready, 1)

                def finish(k, par, j):
                    dve.wait_ge(acc_loaded[par], 32 * (k + 1))
                    V.tensor_tensor(f_acc[:, par, 0], f_acc[:, par, 0], f_x[:, par, 0], ALU.add
                                    ).then_inc(sums_made, 1)
                    dve.wait_ge(sums_made, j + 1)
                    dve.wait_ge(down_done, NG * (j + 1))
                    wait(dve, out_stored[par], 16 * k)
                    V.tensor_tensor(f_out[:, par, 0], bank[6 + par][:, 0:D], f_acc[:, par, 0], ALU.add
                                    ).then_inc(f_ready, 1)

                turn_rows(0, 0)

                def unit(k, r, first, last):
                    u = 2 * NG * k + r
                    g, par = r % NG, r // NG
                    if g < N_GROUP:
                        weigh(u, r % 2, 0, f_rows[:, par, 0, D + g * GE:D + (g + 1) * GE])
                    if g == 2 and not (last and par == 1):
                        turn_rows(2 * k + par + 1, 1 - par)
                    if not (first and r == 0):
                        hidden_lo(u - 1, (r + 1) % 2, 0)
                    if g == 3 and not (first and r == 3):
                        j = 2 * k + par - 1
                        finish(k - 1 + par, 1 - par, j)

                dense_rounds(dve, unit)
                hidden_lo(NG * NT - 1, 1, 0)
                finish(NT // 2 - 1, 1, NT - 1)

            either(dve, sparse_path, dense_path)

        @block.tensor
        def _(pe):
            T_ = nc.tensor
            pe.wait_ge(consts_made, 1)

            def turn_weight(w, b):
                pe.wait_ge(setup_loads[w], 16)
                for r in range(KD):
                    for c in range(KD):
                        last = T_.transpose(bank[b][:, c * D + r * P:c * D + (r + 1) * P],
                                            w_raw[:, w, r, c * P:(c + 1) * P], ident[:, :])
                last.then_inc(turned, 1)

            turn_weight(0, 0)
            turn_weight(1, 1)
            pe.wait_ge(bias_loaded, 16 * 5)
            for c in range(KD):
                last = T_.transpose(bank[3][:, c * E:(c + 1) * E], gate_raw[:, c * P:(c + 1) * P], ident[0:E, 0:E])
            last.then_inc(turned, 1)
            def fold_weights():
                pe.wait_ge(k_ready, 1)
                turn_weight(2, 0)
                pe.wait_ge(setup_loads[3], 16)
                pe.wait_ge(wo_copied, 1)
                pe.wait_ge(k_ready, 2)
                for h in range(KD):
                    for m in range(KD):
                        last = T_.matmul(bank[1][:, h * D:(h + 1) * D], w_raw[:, 3, m, h * P:(h + 1) * P],
                                         woT[:, m, :], start=(m == 0), stop=(m == KD - 1))
                last.then_inc(folded, 1)
                pe.wait_ge(bv_ready, KD)
                for m in range(KD):
                    last = T_.matmul(bank[0][:, 0:D], bv_wide[:, m, :], woT[:, m, :], start=(m == 0),
                                     stop=(m == KD - 1))
                last.then_inc(folded, 1)

            def body(at, before_, now, after):
                c = idx(at)
                even = at[1] % 2 == 0
                if now and not before_:
                    pe.wait_ge(row_biases, 2)
                    pe.wait_ge(turned_lo, 3)
                    pe.wait_ge(consts_cast, 1)
                if now:
                    pe.wait_ge(xt_ready, KD * (c + 1))
                    for s in range(SUB):
                        if isinstance(c, int) and c == 1:
                            pe.wait_ge(bias_rows_ready, 1)
                        wait(pe, attn_ready, SUB * (c - 1))
                        cols = slice(s * P, (s + 1) * P)
                        T_.matmul(bank[s][:, 0:ROW], ones_wide[0:2, :], kb[:, :], start=True, stop=False)
                        split3(bank[s][:, 0:ROW],
                               [(xt_h[:, h, cols], xt_l[:, h, cols], wkg_h[:, h, :], wkg_l[:, h, :])
                                for h in range(KD)], start=False).then_inc(k_done, 1)
                if before_:
                    pe.wait_ge(m_lo, c)
                    pe.wait_ge(ksum_ready, c)
                    for h in range(KD):
                        cols = slice(h * P, (h + 1) * P)
                        T_.matmul(bank[7 - h][:, 0:PW], ksum_rows[:, cols], bias_rows[:, :], start=True, stop=False)
                        last = split3(bank[7 - h][:, 0:D],
                                      [(m_h[:, d, cols], m_l[:, d, cols], wvo_h[:, d, :], wvo_l[:, d, :])
                                       for d in range(KD)], start=False)
                    last.then_inc(p_done, 1)
                if now:
                    for h in range(KD):
                        pe.wait_ge(k_ready, SUB * c + 3 + h)
                        cols = slice(h * P, (h + 1) * P)
                        T_.matmul(bank[2 + h][:, :].rearrange("p (c t) -> p c t", t=P), qb[:, cols],
                                  ones_wide[0:2, :].unsqueeze(1).to_broadcast([2, S // P, P]),
                                  start=True, stop=False)
                        split3(bank[2 + h][:, :],
                               [(wqT_h[:, d, cols], wqT_l[:, d, cols], xt_h[:, d, :], xt_l[:, d, :])
                                for d in range(KD)], start=False).then_inc(q_done, 1)
                if now and not before_:
                    fold_weights()
                if before_ and even:
                    pe.wait_ge(front_ready, half(at))
                    pe.wait_ge(p_lo, KD * c)
                    pe.wait_ge(consts_cast, 1)
                    T_.matmul(bank[7][:, 0:GP], earlier[:, :], g_in_r[:, :, :].rearrange("p s g -> p (s g)"),
                              start=True, stop=False)
                    T_.matmul(bank[7][:, 0:GP], ones_wide[:, :],
                              run_all[:, 0:PAIR, :].rearrange("p s g -> p (s g)"), start=False, stop=True
                              ).then_inc(rank_done, 1)
                if before_ and not now:
                    pe.wait_ge(xt_ready, KD * B)
                    for first, t in ((0, PAIR), (N_GROUP, 0)):
                        last = T_.matmul(bank[4][:, first:first + N_GROUP], ones_wide[:, :], run_all[:, t, :],
                                         start=True, stop=True)
                    last.then_inc(counted, 1)
                if before_:
                    pe.wait_ge(p_lo, KD * c)
                    pe.wait_ge(q_lo, c)
                    for s in range(SUB):
                        if s == 0:
                            pe.wait_ge(k_ready, SUB * (c + 1) if now else SUB * c)
                        elif s >= 2:
                            pe.wait_ge(q_ready, KD * (c + 1 if now else c) + s - 3)
                        cols = slice(s * P, (s + 1) * P)
                        split3(bank[s][:, 0:PW],
                               [(q_h[:, d, cols], q_l[:, d, cols], p_h[:, d, :], p_l[:, d, :])
                                for d in range(KD)]).then_inc(c_done, 1)
                if after:
                    n = later(at, 1)
                    pe.wait_ge(xn_ready, c + 2)
                    wait(pe, xt_ready, KD * (c + 1))
                    for s in range(SUB):
                        for h in range(KD):
                            last = T_.transpose(bank[4 + h][:, s * P:(s + 1) * P], xn[:, n[1], s, h * P:(h + 1) * P],
                                                ident[:, :])
                    last.then_inc(xt_done, 1)
                if now:
                    pe.wait_ge(k_lo, c + 1)
                    wait(pe, p_lo, KD * c)
                    if before_:
                        wait(pe, rank_read, half(at))
                    for n, kk in enumerate((k_h, k_l)):
                        for s in range(SUB):
                            last = T_.matmul(bank[7][0:64, D:2 * D], ones_wide[:, 0:64], kk[:, s, :],
                                             start=(n == 0 and s == 0), stop=(n == 1 and s == SUB - 1))
                    last.then_inc(ksum_done, 1)
                    pe.wait_ge(xr_ready, c + 1)
                    wait(pe, m_lo, c)
                    for h in range(KD):
                        cols = slice(h * P, (h + 1) * P)
                        last = split3(bank[6][:, h * D:(h + 1) * D],
                                      [(xr_h[:, s, cols], xr_l[:, s, cols], k_h[:, s, :], k_l[:, s, :])
                                       for s in range(SUB)])
                    last.then_inc(m_done, 1)

            attention_rounds(pe, body)

            pe.wait_ge(fourth_turned, 1)
            T_.transpose(bank[5][:, 0:P], bv_wide[:, 0, :], ident[:, :]).then_inc(fourth_turned, 1)
            pe.wait_ge(expert_lo, E)
            pe.wait_ge(attn_ready, SUB * B)

            PARTS = ((0, 0), (0, 1), (1, 0))

            def turn_hidden(tile, src):
                for e in range(GE):
                    last = T_.transpose(bank[2 + tile][:, e * P:(e + 1) * P], src[:, tile, e, :], ident[:, :])
                last.then_inc(ht_done, 1)

            def down_moving(w, e):
                return w[:, bass.ds(e, 1), UPW:].rearrange("p o d -> p (o d)")

            def sparse_path():
                def turn_rows(buf, par, count_):
                    pe.wait_ge(rows_loaded[buf], count_)
                    for h in range(KD):
                        for tile in range(2):
                            last = T_.transpose(bank[4 + par][:, (2 * h + tile) * P:(2 * h + tile + 1) * P],
                                                f_rows[:, buf, tile, h * P:(h + 1) * P], ident[:, :])
                    last.then_inc(fx_done, 1)

                def first_expert(s, d):
                    if s.kind(d) == "shared":
                        return E
                    return pe.value_load(unit_expert[0:1, bass.ds(s.u + d, 1)], min_val=0, max_val=E - GE)

                def up(s, first):
                    for h in range(KD):
                        moving = [w[:, bass.ds(first, GE), h * I:(h + 1) * I] for w in (we_h, we_l)]
                        for n, (a, b) in enumerate(PARTS):
                            for tile in range(2):
                                last = T_.matmul(bank[tile][:, :].rearrange("p (e i) -> p e i", e=GE),
                                                 (fx_h, fx_l)[a][:, s.par, h, tile], moving[b],
                                                 start=(h == 0 and n == 0), stop=(h == KD - 1 and n == 2))
                                if h == KD - 1 and n == 2:
                                    last.then_inc(up_done, 1)

                def up_shared(s):
                    for e in range(GE):
                        dst = bank[e // 2][:, (e % 2) * UR:(e % 2 + 1) * UR]
                        last = split3(dst, [(we_h[:, E + e, h * I:(h + 1) * I], we_l[:, E + e, h * I:(h + 1) * I],
                                             fx_h[:, s.par, h].rearrange("p s t -> p (s t)"),
                                             fx_l[:, s.par, h].rearrange("p s t -> p (s t)")) for h in range(KD)])
                        if e % 2 == 1:
                            last.then_inc(up_done, 1)

                def down(s, first):
                    shared = s.kind(-2) == "shared"

                    def hidden_of(t, tile, e):
                        return t[:, e // 2, 2 * (e % 2) + tile] if shared else t[:, tile, e]

                    for e in range(GE):
                        moving = [down_moving(w, first + e) for w in (we_h, we_l)]
                        for n, (a, b) in enumerate(PARTS):
                            for tile in range(2):
                                last = T_.matmul(bank[6 + tile][:, 0:D], hidden_of((ht_h, ht_l)[a][s.par], tile, e),
                                                 moving[b], start=(e == 0 and n == 0),
                                                 stop=(e == GE - 1 and n == 2))
                    last.then_inc(down_done, 1)

                def step(s):
                    if s.near == 0:
                        turn_rows(0, 0, 16)
                    if s.kind(0):
                        first = first_expert(s, 0)
                        pe.wait_ge(fx_ready, s.u + 1)
                        wait(pe, silu_ready, 2 * s.u)
                        if s.near == ROUTED:
                            pe.wait_ge(expert_lo, NE)
                        if s.kind(0) == "shared":
                            up_shared(s)
                        else:
                            up(s, first)
                    if s.kind(1):
                        wait(pe, fx_ready, s.u)
                        turn_rows((s.r + 1) % 4, 1 - s.par, 16 * (s.fours(1) + 1))
                    if s.kind(-1) == "routed":
                        for tile in range(2):
                            pe.wait_ge(weighted, 2 * s.u - 1 + tile)
                            wait(pe, ht_ready, 2 * s.u - 3 + tile)
                            turn_hidden(tile, hidw[1 - s.par])
                    if s.kind(-2):
                        first = first_expert(s, -2)
                        if s.kind(-3) == "shared":
                            pe.wait_ge(f_ready, s.u - 2 - ROUTED)
                        else:
                            wait(pe, y_ready, s.u - 2)
                        pe.wait_ge(ht_ready, 2 * s.u - 2)
                        down(s, first)

                sparse_steps(pe, step)

            def dense_path():
                def turn_rows(par, count_):
                    pe.wait_ge(rows_loaded[par], count_)
                    for h in range(KD):
                        last = T_.transpose(bank[4 + par][:, h * P:(h + 1) * P],
                                            f_rows[:, par, 0, h * P:(h + 1) * P], ident[:, :])
                    last.then_inc(fx_done, 1)

                def up(u, par, rows_par, first):
                    wait(pe, silu_ready, u - 1)
                    mov = [[w[:, first:first + GE, h * I:(h + 1) * I] for w in (we_h, we_l)] for h in range(KD)]
                    split3(bank[par][:, :].rearrange("p (e i) -> p e i", e=GE),
                           [(fx_h[:, rows_par, h, 0], fx_l[:, rows_par, h, 0], mov[h][0], mov[h][1])
                            for h in range(KD)]).then_inc(up_done, 1)

                pe.wait_ge(expert_lo, NE)
                turn_rows(0, 16)

                def unit(k, r, first, last):
                    u = 2 * NG * k + r
                    g, par = r % NG, r // NG
                    if g == 0:
                        pe.wait_ge(fx_ready, 2 * k + par + 1)
                    up(u, r % 2, par, g * GE)
                    if g == 1 and not (last and par == 1):
                        wait(pe, fx_ready, 2 * k + par)
                        turn_rows(1 - par, 16 * (k + 1 + par))
                    if not (first and r < 1):
                        turn(k, r - 1)
                    if not (first and r < 2):
                        fold(k, r - 2)

                def turn(k, r):
                    u = 2 * NG * k + r
                    g = r % NG
                    if g < N_GROUP:
                        pe.wait_ge(weighted, N_GROUP * (2 * k + r // NG) + g + 1)
                    else:
                        pe.wait_ge(silu_ready, u + 1)
                    wait(pe, ht_ready, u - 1)
                    turn_hidden(r % 2, (hidw if g < N_GROUP else hid)[0])

                def fold(k, r):
                    g, par = r % NG, (r // NG) % 2
                    u = 2 * NG * k + r
                    if g == 0:
                        wait(pe, f_ready, 2 * k + r // NG - 1)
                    pe.wait_ge(ht_ready, u + 1)
                    split3(bank[6 + par][:, 0:D],
                           [(ht_h[0][:, r % 2, e], ht_l[0][:, r % 2, e], down_moving(we_h, g * GE + e),
                             down_moving(we_l, g * GE + e)) for e in range(GE)],
                           start=g == 0, stop=g == NG - 1).then_inc(down_done, 1)

                dense_rounds(pe, unit)
                k = NT // 2 - 1
                turn(k, 2 * NG - 1)
                fold(k, 2 * NG - 2)
                fold(k, 2 * NG - 1)

            either(pe, sparse_path, dense_path)


_INS = ['L0_attn_x', 'L0_attn_Wq', 'L0_attn_bq', 'L0_attn_Wk', 'L0_attn_bk', 'L0_attn_Wv', 'L0_attn_bv', 'L0_attn_Wo',
        'L0_attn_bo', 'L0_ffn_gate_weight', 'L0_ffn_expert_up', 'L0_ffn_expert_down', 'L0_ffn_shared_up',
        'L0_ffn_shared_down']
_OUTS = [((16, 512, 256), 'float32')]


def kernel(**inputs):
    import numpy as _np
    import concourse.bacc as _bacc
    from concourse import mybir as _mybir
    from concourse.bass_utils import run_bass_kernel_spmd as _run

    nc = _bacc.Bacc("TRN2", target_bir_lowering=False, num_devices=1)
    arrays, args = {}, []
    for name in _INS:
        a = _np.ascontiguousarray(inputs[name])
        arrays[f"in_{name}_dram"] = a
        args.append(nc.dram_tensor(f"in_{name}_dram", a.shape, _mybir.dt.from_np(a.dtype), kind="ExternalInput").ap())
    for i, (shape, dtype) in enumerate(_OUTS):
        dt = _mybir.dt.from_np(_np.dtype(dtype))
        args.append(nc.dram_tensor(f"out_{i}_dram", shape, dt, kind="ExternalOutput").ap())
    attention_and_routed_ffn(nc, *args)
    r = _run(nc, [arrays], core_ids=[0])
    got = tuple(r.results[0][f"out_{i}_dram"] for i in range(len(_OUTS)))
    return got[0]
```
